# Optimizing a Trainium2 kernel written in Bass

```python
import numpy as np
import jax
import jax.numpy as jnp

def _softmax(x, axis=-1):
    return jax.nn.softmax(x, axis=axis)

def _gelu(x):
    return jax.nn.gelu(x, approximate=True)

def _silu(x):
    return jax.nn.silu(x)

def _sigmoid(x):
    return jax.nn.sigmoid(x)

def _layernorm(x, axis=-1, eps=1e-05):
    m = jnp.mean(x, axis=axis, keepdims=True)
    v = jnp.var(x, axis=axis, keepdims=True)
    return (x - m) / jnp.sqrt(v + eps)

def _scatter_add(tgt, idx, src, axis=0):
    return tgt.at[idx].add(src)

def _segment_sum(src, seg, n):
    return jax.ops.segment_sum(src, seg, n)
kernel_name = 'mk_adaln_d1_jaxref_r8_e7a46e'

def setup_inputs(seed: int=0):
    np.random.seed(seed)
    _w = jnp.asarray

    def _L0_attn_setup():
        import jax, jax.numpy as jnp
        import numpy as np
        B, T, D_MODEL = (2, 256, 256)
        N_HEADS, D_HEAD = (16, 128)
        MAX_SEQ_LEN = 256
        LOGIT_SOFTCAP = 50.0
        EPS = 1e-06

        def precompute_rope(dim, max_seq_len, theta=10000.0):
            freqs = 1.0 / theta ** (np.arange(0, dim, 2, dtype=np.float32) / dim)
            t = np.arange(max_seq_len, dtype=np.float32)
            angles = np.outer(t, freqs)
            return (jnp.asarray(np.cos(angles)), jnp.asarray(np.sin(angles)))

        def rmsnorm(x, w):
            return x * jax.lax.rsqrt(jnp.mean(x * x, axis=-1, keepdims=True) + EPS) * w

        def apply_rope(x, cos, sin):
            n = x.shape[1]
            x1, x2 = (x[..., ::2], x[..., 1::2])
            c = cos[:n][None, :, None, :]
            s = sin[:n][None, :, None, :]
            out = jnp.stack([x1 * c - x2 * s, x1 * s + x2 * c], axis=-1)
            return out.reshape(x.shape)
        key = jax.random.key(seed)
        ks = jax.random.split(key, 6)
        x = jax.random.normal(ks[0], (B, T, D_MODEL), dtype=jnp.float32)
        wq = 0.02 * jax.random.normal(ks[1], (N_HEADS * D_HEAD, D_MODEL), dtype=jnp.float32)
        wk = 0.02 * jax.random.normal(ks[2], (N_HEADS * D_HEAD, D_MODEL), dtype=jnp.float32)
        wv = 0.02 * jax.random.normal(ks[3], (N_HEADS * D_HEAD, D_MODEL), dtype=jnp.float32)
        wo = 0.02 * jax.random.normal(ks[4], (D_MODEL, N_HEADS * D_HEAD), dtype=jnp.float32)
        q_norm_w = jnp.ones((D_HEAD,), dtype=jnp.float32)
        k_norm_w = jnp.ones((D_HEAD,), dtype=jnp.float32)
        rope_cos, rope_sin = precompute_rope(D_HEAD, MAX_SEQ_LEN)
        return {'x': x, 'wq': wq, 'wk': wk, 'wv': wv, 'wo': wo, 'q_norm_w': q_norm_w, 'k_norm_w': k_norm_w, 'rope_cos': rope_cos, 'rope_sin': rope_sin}
    _L0_attn_in = _L0_attn_setup()

    def _L0_ffn_setup():
        import jax, jax.numpy as jnp
        import numpy as np
        TOP_K = 6
        N_GROUP = 8
        TOPK_GROUP = 3
        CAPACITY = 96
        RSF = 1.0
        key = jax.random.key(seed)
        ks = jax.random.split(key, 8)
        B, S, H = (1, 512, 256)
        E, M = (64, 176)
        MS = 352
        sc = 0.02
        return {'hidden_states': jax.random.normal(ks[0], (B, S, H), jnp.float32), 'gate_weight': jax.random.normal(ks[1], (E, H), jnp.float32) * sc, 'Wg': jax.random.normal(ks[2], (E, M, H), jnp.float32) * sc, 'Wu': jax.random.normal(ks[3], (E, M, H), jnp.float32) * sc, 'Wd': jax.random.normal(ks[4], (E, H, M), jnp.float32) * sc, 'Sg': jax.random.normal(ks[5], (MS, H), jnp.float32) * sc, 'Su': jax.random.normal(ks[6], (MS, H), jnp.float32) * sc, 'Sd': jax.random.normal(ks[7], (H, MS), jnp.float32) * sc}
    _L0_ffn_in = _L0_ffn_setup()
    _L0_c = _w((lambda *s: np.random.randn(*s).astype(np.float32) * 0.05)(4, 256))
    _L0_wmod = _w((lambda *s: np.random.randn(*s).astype(np.float32) * 0.05)(256, 6 * 256) * 256 ** (-0.5))
    _d = {'L0_attn_x': _L0_attn_in['x'], 'L0_attn_wq': _L0_attn_in['wq'], 'L0_attn_wk': _L0_attn_in['wk'], 'L0_attn_wv': _L0_attn_in['wv'], 'L0_attn_wo': _L0_attn_in['wo'], 'L0_attn_q_norm_w': _L0_attn_in['q_norm_w'], 'L0_attn_k_norm_w': _L0_attn_in['k_norm_w'], 'L0_attn_rope_cos': _L0_attn_in['rope_cos'], 'L0_attn_rope_sin': _L0_attn_in['rope_sin'], 'L0_ffn_gate_weight': _L0_ffn_in['gate_weight'], 'L0_ffn_Wg': _L0_ffn_in['Wg'], 'L0_ffn_Wu': _L0_ffn_in['Wu'], 'L0_ffn_Wd': _L0_ffn_in['Wd'], 'L0_ffn_Sg': _L0_ffn_in['Sg'], 'L0_ffn_Su': _L0_ffn_in['Su'], 'L0_ffn_Sd': _L0_ffn_in['Sd'], 'L0_c': _L0_c, 'L0_wmod': _L0_wmod}
    _x0 = _d['L0_attn_x']
    _d['L0_attn_x'] = jax.random.normal(jax.random.fold_in(jax.random.key(seed), 1), (4, 512, 256), dtype=_x0.dtype)
    del _x0
    return _d

def reference(L0_attn_x, L0_attn_wq, L0_attn_wk, L0_attn_wv, L0_attn_wo, L0_attn_q_norm_w, L0_attn_k_norm_w, L0_attn_rope_cos, L0_attn_rope_sin, L0_ffn_gate_weight, L0_ffn_Wg, L0_ffn_Wu, L0_ffn_Wd, L0_ffn_Sg, L0_ffn_Su, L0_ffn_Sd, L0_c, L0_wmod):

    def _L0_attn_ref(x, wq, wk, wv, wo, q_norm_w, k_norm_w, rope_cos, rope_sin):
        import jax, jax.numpy as jnp
        import numpy as np
        B, T, D_MODEL = (2, 256, 256)
        N_HEADS, D_HEAD = (16, 128)
        MAX_SEQ_LEN = 256
        LOGIT_SOFTCAP = 50.0
        EPS = 1e-06

        def precompute_rope(dim, max_seq_len, theta=10000.0):
            freqs = 1.0 / theta ** (np.arange(0, dim, 2, dtype=np.float32) / dim)
            t = np.arange(max_seq_len, dtype=np.float32)
            angles = np.outer(t, freqs)
            return (jnp.asarray(np.cos(angles)), jnp.asarray(np.sin(angles)))

        def rmsnorm(x, w):
            return x * jax.lax.rsqrt(jnp.mean(x * x, axis=-1, keepdims=True) + EPS) * w

        def apply_rope(x, cos, sin):
            n = x.shape[1]
            x1, x2 = (x[..., ::2], x[..., 1::2])
            c = cos[:n][None, :, None, :]
            s = sin[:n][None, :, None, :]
            out = jnp.stack([x1 * c - x2 * s, x1 * s + x2 * c], axis=-1)
            return out.reshape(x.shape)
        Bx, Tx, _ = x.shape
        scale = D_HEAD ** (-0.5)
        q = (x @ wq.T).reshape(Bx, Tx, N_HEADS, D_HEAD).transpose(0, 2, 1, 3)
        k = (x @ wk.T).reshape(Bx, Tx, N_HEADS, D_HEAD).transpose(0, 2, 1, 3)
        v = (x @ wv.T).reshape(Bx, Tx, N_HEADS, D_HEAD).transpose(0, 2, 1, 3)
        q = rmsnorm(q, q_norm_w)
        k = rmsnorm(k, k_norm_w)
        q = apply_rope(q, rope_cos, rope_sin)
        k = apply_rope(k, rope_cos, rope_sin)
        scores = jnp.einsum('bhtd,bhsd->bhts', q, k) * scale
        scores = LOGIT_SOFTCAP * jnp.tanh(scores / LOGIT_SOFTCAP)
        mask = jnp.triu(jnp.ones((Tx, Tx), dtype=bool), k=1)
        scores = jnp.where(mask[None, None], -jnp.inf, scores)
        attn = jax.nn.softmax(scores, axis=-1)
        out = jnp.einsum('bhts,bhsd->bhtd', attn, v)
        out = out.transpose(0, 2, 1, 3).reshape(Bx, Tx, N_HEADS * D_HEAD)
        return out @ wo.T

    def _L0_ffn_ref(hidden_states, gate_weight, Wg, Wu, Wd, Sg, Su, Sd):
        import jax, jax.numpy as jnp
        import numpy as np
        TOP_K = 6
        N_GROUP = 8
        TOPK_GROUP = 3
        CAPACITY = 96
        RSF = 1.0
        B, S, H = hidden_states.shape
        E, M, _ = Wg.shape
        K, NG, TG, C = (TOP_K, N_GROUP, TOPK_GROUP, CAPACITY)
        x = hidden_states.reshape(-1, H)
        T = x.shape[0]
        logits = x.astype(jnp.float32) @ gate_weight.astype(jnp.float32).T
        scores = jax.nn.softmax(logits, axis=-1)
        group_scores = scores.reshape(T, NG, E // NG).max(axis=-1)
        _, gidx = jax.lax.top_k(group_scores, TG)
        gmask = jnp.zeros((T, NG), scores.dtype).at[jnp.arange(T)[:, None], gidx].set(1.0)
        smask = jnp.repeat(gmask, E // NG, axis=1)
        tmp_scores = jnp.where(smask > 0, scores, 0.0)
        topk_w, topk_i = jax.lax.top_k(tmp_scores, K)
        topk_w = topk_w * RSF
        flat = topk_i.reshape(-1)
        oh = jax.nn.one_hot(flat, E, dtype=jnp.int32)
        pos = jnp.sum(jnp.cumsum(oh, axis=0) * oh, axis=-1) - 1
        slot = flat * C + jnp.minimum(pos, C - 1)
        tok = jnp.arange(T * K) // K
        buf = jnp.zeros((E * C, H), x.dtype).at[slot].set(x[tok]).reshape(E, C, H)
        g = jnp.einsum('ech,emh->ecm', buf, Wg)
        u = jnp.einsum('ech,emh->ecm', buf, Wu)
        out = jnp.einsum('ecm,ehm->ech', jax.nn.silu(g) * u, Wd).reshape(E * C, H)
        yk = out[slot].reshape(T, K, H)
        y = jnp.sum(yk * topk_w[..., None].astype(yk.dtype), axis=1)
        shared = jax.nn.silu(x @ Sg.T) * (x @ Su.T) @ Sd.T
        return (y + shared).reshape(B, S, H)
    x = L0_attn_x
    mod = (_silu(L0_c) @ L0_wmod).reshape(L0_c.shape[0], 6, 1, -1)
    sa, ca, ga, sb, cb, gb = (mod[:, 0], mod[:, 1], mod[:, 2], mod[:, 3], mod[:, 4], mod[:, 5])
    ga = (2 * (ga >= 0) - 1) * jnp.maximum(jnp.abs(ga), 0.25)
    gb = (2 * (gb >= 0) - 1) * jnp.maximum(jnp.abs(gb), 0.25)
    h = _layernorm(x, axis=-1) * (1 + ca) + sa
    x = x + ga * _L0_attn_ref(h, L0_attn_wq, L0_attn_wk, L0_attn_wv, L0_attn_wo, L0_attn_q_norm_w, L0_attn_k_norm_w, L0_attn_rope_cos, L0_attn_rope_sin)
    h = _layernorm(x, axis=-1) * (1 + cb) + sb
    x = x + gb * _L0_ffn_ref(h, L0_ffn_gate_weight, L0_ffn_Wg, L0_ffn_Wu, L0_ffn_Wd, L0_ffn_Sg, L0_ffn_Su, L0_ffn_Sd)
    return x

_drawn_inputs = setup_inputs


def setup_inputs(seed=0):
    import zlib

    import numpy as np

    out = dict(_drawn_inputs(seed))
    spreads = {'L0_attn_q_norm_w': (1.0, 0.6), 'L0_attn_k_norm_w': (1.0, 0.6)}
    factors = {'L0_attn_wq': 5.729,
     'L0_attn_wk': 5.74,
     'L0_attn_wv': 4.396,
     'L0_attn_wo': 4.431,
     'L0_attn_rope_cos': 8.0,
     'L0_attn_rope_sin': 8.0,
     'L0_ffn_gate_weight': 8.0,
     'L0_ffn_Wg': 8.0,
     'L0_ffn_Wu': 8.0,
     'L0_ffn_Wd': 8.0,
     'L0_ffn_Sg': 8.0,
     'L0_ffn_Su': 8.0,
     'L0_ffn_Sd': 8.0,
     'L0_c': 4.101,
     'L0_wmod': 4.091}
    for name, (base, spread) in spreads.items():
        noise = np.random.default_rng([zlib.crc32(name.encode()), seed]).standard_normal(out[name].shape)
        drawn = base * np.exp(spread * noise) if base else spread * noise
        out[name] = jnp.asarray(drawn.astype(out[name].dtype))
    for name, factor in factors.items():
        out[name] = (out[name] * factor).astype(out[name].dtype)
    return out
```

```python
from contextlib import ExitStack

import concourse.bass as bass
from concourse import mybir

F32 = mybir.dt.float32
I32 = mybir.dt.int32
U32 = mybir.dt.uint32
ALU = mybir.AluOpType
ACT = mybir.ActivationFunctionType
X = mybir.AxisListType.X

P = 128
B, T, D = 4, 512, 256
TT = T // P
NT = B * TT
NTOK = B * T
KC = D // P
H, DH = 16, 128
CAP = 50.0
E, M = 64, 176
MC = 88
MS = 352
K, NG, GS, TG = 6, 8, 8, 3
C = 96
MSC = [(0, 128), (128, 128), (256, 96)]
OFF = [0, 512, 1024, 896]
PW = 1536
RING = 4
XR = 8
AHEAD = 7
NACC = 2
SKIP = 8192.0
NOTOK = 4096.0


def build(nc, x, wqkv, wo, qkw, cossin, ct, wmod, gate, sgu, sd, wgu, wd, out):
    with ExitStack() as ctx:
        def sb(name, shape, dt=F32):
            return ctx.enter_context(nc.sbuf_tensor(name, shape, dt))

        def sem(name):
            return ctx.enter_context(nc.semaphore(name))

        ps = ctx.enter_context(nc.psum_tensor("ps", [P, 8, 512], F32))

        h2_d = nc.dram_tensor("h2_rows", (NTOK, D), F32, kind="Internal").ap()
        tab_d = nc.dram_tensor("slot_table", (E * C, 2), F32, kind="Internal").ap()
        acc_d = [nc.dram_tensor(f"acc{a}", (NTOK, D), F32, kind="Internal").ap() for a in range(NACC)]
        o95_d = nc.dram_tensor("last_rows", (E, D), F32, kind="Internal").ap()

        xs = sb("xs", [P, NT, D])
        rows = sb("rows", [P, B, 4, D])
        modt = sb("modt", [P, 4, B])
        h2t = sb("h2t", [P, KC, NTOK])
        logits = sb("logits", [P, NT, E])
        ident = sb("ident", [P, P])
        neghalf = sb("neghalf", [P, 8])
        gates = sb("gates", [P, KC, E])
        wgus = sb("wgus", [P, RING, KC, 2 * M])
        wds = sb("wds", [MC, RING, 2, D])
        warena = sb("warena", [P, KC * H * 3 * DH])
        wq = warena[:].rearrange("p (k h c) -> p k h c", k=KC, h=H)
        wos = sb("wos", [P, H, D])
        arena2 = sb("arena2", [P, 8704])
        at = [0]

        def part(n):
            v = arena2[:, at[0]:at[0] + n]
            at[0] += n
            return v

        ht = sb("ht", [P, KC, T])
        xn = sb("xn", [P, TT, D])
        qt = sb("qt", [P, T])
        kt = sb("kt", [P, T])
        prob = sb("prob", [P, PW])
        vx = sb("vx", [P, 4 * TT * (DH + 1)])
        sq = part(TT * 2 * DH).rearrange("p (i c d) -> p i c d", i=TT, c=2)
        qn = part(TT * DH).rearrange("p (i d) -> p i d", i=TT)
        kr = part(TT * DH).rearrange("p (i d) -> p i d", i=TT)
        on = part(TT * DH).rearrange("p (i d) -> p i d", i=TT)
        ot = part(T)
        yacc = part(TT * D).rearrange("p (i d) -> p i d", i=TT)
        wmods = part(KC * 6 * D).rearrange("p (k n) -> p k n", k=KC)
        scb = part(KC * B * P).rearrange("p (k b m) -> p k b m", k=KC, b=B)
        tmpg = h2t[:].rearrange("p k t -> p (k t)").rearrange("p (a c b d) -> p a c b d", a=2, b=B, c=2)
        ss = sb("ss", [P, 2 * TT])
        rtmp = sb("rtmp", [P, 2 * TT])
        rn = sb("rn", [P, H, 2 * TT])
        rden = sb("rden", [P, TT])
        g = sb("g", [P, H])
        qkws = sb("qkws", [P, 2])
        css = sb("css", [P, 2, H])
        cts = sb("cts", [P, KC, B])
        sc = sb("sc", [P, KC, B])
        bst = sb("bst", [P, TT, 6])
        mv = sb("mv", [P, TT, 2])
        rstd = sb("rstd", [P, TT])
        holdp = sb("holdp", [P, 4])
        holdv = sb("holdv", [P, 2])

        apos = [0]

        def again(shape, dt=F32, parts=P):
            n = 1
            for s in shape:
                n *= s
            v = warena[0:parts, apos[0]:apos[0] + n]
            apos[0] += n
            assert apos[0] <= KC * H * 3 * DH
            if dt != F32:
                v = v.bitcast(dt)
            if len(shape) == 2:
                return v.rearrange("p (a b) -> p a b", a=shape[0])
            if len(shape) == 3:
                return v.rearrange("p (a b c) -> p a b c", a=shape[0], b=shape[1])
            return v

        oh = again([NT, K, E])
        sel = again([NT, E])
        cum = again([NT + 1, E])
        tmp = again([NT, E])
        over = again([NT, E])
        sgus = again([KC * 2, MS]).rearrange("p (k u) m -> p k u m", k=KC)
        sds = wos[:, 8:11, :]
        acts = arena2[:, 0:3 * T].rearrange("p (m t) -> p m t", m=3)
        sg = arena2[:, 3 * T:5 * T].rearrange("p (a t) -> p a t", a=2)
        shr = arena2[:, 5 * T:5 * T + NT * D].rearrange("p (i d) -> p i d", i=NT)
        w95t = arena2[0:E, 5 * T + NT * D:5 * T + NT * D + NTOK]
        assert 5 * T + NT * D + NTOK <= 8704 and at[0] <= 8704
        small = prob
        mx = small[:, 0:16]
        rs = small[:, 16:32]
        gsc = small[:, 32:160].rearrange("p (i n) -> p i n", i=NT)
        g8 = small[:, 160:288].rearrange("p (i n) -> p i n", i=NT)
        gi = small[:, 288:416].bitcast(U32).rearrange("p (i n) -> p i n", i=NT)
        gif = small[:, 416:544].rearrange("p (i n) -> p i n", i=NT)
        gm = small[:, 544:672].rearrange("p (i n) -> p i n", i=NT)
        gm2 = small[:, 672:800].rearrange("p (i n) -> p i n", i=NT)
        w8 = small[:, 800:928].rearrange("p (i n) -> p i n", i=NT)
        ei = small[:, 928:1056].bitcast(U32).rearrange("p (i n) -> p i n", i=NT)
        eif = small[:, 1056:1184].rearrange("p (i n) -> p i n", i=NT)
        slotf = small[:, 1184:1280].rearrange("p (i n) -> p i n", i=NT)
        sloti = small[:, 1280:1376].bitcast(I32)
        lastp = small[:, 1376:1440]
        pair = vx[:, 0:192].rearrange("p (i k c) -> p i k c", i=NT, k=K)
        lastr = vx[0:E, 192:194]
        tabs = vx[0:E, 200:392].rearrange("p (s c) -> p s c", c=2)
        gidx = vx[0:C, 392:456].bitcast(I32)
        sidx = vx[0:C, 456:520].bitcast(I32)
        idf = vx[0:C, 520:584]
        wcol = vx[0:C, 584:648]
        o95 = vx[0:E, 648:904]
        xg = arena2[:, 0:XR * D].rearrange("p (u d) -> p u d", u=XR)
        xgt = qt[:, 0:2 * KC * C].rearrange("p (u k c) -> p u k c", u=2, k=KC)
        gact = kt[0:C, 0:2 * M].rearrange("p (u m) -> p u m", u=2)
        act = ht[0:C, 0, 0:2 * M].rearrange("p (u m) -> p u m", u=2)
        actt = ht[0:MC, 1, 0:4 * C].rearrange("p (u m c) -> p u m c", u=2, m=2)
        orow = wos[0:C, 0:RING, :]
        accs = [warena[:, a * NT * D:(a + 1) * NT * D].rearrange("p (i d) -> p i d", i=NT) for a in range(NACC)]

        tri = sb("tri", [P, P])
        ones = sb("ones", [P, P])
        iota8 = sb("iota8", [P, NG])
        iotae = sb("iotae", [P, E])
        iota96 = sb("iota96", [P, E])
        iotat = sb("iotat", [P, NT])
        fill = sb("fill", [E, C, 2])
        zrow = sb("zrow", [P, D])

        names = """ld_x ld_c ld_wmod ld_small ld_wqkv ld_wo ld_gate ld_sh consts fills zeros tables
            silu_c scb_rdy modt_ps rows_ps modt_sb rows_sb clamp g_rdy
            stats aggr var_eps rstd_rdy xn_rdy hmod xt_ps ht_rdy h2t_rdy h2_out logit_ps logit_sb
            qkv_rdy squared k_copied v_copied ss_rdy r_tmp r_rdy q_scaled qt_ps kt_ps qt_rdy kt_rdy
            s_rdy capped expd p_rdy o_rdy den_rdy o_normed ot_ps ot_rdy y_rdy y_added yzero x2_rdy
            ones_rdy rt soft rt_exp sel_rdy pos_rdy lastp_rdy lastt_ps slot_rdy tabw tabl tabr tabt tabt_sb
            last_out w95_rdy w95_ps w95_sb idx_rdy sg_ps sg_act sa_rdy sdn_ps shr_rdy
            tr1_ps xgt_rdy gu_ps gact_rdy act_rdy tr2_ps actt_rdy dn_ps orow_rdy
            acc_ld o95_ld cmb_ps cmb cmb2 outd""".split()
        s = {n: sem(n) for n in names}
        xg_in = [sem(f"xg_in{i}") for i in range(XR)]
        w_in = [sem(f"w_in{i}") for i in range(RING)]
        ys = [sem(f"ys{a}") for a in range(NACC)]
        o95s = [sem(f"o95s{i}") for i in range(RING)]

        block = ctx.enter_context(nc.Block())

        sflat = ps[:, 4:7, :].rearrange("p a c -> p (a c)")
        yps = ps[:, 4:6, :].rearrange("p a (u d) -> p (a u) d", d=D)

        def cnt(b, n):
            if isinstance(n, int) and n < -1:
                n = -1
            return b * H + (n + 1)

        def vslot(n):
            return n % 4

        @block.sync
        def _(sp):
            sp.dma_start(cts[:], ct).then_inc(s["ld_c"], 16)
            sp.dma_start(wmods, wmod).then_inc(s["ld_wmod"], 16)
            sp.dma_start(xs[:], x.rearrange("(i p) d -> p i d", p=P)).then_inc(s["ld_x"], 16)
            sp.dma_start(qkws[:], qkw).then_inc(s["ld_small"], 16)
            sp.dma_start(css[:], cossin).then_inc(s["ld_small"], 16)
            sp.dma_start(wq, wqkv).then_inc(s["ld_wqkv"], 16)
            sp.dma_start(wos[:], wo).then_inc(s["ld_wo"], 16)
            sp.dma_start(gates[:], gate).then_inc(s["ld_gate"], 16)
            for u in range(RING):
                sp.dma_start(wgus[:, u], wgu[u]).then_inc(w_in[u], 16)
                sp.dma_start(wds[:, u], wd[u]).then_inc(w_in[u], 16)
            sp.wait_ge(s["fills"], 2)
            sp.dma_start(tab_d.rearrange("(e s) c -> e (s c)", e=E), fill[:].rearrange("e s c -> e (s c)")).then_inc(s["tables"], 16)
            sp.wait_ge(s["zeros"], 1)
            for a in range(NACC):
                sp.dma_start(acc_d[a].rearrange("(i p) d -> p i d", p=P),
                             zrow[:].unsqueeze(1).to_broadcast([P, NT, D])).then_inc(s["tables"], 16)
            with sp.Fori(0, B) as b:
                sp.wait_ge(s["hmod"], 2 * b + 2)
                sp.dma_start(h2_d.rearrange("(b i p) d -> p b i d", b=B, p=P)[:, bass.ds(b, 1)].squeeze(1), xn[:]).then_inc(s["h2_out"], 16)
            sp.wait_ge(s["logit_ps"], B)
            sp.dma_start(sgus, sgu).then_inc(s["ld_sh"], 16)
            sp.dma_start(sds[:, 0:2, :], sd[0:2 * P, :].rearrange("(m p) d -> p m d", p=P)).then_inc(s["ld_sh"], 16)
            sp.dma_start(sds[0:MS - 2 * P, 2, :], sd[2 * P:MS, :]).then_inc(s["ld_sh"], 16)
            sp.wait_ge(s["lastp_rdy"], 3)
            sp.wait_ge(s["tables"], 16 * (1 + NACC))
            sp.wait_ge(s["tabw"], 16 * NT * K)
            sp.dma_start(tab_d.rearrange("(e s) c -> e s c", e=E)[:, C - 1, :], lastr).then_inc(s["last_out"], 16)
            sp.wait_ge(s["last_out"], 16)
            sp.dma_start(tabs.rearrange("e s c -> e (s c)"), tab_d.rearrange("(e s) c -> e (s c)", e=E)).then_inc(s["tabl"], 16)
            with sp.Fori(0, E // RING - 1) as r:
                for u in range(RING):
                    sp.wait_ge(s["dn_ps"], r * RING + (u + 1))
                    sp.dma_start(wgus[:, u], wgu[bass.ds((r + 1) * RING + u, 1)].squeeze(0)).then_inc(w_in[u], 16)
                    sp.dma_start(wds[:, u], wd[bass.ds((r + 1) * RING + u, 1)].squeeze(0)).then_inc(w_in[u], 16)
                    sp.wait_ge(s["orow_rdy"], r * RING + (u + 1))
                    sp.dma_start(o95_d[bass.ds(r * RING + u, 1)], orow[C - 1:C, u, :]).then_inc(o95s[u], 16)
            for u in range(RING):
                sp.wait_ge(s["orow_rdy"], E - RING + u + 1)
                sp.dma_start(o95_d[E - RING + u:E - RING + u + 1], orow[C - 1:C, u, :]).then_inc(o95s[u], 16)
            for u in range(RING):
                sp.wait_ge(o95s[u], 16 * (E // RING))
            sp.dma_start(o95, o95_d).then_inc(s["o95_ld"], 16)
            for a in range(NACC):
                sp.wait_ge(ys[a], 16 * (E // NACC))
                sp.dma_start(accs[a], acc_d[a].rearrange("(i p) d -> p i d", p=P)).then_inc(s["acc_ld"], 16)
            for b in range(B):
                sp.wait_ge(s["cmb"], 4 * (b + 1))
                sp.dma_start(out[b * T:(b + 1) * T].rearrange("(i p) d -> p i d", p=P), xs[:, b * TT:(b + 1) * TT, :]).then_inc(s["outd"], 16)
            sp.wait_ge(s["outd"], 16 * B)
            sp.wait_ge(s["h2_out"], 16 * B)

        @block.gpsimd
        def _(pool):
            def hold(c):
                pool.tensor_tensor(holdp[:, c:c + 1], neghalf[:, 0:1], neghalf[:, 0:1], ALU.mult)

            pool.memset(ident[:], 0.0).then_inc(s["consts"], 1)
            pool.memset(tri[:], 1.0).then_inc(s["consts"], 1)
            pool.memset(neghalf[:], -0.5).then_inc(s["consts"], 1)
            pool.wait_ge(s["consts"], 3)
            pool.affine_select(out=ident[:], in_=ident[:], compare_op=ALU.not_equal, fill=1.0, base=0,
                               pattern=[[-1, P]], channel_multiplier=1).then_inc(s["consts"], 1)
            pool.affine_select(out=tri[:], in_=tri[:], compare_op=ALU.is_gt, fill=0.0, base=0,
                               pattern=[[1, P]], channel_multiplier=-1).then_inc(s["consts"], 1)
            pool.memset(ones[:], 1.0).then_inc(s["consts"], 1)
            pool.memset(vx[:], 1.0).then_inc(s["ones_rdy"], 1)
            pool.memset(zrow[:], 0.0).then_inc(s["zeros"], 1)
            pool.memset(fill[:, :, 0:1], NOTOK).then_inc(s["fills"], 1)
            pool.memset(fill[:, :, 1:2], 0.0).then_inc(s["fills"], 1)
            pool.iota(iota8[:], pattern=[[1, NG]], base=0, channel_multiplier=0, allow_small_or_imprecise_dtypes=True).then_inc(s["consts"], 1)
            pool.iota(iotae[:], pattern=[[1, E]], base=0, channel_multiplier=0, allow_small_or_imprecise_dtypes=True).then_inc(s["consts"], 1)
            pool.iota(iota96[:], pattern=[[C, E]], base=0, channel_multiplier=0, allow_small_or_imprecise_dtypes=True).then_inc(s["consts"], 1)
            pool.iota(iotat[:], pattern=[[P, NT]], base=0, channel_multiplier=1, allow_small_or_imprecise_dtypes=True).then_inc(s["consts"], 1)

            def ln_rstd(l):
                pool.wait_ge(s["aggr"], TT * (l + 1))
                hold(3)
                pool.tensor_scalar(rstd[:], mv[:, :, 1], 1e-5, None, ALU.add).then_inc(s["var_eps"], 1)
                pool.wait_ge(s["var_eps"], l + 1)
                pool.tensor_tensor(rstd[:], rstd[:], neghalf[:, 0:TT], ALU.pow).then_inc(s["rstd_rdy"], 1)

            def norms(b, n):
                pool.wait_ge(s["ss_rdy"], cnt(b, n))
                hold(2)
                pool.tensor_scalar(rtmp[:], ss[:], 1.0 / DH, 1e-6, ALU.mult, ALU.add).then_inc(s["r_tmp"], 1)
                pool.wait_ge(s["r_tmp"], cnt(b, n))
                pool.tensor_tensor(rn[:, bass.ds(n, 1), :].squeeze(1), rtmp[:], neghalf[:], ALU.pow).then_inc(s["r_rdy"], 1)

            def mask(b, n):
                pool.wait_ge(s["expd"], cnt(b, n))
                hold(1 if isinstance(n, int) and n == H - 1 else 0)
                d = prob[:].rearrange("p (a c) -> p a c", a=3)[:, :, 0:P]
                pool.affine_select(out=d, in_=d, compare_op=ALU.is_ge, fill=0.0, base=0,
                                   pattern=[[0, 3], [1, P]], channel_multiplier=-1).then_inc(s["p_rdy"], 1)
                d = prob[:, OFF[3]:OFF[3] + P]
                pool.affine_select(out=d, in_=d, compare_op=ALU.is_ge, fill=0.0, base=0,
                                   pattern=[[1, P]], channel_multiplier=-1).then_inc(s["p_rdy"], 1)

            with pool.Fori(0, B) as b:
                ln_rstd(2 * b)
                norms(b, 0)
                norms(b, 1)
                with pool.Fori(0, H - 2) as p:
                    mask(b, p)
                    norms(b, p + 2)
                mask(b, H - 2)
                mask(b, H - 1)
                ln_rstd(2 * b + 1)

            pool.wait_ge(s["slot_rdy"], 1)
            pool.wait_ge(s["tables"], 16 * (1 + NACC))
            for i in range(NT):
                for k in range(K):
                    pool.indirect_dma_start(tab_d, bass.IndirectOffsetOnAxis(ap=sloti[:, i * K + k:i * K + k + 1], axis=0),
                                            pair[:, i, k, :], None, bounds_check=E * C - 1, oob_is_err=False).then_inc(s["tabw"], 16)

            def gather(e):
                if e >= XR:
                    pool.wait_ge(s["tr1_ps"], e - XR + 1)
                pool.indirect_dma_start(xg[0:C, e % XR, :], None, h2_d, bass.IndirectOffsetOnAxis(ap=gidx[:, e:e + 1], axis=0),
                                        bounds_check=NTOK - 1, oob_is_err=False).then_inc(xg_in[e % XR], 16)

            pool.wait_ge(s["idx_rdy"], 4)
            pool.wait_ge(s["h2_out"], 16 * B)
            for e in range(AHEAD):
                gather(e)
            for e in range(E):
                if e + AHEAD < E:
                    gather(e + AHEAD)
                pool.wait_ge(s["orow_rdy"], e + 1)
                if e >= NACC:
                    pool.wait_ge(ys[e % NACC], 16 * (e // NACC))
                pool.indirect_dma_start(acc_d[e % NACC], bass.IndirectOffsetOnAxis(ap=sidx[0:C - 1, e:e + 1], axis=0),
                                        orow[0:C - 1, e % RING, :], None, bounds_check=NTOK - 1, oob_is_err=False,
                                        compute_op=ALU.add).then_inc(ys[e % NACC], 16)

        @block.scalar
        def _(a):
            act_ = nc.scalar.activation
            a.wait_ge(s["ld_c"], 16)
            act_(sc[:], cts[:], ACT.Silu).then_inc(s["silu_c"], 1)
            a.wait_ge(s["silu_c"], 1)
            a.wait_ge(s["modt_ps"], 1)
            act_(modt[:].rearrange("p j b -> p (j b)"), ps[:, 0, 0:4 * B], ACT.Tanh).then_inc(s["modt_sb"], 1)
            a.wait_ge(s["modt_sb"], 1)
            act_(modt[:].rearrange("p j b -> p (j b)"), ps[:, 0, 0:4 * B], ACT.Copy).then_inc(s["modt_sb"], 1)

            def take(b, n):
                a.wait_ge(s["qkv_rdy"], cnt(b, n))
                a.wait_ge(s["ss_rdy"], cnt(b, n - 1) if not isinstance(n, int) or n > 0 else b * H)
                act_(sq, ps[:, 0:TT, 0:2 * DH].rearrange("p i (c d) -> p i c d", c=2), ACT.Square).then_inc(s["squared"], 1)
                act_(kr, ps[:, 0:TT, DH:2 * DH], ACT.Copy).then_inc(s["k_copied"], 1)
                dst = vx[:, bass.ds(vslot(n) * TT * (DH + 1), TT * (DH + 1))].rearrange("p (i d) -> p i d", i=TT)[:, :, 0:DH]
                a.wait_ge(s["ones_rdy"], 1)
                act_(dst, ps[:, 0:TT, 2 * DH:3 * DH], ACT.Copy).then_inc(s["v_copied"], 1)

            def cap(b, n):
                for q, (j, w) in ((1, (0, 512)), (2, (1, 384)), (2, (3, 128)), (3, (2, 256))):
                    a.wait_ge(s["s_rdy"], 3 * cnt(b, n - 1) + q)
                    act_(prob[:, OFF[j]:OFF[j] + w], sflat[:, OFF[j]:OFF[j] + w], ACT.Tanh,
                         scale=rn[:, bass.ds(n, 1), TT + j:TT + j + 1].squeeze(1)).then_inc(s["capped"], 1)

            def exps(b, n):
                a.wait_ge(s["capped"], 4 * cnt(b, n))
                act_(prob[:, 0:1280], prob[:, 0:1280], ACT.Exp, scale=CAP).then_inc(s["expd"], 1)

            def out_t(b, n):
                a.wait_ge(s["ot_ps"], cnt(b, n))
                act_(ot, ps[:, 7, :], ACT.Copy).then_inc(s["ot_rdy"], 1)

            with a.Fori(0, B) as b:
                take(b, 0)
                take(b, 1)
                cap(b, 0)
                exps(b, 0)
                take(b, 2)
                with a.Fori(1, H - 2) as p:
                    cap(b, p)
                    out_t(b, p - 1)
                    exps(b, p)
                    take(b, p + 2)
                for p in (H - 2, H - 1):
                    cap(b, p)
                    out_t(b, p - 1)
                    exps(b, p)
                out_t(b, H - 1)
                a.wait_ge(s["xt_ps"], 2 * b + 2)
                act_(ht[:], ps[:, 0:KC, :], ACT.Copy).then_inc(s["h2t_rdy"], 1)
                a.wait_ge(s["logit_ps"], b + 1)
                act_(logits[:, bass.ds(b * TT, TT), :], ps[:, 2, 0:TT * E].rearrange("p (i e) -> p i e", i=TT), ACT.Copy).then_inc(s["logit_sb"], 1)

            a.wait_ge(s["soft"], 2)
            act_(logits[:], logits[:], ACT.Exp).then_inc(s["rt_exp"], 1)

            with a.Fori(0, B) as b:
                for m, (m0, mw) in enumerate(MSC):
                    a.wait_ge(s["sg_ps"], b * 3 + (m + 1))
                    if m < 2:
                        a.wait_ge(s["sa_rdy"], b * 3 + max(m - 1, 0) if m else b * 3)
                    else:
                        a.wait_ge(s["sa_rdy"], b * 3 + 1)
                    act_(sg[0:mw, m % 2, :], ps[0:mw, 2 * (m % 2), :], ACT.Silu).then_inc(s["sg_act"], 1)

            def e_xgt(e, base):
                a.wait_ge(s["tr1_ps"], base + e + 1)
                act_(xgt[:, e % 2], ps[:, 0, 0:KC * C].rearrange("p (k c) -> p k c", k=KC), ACT.Copy).then_inc(s["xgt_rdy"], 1)

            def e_silu(e, base):
                a.wait_ge(s["gu_ps"], base + e + 1)
                act_(gact[:, e % 2], ps[0:C, 1 + e % 2, 0:M], ACT.Silu).then_inc(s["gact_rdy"], 1)

            def e_orow(e, base):
                a.wait_ge(s["dn_ps"], base + e + 1)
                if isinstance(base, int):
                    if e >= RING:
                        a.wait_ge(ys[e % NACC], 16 * ((e - RING) // NACC + 1))
                        a.wait_ge(o95s[e % RING], 16 * (e // RING))
                else:
                    a.wait_ge(ys[e % NACC], (base + e - RING + NACC - e % NACC) * (16 // NACC))
                    a.wait_ge(o95s[e % RING], (base + e - e % RING) * (16 // RING))
                act_(orow[:, e % RING, :], ps[0:C, 4 + e % 2, 0:D], ACT.Copy,
                     scale=wcol[:, bass.ds(base + e, 1)]).then_inc(s["orow_rdy"], 1)

            def e_period(e, base):
                if e == 0 and isinstance(base, int):
                    e_xgt(0, 0)
                if not (isinstance(base, int) and base + e + 1 >= E):
                    e_xgt(e + 1, base)
                e_silu(e, base)
                if not (isinstance(base, int) and base + e < 2):
                    e_orow(e - 2, base) if e >= 2 or isinstance(base, int) else e_orow(e - 2 + RING, base - RING)

            a.wait_ge(s["idx_rdy"], 4)
            for e in range(RING):
                e_period(e, 0)
            with a.Fori(1, E // RING - 1) as r:
                for e in range(RING):
                    e_period(e, r * RING)
            for e in range(E - RING, E):
                e_period(e, 0)
            e_orow(E - 2, 0)
            e_orow(E - 1, 0)

        @block.vector
        def _(v):
            tt, ts, cp = nc.vector.tensor_tensor, nc.vector.tensor_scalar, nc.vector.tensor_copy

            def hold(c):
                nc.vector.memset(holdv[:, c:c + 1], 0.0)

            def ln(l, b, before):
                v.wait_ge(s["x2_rdy"], before)
                hold(0)
                for i in range(TT):
                    nc.vector.bn_stats(bst[:, i, :], xs[:, bass.ds(b * TT + i, 1), :].squeeze(1)).then_inc(s["stats"], 1)
                v.wait_ge(s["stats"], TT * (l + 1))
                hold(1)
                for i in range(TT):
                    nc.vector.bn_aggr(mv[:, i, :], bst[:, i, :]).then_inc(s["aggr"], 1)
                v.wait_ge(s["aggr"], TT * (l + 1))
                v.wait_ge(s["rstd_rdy"], l + 1)
                for i in range(TT):
                    ts(xn[:, i, :], xs[:, bass.ds(b * TT + i, 1), :].squeeze(1), mv[:, i, 0:1], rstd[:, i:i + 1],
                       ALU.subtract, ALU.mult).then_inc(s["xn_rdy"], 1)

            v.wait_ge(s["silu_c"], 1)
            for k in range(KC):
                cp(scb[:, k], sc[:, k].unsqueeze(2).to_broadcast([P, B, P])).then_inc(s["scb_rdy"], 1)
            v.wait_ge(s["ld_small"], 32)
            tt(css[:].rearrange("p a h -> p (a h)"), css[:].rearrange("p a h -> p (a h)"), css[:].rearrange("p a h -> p (a h)"), ALU.mult).then_inc(s["g_rdy"], 1)
            tt(qkws[:, 0:1], qkws[:, 0:1], qkws[:, 1:2], ALU.mult).then_inc(s["g_rdy"], 1)
            v.wait_ge(s["g_rdy"], 2)
            tt(g[:], css[:, 0, :], css[:, 1, :], ALU.add).then_inc(s["g_rdy"], 1)
            v.wait_ge(s["g_rdy"], 3)
            ts(g[:], g[:], qkws[:, 0:1], DH ** -0.5 / CAP, ALU.mult, ALU.mult).then_inc(s["g_rdy"], 1)
            v.wait_ge(s["modt_sb"], 2)
            ts(modt[:, 2:4, :], modt[:, 2:4, :], 1.0, None, ALU.add).then_inc(s["modt_sb"], 1)
            for b in range(B):
                v.wait_ge(s["rows_ps"], b + 1)
                bk = (2 * b + 2) % 8
                cp(rows[:, b], ps[:, bk:bk + 2, :].rearrange("p a (u d) -> p (a u) d", d=D)).then_inc(s["rows_sb"], 1)
            v.wait_ge(s["rows_sb"], B)
            for n, c in enumerate((0, 3)):
                gate_rows = rows[:, :, c, :]
                ts(tmpg[:, 0, n], gate_rows, 0.0, 2.0, ALU.is_ge, ALU.mult).then_inc(s["clamp"], 1)
                nc.vector.scalar_tensor_tensor(out=tmpg[:, 1, n], in0=gate_rows, scalar=-1.0, in1=gate_rows, op0=ALU.mult, op1=ALU.max).then_inc(s["clamp"], 1)
            v.wait_ge(s["clamp"], 4)
            ts(tmpg[:, 1], tmpg[:, 1], 0.25, None, ALU.max).then_inc(s["clamp"], 1)
            ts(rows[:, :, 2, :], rows[:, :, 2, :], 1.0, None, ALU.add).then_inc(s["clamp"], 1)
            v.wait_ge(s["clamp"], 6)
            for n, c in enumerate((0, 3)):
                nc.vector.scalar_tensor_tensor(out=rows[:, :, c, :], in0=tmpg[:, 0, n], scalar=-1.0, in1=tmpg[:, 1, n], op0=ALU.add, op1=ALU.mult).then_inc(s["clamp"], 1)
            v.wait_ge(s["clamp"], 8)
            v.wait_ge(s["g_rdy"], 4)
            v.wait_ge(s["modt_sb"], 3)
            v.wait_ge(s["ld_x"], 16)

            def squares_sum(b, n):
                v.wait_ge(s["squared"], cnt(b, n))
                v.wait_ge(s["r_rdy"], cnt(b, n - 1))
                nc.vector.tensor_reduce(ss[:].rearrange("p (c i) -> p i c", c=2), sq, X, ALU.add).then_inc(s["ss_rdy"], 1)

            def q_scale(b, n):
                v.wait_ge(s["r_rdy"], cnt(b, n))
                v.wait_ge(s["v_copied"], cnt(b, n))
                tt(qn, ps[:, 0:TT, 0:DH], rn[:, bass.ds(n, 1), 0:TT].squeeze(1).unsqueeze(2).to_broadcast([P, TT, DH]), ALU.mult).then_inc(s["q_scaled"], 1)

            def qk_t(b, n):
                v.wait_ge(s["qt_ps"], cnt(b, n))
                cp(qt[:], ps[:, 2, :]).then_inc(s["qt_rdy"], 1)
                v.wait_ge(s["kt_ps"], cnt(b, n))
                ts(kt[:], ps[:, 3, :], g[:, bass.ds(n, 1)], None, ALU.mult).then_inc(s["kt_rdy"], 1)

            def y_add(b, n):
                v.wait_ge(s["y_rdy"], cnt(b, n))
                v.wait_ge(s["y_added"], cnt(b, n - 1))
                tt(yacc, yps, yacc, ALU.add).then_inc(s["y_added"], 1)

            def o_norm(b, n):
                v.wait_ge(s["o_rdy"], cnt(b, n))
                o3 = ps[:, 7, 0:3 * (DH + 1)].rearrange("p (i d) -> p i d", i=3)
                nc.vector.reciprocal(rden[:, 0:3], o3[:, :, DH]).then_inc(s["den_rdy"], 1)
                nc.vector.reciprocal(rden[:, 3:4], ps[:, 6, 256 + DH:257 + DH]).then_inc(s["den_rdy"], 1)
                v.wait_ge(s["den_rdy"], 2 * cnt(b, n))
                tt(on[:, 0:3, :], o3[:, :, 0:DH], rden[:, 0:3].unsqueeze(2).to_broadcast([P, 3, DH]), ALU.mult).then_inc(s["o_normed"], 1)
                ts(on[:, 3, :], ps[:, 6, 256:256 + DH], rden[:, 3:4], None, ALU.mult).then_inc(s["o_normed"], 1)

            with v.Fori(0, B) as b:
                ln(2 * b, b, 2 * b)
                v.wait_ge(s["xt_ps"], 2 * b + 1)
                for k in range(KC):
                    ts(ht[:, k, :], ps[:, k, :], modt[:, 2 + k, bass.ds(b, 1)], modt[:, k, bass.ds(b, 1)], ALU.mult, ALU.add).then_inc(s["ht_rdy"], 1)
                nc.vector.memset(yacc, 0.0).then_inc(s["yzero"], 1)
                squares_sum(b, 0)
                q_scale(b, 0)
                qk_t(b, 0)
                squares_sum(b, 1)
                q_scale(b, 1)
                qk_t(b, 1)
                squares_sum(b, 2)
                v.wait_ge(s["yzero"], b + 1)
                o_norm(b, 0)
                q_scale(b, 2)
                with v.Fori(1, H - 2) as p:
                    qk_t(b, p + 1)
                    squares_sum(b, p + 2)
                    y_add(b, p - 1)
                    o_norm(b, p)
                    q_scale(b, p + 2)
                qk_t(b, H - 1)
                y_add(b, H - 3)
                o_norm(b, H - 2)
                y_add(b, H - 2)
                o_norm(b, H - 1)
                y_add(b, H - 1)
                v.wait_ge(s["y_added"], cnt(b, H - 1))
                tt(yacc, yacc, rows[:, bass.ds(b, 1), 0:1, :].squeeze(1).to_broadcast([P, TT, D]), ALU.mult).then_inc(s["x2_rdy"], 1)
                v.wait_ge(s["x2_rdy"], 2 * b + 1)
                xb = xs[:, bass.ds(b * TT, TT), :]
                tt(xb, xb, yacc, ALU.add).then_inc(s["x2_rdy"], 1)
                ln(2 * b + 1, b, 2 * b + 2)
                v.wait_ge(s["xn_rdy"], TT * (2 * b + 2))
                tt(xn[:], xn[:], rows[:, bass.ds(b, 1), 2:3, :].squeeze(1).to_broadcast([P, TT, D]), ALU.mult).then_inc(s["hmod"], 1)
                v.wait_ge(s["hmod"], 2 * b + 1)
                tt(xn[:], xn[:], rows[:, bass.ds(b, 1), 1:2, :].squeeze(1).to_broadcast([P, TT, D]), ALU.add).then_inc(s["hmod"], 1)
                v.wait_ge(s["h2t_rdy"], 2 * b + 1)
                cp(h2t[:, :, bass.ds(b * T, T)], ps[:, 0:KC, :]).then_inc(s["h2t_rdy"], 1)
                v.wait_ge(s["h2_out"], 16 * b + 16)
                v.wait_ge(s["h2t_rdy"], 2 * b + 2)

            rt = [0]

            def step(ins):
                rt[0] += 1
                ins.then_inc(s["rt"], 1)
                v.wait_ge(s["rt"], rt[0])

            def e3(ap, n):
                return ap.unsqueeze(2).to_broadcast([P, NT, n])

            v.wait_ge(s["logit_sb"], B)
            v.wait_ge(s["consts"], 10)
            step(nc.vector.tensor_reduce(mx, logits[:], X, ALU.max))
            tt(logits[:], logits[:], e3(mx, E), ALU.subtract).then_inc(s["soft"], 2)
            v.wait_ge(s["rt_exp"], 1)
            step(nc.vector.tensor_reduce(rs, logits[:], X, ALU.add))
            step(nc.vector.reciprocal(rs, rs))
            step(tt(logits[:], logits[:], e3(rs, E), ALU.mult))
            step(nc.vector.tensor_reduce(gsc.rearrange("p i n -> p (i n)"), logits[:].rearrange("p i (n c) -> p (i n) c", n=NG), X, ALU.max))
            for i in range(NT):
                ins = nc.vector.max(g8[:, i, :], gsc[:, i, :])
                if i < NT - 1:
                    ins.then_inc(s["rt"], 1)
                    rt[0] += 1
            step(ins)
            for i in range(NT):
                ins = nc.vector.max_index(gi[:, i, :], g8[:, i, :], gsc[:, i, :])
                if i < NT - 1:
                    ins.then_inc(s["rt"], 1)
                    rt[0] += 1
            step(ins)
            step(cp(gif, gi))
            i8b = iota8[:].unsqueeze(1).to_broadcast([P, NT, NG])
            step(tt(gm, i8b, e3(gif[:, :, 0], NG), ALU.is_equal))
            for k in range(1, TG):
                step(tt(gm2, i8b, e3(gif[:, :, k], NG), ALU.is_equal))
                step(tt(gm, gm, gm2, ALU.add))
            step(tt(tmp.rearrange("p i (n c) -> p (i n) c", n=NG), logits[:].rearrange("p i (n c) -> p (i n) c", n=NG),
                    gm.rearrange("p i n -> p (i n)").unsqueeze(2).to_broadcast([P, NT * NG, GS]), ALU.mult))
            for i in range(NT):
                ins = nc.vector.max(w8[:, i, :], tmp[:, i, :])
                if i < NT - 1:
                    ins.then_inc(s["rt"], 1)
                    rt[0] += 1
            step(ins)
            for i in range(NT):
                ins = nc.vector.max_index(ei[:, i, :], w8[:, i, :], tmp[:, i, :])
                if i < NT - 1:
                    ins.then_inc(s["rt"], 1)
                    rt[0] += 1
            step(ins)
            step(cp(eif, ei))
            for k in range(K):
                step(tt(oh[:, :, k, :], iotae[:].unsqueeze(1).to_broadcast([P, NT, E]), e3(eif[:, :, k], E), ALU.is_equal))
            step(nc.vector.tensor_reduce(sel, oh.rearrange("p i k e -> p i e k"), X, ALU.add))
            step(nc.vector.memset(cum[:, 0, :], 0.0))
            for i in range(NT):
                step(tt(cum[:, i + 1, :], cum[:, i, :], sel[:, i, :], ALU.add))
            v.sem_inc(s["sel_rdy"], 1)
            v.wait_ge(s["pos_rdy"], 1)
            posv = ps[:, 6:8, :].rearrange("p a (i e) -> p (a i) e", e=E)
            step(ts(over, posv, float(C - 1), None, ALU.is_ge))
            step(tt(cum[:, 0:NT, :], posv, iota96[:].unsqueeze(1).to_broadcast([P, NT, E]), ALU.add))
            step(nc.vector.scalar_tensor_tensor(out=cum[:, 0:NT, :], in0=over, scalar=SKIP, in1=cum[:, 0:NT, :], op0=ALU.mult, op1=ALU.add))
            for k in range(K):
                step(tt(oh[:, :, k, :], oh[:, :, k, :], cum[:, 0:NT, :], ALU.mult))
            step(nc.vector.tensor_reduce(slotf, oh, X, ALU.add))
            step(cp(sloti, slotf.rearrange("p i k -> p (i k)")))
            step(cp(pair[:, :, :, 0], iotat[:].unsqueeze(2).to_broadcast([P, NT, K])))
            step(cp(pair[:, :, :, 1], w8[:, :, 0:K]))
            v.sem_inc(s["slot_rdy"], 1)
            step(tt(over, over, sel, ALU.mult))
            step(tt(over, over, tmp, ALU.mult))
            v.sem_inc(s["w95_rdy"], 1)
            step(ts(iotat[:], iotat[:], 1.0, None, ALU.add))
            step(tt(sel, sel, e3(iotat[:], E), ALU.mult))
            step(nc.vector.tensor_reduce(lastp, sel.rearrange("p i e -> p e i"), X, ALU.max))
            v.sem_inc(s["lastp_rdy"], 1)
            v.wait_ge(s["lastt_ps"], 1)
            step(nc.vector.tensor_reduce(lastr[:, 0:1], ps[0:E, 6, 0:P], X, ALU.max))
            step(ts(lastr[:, 0:1], lastr[:, 0:1], -1.0, 0.0, ALU.add, ALU.max))
            step(nc.vector.memset(lastr[:, 1:2], 1.0))
            v.sem_inc(s["lastp_rdy"], 2)
            for q in range(4):
                v.wait_ge(s["w95_ps"], q + 1)
                cp(w95t[:, q * T:(q + 1) * T], ps[0:E, 6 + q % 2, :]).then_inc(s["w95_sb"], 1)

            with v.Fori(0, B) as b:
                for m, (m0, mw) in enumerate(MSC):
                    v.wait_ge(s["sg_act"], b * 3 + (m + 1))
                    if m == 0:
                        v.wait_ge(s["sdn_ps"], 2 * b)
                    tt(acts[0:mw, m, :], ps[0:mw, 2 * (m % 2) + 1, :], sg[0:mw, m % 2, :], ALU.mult).then_inc(s["sa_rdy"], 1)
                for q in range(2):
                    v.wait_ge(s["sdn_ps"], 2 * b + (q + 1))
                    cp(shr[:, bass.ds(b * TT + 2 * q, 2), :], ps[:, 4 + q, :].rearrange("p (i d) -> p i d", i=2)).then_inc(s["shr_rdy"], 1)

            v.wait_ge(s["tabt"], 1)
            cp(idf, ps[0:C, 6, 0:E]).then_inc(s["tabt_sb"], 1)
            cp(wcol, ps[0:C, 6, E:2 * E]).then_inc(s["idx_rdy"], 1)
            v.wait_ge(s["tabt_sb"], 1)
            cp(sidx, idf).then_inc(s["idx_rdy"], 1)
            v.wait_ge(s["idx_rdy"], 2)
            ts(idf, idf, float(NTOK - 1), None, ALU.min).then_inc(s["idx_rdy"], 1)
            v.wait_ge(s["idx_rdy"], 3)
            cp(gidx, idf).then_inc(s["idx_rdy"], 1)

            def e_mul(e, base):
                v.wait_ge(s["gact_rdy"], base + e + 1)
                v.wait_ge(s["gu_ps"], base + e + 1)
                tt(act[:, e % 2], ps[0:C, 1 + e % 2, M:2 * M], gact[:, e % 2], ALU.mult).then_inc(s["act_rdy"], 1)

            def e_act_t(e, base):
                v.wait_ge(s["tr2_ps"], base + e + 1)
                cp(actt[:, e % 2], ps[0:MC, 3, 0:2 * C].rearrange("p (m c) -> p m c", m=2)).then_inc(s["actt_rdy"], 1)

            def e_period(e, base):
                e_mul(e, base)
                if not (isinstance(base, int) and base + e < 1):
                    e_act_t(e - 1, base)

            for e in range(2):
                e_period(e, 0)
            with v.Fori(0, (E - 2) // 2) as r:
                e_period(2, r * 2)
                e_period(3, r * 2)
            e_act_t(E - 1, 0)

            v.wait_ge(s["acc_ld"], 16 * NACC)
            v.wait_ge(s["shr_rdy"], 2 * B)
            for b in range(B):
                sl = slice(b * TT, (b + 1) * TT)
                tt(accs[0][:, sl], accs[0][:, sl], accs[1][:, sl], ALU.add).then_inc(s["cmb2"], 1)
                v.wait_ge(s["cmb2"], 5 * b + 1)
                tt(accs[0][:, sl], accs[0][:, sl], shr[:, sl], ALU.add).then_inc(s["cmb2"], 1)
                v.wait_ge(s["cmb2"], 5 * b + 2)
                v.wait_ge(s["cmb_ps"], b + 1)
                tt(accs[0][:, sl], ps[:, 2 * b:2 * b + 2, :].rearrange("p a (u d) -> p (a u) d", d=D), accs[0][:, sl], ALU.add).then_inc(s["cmb2"], 1)
                v.wait_ge(s["cmb2"], 5 * b + 3)
                tt(accs[0][:, sl], accs[0][:, sl], rows[:, b, 3:4, :].to_broadcast([P, TT, D]), ALU.mult).then_inc(s["cmb2"], 1)
                v.wait_ge(s["cmb2"], 5 * b + 4)
                tt(xs[:, sl], xs[:, sl], accs[0][:, sl], ALU.add).then_inc(s["cmb"], 4)
                v.sem_inc(s["cmb2"], 1)

        @block.tensor
        def _(pe):
            mm = pe.matmul
            pe.wait_ge(s["ld_wmod"], 16)
            pe.wait_ge(s["silu_c"], 1)
            for j in range(4):
                for k in range(KC):
                    last = mm(ps[:, 0, j * B:(j + 1) * B], wmods[:, k, j * P:(j + 1) * P], sc[:, k, :], start=(k == 0), stop=(k == KC - 1))
            last.then_inc(s["modt_ps"], 1)
            pe.wait_ge(s["scb_rdy"], KC)
            for b in range(B):
                if b == B - 1:
                    pe.wait_ge(s["modt_sb"], 2)
                for h in range(2):
                    for k in range(KC):
                        last = mm(ps[:, (2 * b + 2 + h) % 8, :], scb[:, k, b, :], wmods[:, k, 2 * D + h * T:2 * D + (h + 1) * T],
                                  start=(k == 0), stop=(k == KC - 1))
                last.then_inc(s["rows_ps"], 1)

            def xn_t(l):
                for k in range(KC):
                    for i in range(TT):
                        last = pe.transpose(ps[:, k, i * P:(i + 1) * P], xn[:, i, k * P:(k + 1) * P], ident[:])
                last.then_inc(s["xt_ps"], 1)

            def qkv(b, n):
                pe.wait_ge(s["v_copied"], cnt(b, n - 1))
                pe.wait_ge(s["q_scaled"], cnt(b, n - 1))
                for i in range(TT):
                    if i == 2:
                        pe.wait_ge(s["qt_rdy"], cnt(b, n - 1))
                    if i == 3:
                        pe.wait_ge(s["kt_rdy"], cnt(b, n - 1))
                    for k in range(KC):
                        last = mm(ps[:, i, 0:3 * DH], ht[:, k, i * P:(i + 1) * P], wq[:, k, bass.ds(n, 1), :].squeeze(1),
                                  start=(k == 0), stop=(k == KC - 1))
                last.then_inc(s["qkv_rdy"], 1)

            def qk_t(b, n):
                pe.wait_ge(s["q_scaled"], cnt(b, n))
                pe.wait_ge(s["v_copied"], cnt(b, n))
                for i in range(TT):
                    last = pe.transpose(ps[:, 2, i * P:(i + 1) * P], qn[:, i, :], ident[:])
                last.then_inc(s["qt_ps"], 1)
                for i in range(TT):
                    last = pe.transpose(ps[:, 3, i * P:(i + 1) * P], kr[:, i, :], ident[:])
                last.then_inc(s["kt_ps"], 1)

            def scores(b, n):
                pe.wait_ge(s["qt_rdy"], cnt(b, n))
                pe.wait_ge(s["kt_rdy"], cnt(b, n))
                pe.wait_ge(s["y_added"], cnt(b, n - 2))
                for j, w in ((0, 512), (1, 384), (3, 128), (2, 256)):
                    if j == 2:
                        pe.wait_ge(s["o_normed"], 2 * cnt(b, n - 1))
                    last = mm(sflat[:, OFF[j]:OFF[j] + w], kt[:, j * P:(j + 1) * P], qt[:, T - w:T], start=True, stop=True)
                    if j != 1:
                        last.then_inc(s["s_rdy"], 1)

            def o_t(b, n):
                pe.wait_ge(s["o_normed"], 2 * cnt(b, n))
                for i in range(TT):
                    last = pe.transpose(ps[:, 7, i * P:(i + 1) * P], on[:, i, :], ident[:])
                last.then_inc(s["ot_ps"], 1)

            def proj(b, n):
                pe.wait_ge(s["ot_rdy"], cnt(b, n))
                for i in range(TT):
                    last = mm(yps[:, i, :], ot[:, i * P:(i + 1) * P], wos[:, bass.ds(n, 1), :].squeeze(1), start=True, stop=True)
                last.then_inc(s["y_rdy"], 1)

            def pv(b, n):
                pe.wait_ge(s["p_rdy"], 2 * cnt(b, n))
                pe.wait_ge(s["ot_rdy"], cnt(b, n - 1))
                for i in range(TT):
                    o = ps[:, 7, i * (DH + 1):(i + 1) * (DH + 1)] if i < 3 else ps[:, 6, 256:257 + DH]
                    for j in range(i + 1):
                        c = OFF[j] + (i - j) * P
                        last = mm(o, prob[:, c:c + P], vx[:, bass.ds((vslot(n) * TT + j) * (DH + 1), DH + 1)],
                                  start=(j == 0), stop=(j == i))
                last.then_inc(s["o_rdy"], 1)

            pe.wait_ge(s["consts"], 4)
            pe.wait_ge(s["rows_sb"], B)
            pe.wait_ge(s["ld_wqkv"], 16)
            pe.wait_ge(s["ld_wo"], 16)
            pe.wait_ge(s["ld_gate"], 16)
            with pe.Fori(0, B) as b:
                pe.wait_ge(s["xn_rdy"], TT * (2 * b + 1))
                xn_t(2 * b)
                pe.wait_ge(s["logit_sb"], b)
                pe.wait_ge(s["ht_rdy"], KC * (b + 1))
                qkv(b, 0)
                qk_t(b, 0)
                qkv(b, 1)
                scores(b, 0)
                qk_t(b, 1)
                qkv(b, 2)
                pv(b, 0)
                with pe.Fori(1, H - 2) as p:
                    scores(b, p)
                    o_t(b, p - 1)
                    qk_t(b, p + 1)
                    qkv(b, p + 2)
                    pe.wait_ge(s["capped"], 4 * cnt(b, p))
                    proj(b, p - 1)
                    pv(b, p)
                scores(b, H - 2)
                o_t(b, H - 3)
                qk_t(b, H - 1)
                pe.wait_ge(s["capped"], 4 * cnt(b, H - 2))
                proj(b, H - 3)
                pv(b, H - 2)
                scores(b, H - 1)
                o_t(b, H - 2)
                pe.wait_ge(s["capped"], 4 * cnt(b, H - 1))
                proj(b, H - 2)
                pv(b, H - 1)
                o_t(b, H - 1)
                pe.wait_ge(s["y_added"], cnt(b, H - 2))
                proj(b, H - 1)
                pe.wait_ge(s["hmod"], 2 * b + 2)
                xn_t(2 * b + 1)
                pe.wait_ge(s["h2t_rdy"], 2 * b + 2)
                for i in range(TT):
                    for k in range(KC):
                        last = mm(ps[:, 2, i * E:(i + 1) * E], ht[:, k, i * P:(i + 1) * P], gates[:, k, :], start=(k == 0), stop=(k == KC - 1))
                last.then_inc(s["logit_ps"], 1)

            pe.wait_ge(s["logit_sb"], B)
            pe.wait_ge(s["sel_rdy"], 1)
            for q in range(2):
                n = NT // 2
                mm(ps[:, 6 + q, :], tri[:], sel[:, q * n:(q + 1) * n, :].rearrange("p i e -> p (i e)"), start=True, stop=False)
                last = mm(ps[:, 6 + q, :], ones[:], cum[:, q * n:(q + 1) * n, :].rearrange("p i e -> p (i e)"), start=False, stop=True)
            last.then_inc(s["pos_rdy"], 1)
            pe.wait_ge(s["lastp_rdy"], 1)
            pe.transpose(ps[0:E, 6, 0:P], lastp, ident[:]).then_inc(s["lastt_ps"], 1)
            pe.wait_ge(s["lastp_rdy"], 3)
            for q in range(4):
                if q >= 2:
                    pe.wait_ge(s["w95_sb"], q - 1)
                for i in range(TT):
                    last = pe.transpose(ps[0:E, 6 + q % 2, i * P:(i + 1) * P], over[:, q * TT + i, :], ident[:])
                last.then_inc(s["w95_ps"], 1)

            pe.wait_ge(s["ld_sh"], 48)
            with pe.Fori(0, B) as b:
                for m, (m0, mw) in enumerate(MSC):
                    pe.wait_ge(s["sa_rdy"], b * 3 + (m - 1) if m else b * 3)
                    for u in range(2):
                        for k in range(KC):
                            last = mm(ps[0:mw, 2 * (m % 2) + u, :], sgus[:, k, u, m0:m0 + mw], h2t[:, k, bass.ds(b * T, T)],
                                      start=(k == 0), stop=(k == KC - 1))
                    last.then_inc(s["sg_ps"], 1)
                pe.wait_ge(s["sa_rdy"], b * 3 + 3)
                for q in range(2):
                    pe.wait_ge(s["shr_rdy"], 2 * b)
                    for i in range(2 * q, 2 * q + 2):
                        for m, (m0, mw) in enumerate(MSC):
                            last = mm(ps[:, 4 + q, (i % 2) * D:(i % 2 + 1) * D], acts[0:mw, m, i * P:(i + 1) * P], sds[0:mw, m, :],
                                      start=(m == 0), stop=(m == 2))
                    last.then_inc(s["sdn_ps"], 1)

            pe.wait_ge(s["tabl"], 16)
            pe.wait_ge(s["w95_sb"], 4)
            pe.wait_ge(s["shr_rdy"], 2 * B)
            for c in range(2):
                last = pe.transpose(ps[0:C, 6, c * E:(c + 1) * E], tabs[:, :, c], ident[0:E, 0:E])
            last.then_inc(s["tabt"], 1)

            def tr1(e, base, use):
                pe.wait_ge(xg_in[e % XR], 16 * use)
                pe.wait_ge(s["xgt_rdy"], base + e)
                for k in range(KC):
                    last = pe.transpose(ps[:, 0, k * C:(k + 1) * C], xg[0:C, e % XR, k * P:(k + 1) * P], ident[0:C, 0:C])
                last.then_inc(s["tr1_ps"], 1)

            def gu(e, base, use):
                pe.wait_ge(s["xgt_rdy"], base + e + 1)
                pe.wait_ge(w_in[e % RING], 32 * use)
                for k in range(KC):
                    last = mm(ps[0:C, 1 + e % 2, 0:2 * M], xgt[:, e % 2, k, :], wgus[:, e % RING, k, :], start=(k == 0), stop=(k == KC - 1))
                last.then_inc(s["gu_ps"], 1)

            def tr2(e, base):
                pe.wait_ge(s["act_rdy"], base + e + 1)
                pe.wait_ge(s["actt_rdy"], base + e)
                for m in range(2):
                    last = pe.transpose(ps[0:MC, 3, m * C:(m + 1) * C], act[:, e % 2, m * MC:(m + 1) * MC], ident[0:C, 0:C])
                last.then_inc(s["tr2_ps"], 1)

            def down(e, base):
                pe.wait_ge(s["actt_rdy"], base + e + 1)
                if not (isinstance(base, int) and base + e < 2):
                    pe.wait_ge(s["orow_rdy"], base + e - 1)
                for m in range(2):
                    last = mm(ps[0:C, 4 + e % 2, 0:D], actt[:, e % 2, m, :], wds[:, e % RING, m, :], start=(m == 0), stop=(m == 1))
                last.then_inc(s["dn_ps"], 1)

            def period(e, base, r):
                static = isinstance(base, int)
                if not (static and base + e + 1 >= E):
                    tr1(e + 1, base, r + 1 if e + 1 < XR else r + 2)
                gu(e, base, (XR // RING) * r + (e // RING + 1))
                if not (static and base + e < 1):
                    tr2(e + XR - 1, base - XR) if e < 1 else tr2(e - 1, base)
                if not (static and base + e < 2):
                    down(e + XR - 2, base - XR) if e < 2 else down(e - 2, base)

            pe.wait_ge(s["idx_rdy"], 4)
            tr1(0, 0, 1)
            for e in range(XR):
                period(e, 0, 0)
            with pe.Fori(1, E // XR - 1) as r:
                for e in range(XR):
                    period(e, r * XR, r)
            for e in range(XR):
                period(e, E - XR, E // XR - 1)
            down(E - 2, 0)
            tr2(E - 1, 0)
            down(E - 1, 0)

            pe.wait_ge(s["o95_ld"], 16)
            pe.wait_ge(s["orow_rdy"], E)
            for b in range(B):
                for i in range(TT):
                    t = b * TT + i
                    last = mm(ps[:, 2 * b + i // 2, (i % 2) * D:(i % 2 + 1) * D], w95t[:, t * P:(t + 1) * P], o95, start=True, stop=True)
                last.then_inc(s["cmb_ps"], 1)


def kernel(**inputs):
    import numpy as np
    import concourse.bacc as bacc
    from concourse.bass_utils import run_bass_kernel_spmd as run

    def a(name):
        return np.asarray(inputs[name])

    def headw(name):
        return a(name).reshape(H, DH, D).transpose(2, 0, 1)

    c = np.ascontiguousarray
    arrays = {
        "x": a("L0_attn_x").reshape(NTOK, D),
        "wqkv": np.concatenate([headw("L0_attn_wq"), headw("L0_attn_wk"), headw("L0_attn_wv")], axis=2)
                .reshape(KC, P, H, 3 * DH).transpose(1, 0, 2, 3),
        "wo": a("L0_attn_wo").reshape(D, H, DH).transpose(2, 1, 0),
        "qkw": np.stack([a("L0_attn_q_norm_w"), a("L0_attn_k_norm_w")], axis=1),
        "cossin": np.stack([np.repeat(a("L0_attn_rope_cos")[:H].T, 2, axis=0),
                            np.repeat(a("L0_attn_rope_sin")[:H].T, 2, axis=0)], axis=1),
        "ct": a("L0_c").T.reshape(KC, P, B).transpose(1, 0, 2),
        "wmod": a("L0_wmod").reshape(KC, P, 6 * D).transpose(1, 0, 2),
        "gate": a("L0_ffn_gate_weight").T.reshape(KC, P, E).transpose(1, 0, 2),
        "sgu": np.stack([a("L0_ffn_Sg").T, a("L0_ffn_Su").T], axis=1).reshape(KC, P, 2, MS).transpose(1, 0, 2, 3),
        "sd": a("L0_ffn_Sd").T,
        "wgu": np.concatenate([a("L0_ffn_Wg"), a("L0_ffn_Wu")], axis=1).transpose(0, 2, 1)
               .reshape(E, KC, P, 2 * M).transpose(0, 2, 1, 3),
        "wd": a("L0_ffn_Wd").transpose(0, 2, 1).reshape(E, 2, MC, D).transpose(0, 2, 1, 3),
    }
    nc = bacc.Bacc("TRN2", target_bir_lowering=False, num_devices=1)
    feed, args = {}, []
    for name, v in arrays.items():
        feed[f"in_{name}"] = c(v)
        args.append(nc.dram_tensor(f"in_{name}", v.shape, F32, kind="ExternalInput").ap())
    args.append(nc.dram_tensor("out_0", (NTOK, D), F32, kind="ExternalOutput").ap())
    build(nc, *args)
    r = run(nc, [feed], core_ids=[0])
    return r.results[0]["out_0"].reshape(B, T, D)
```

```python
from contextlib import ExitStack

import concourse.bass as bass
from concourse import mybir

F32 = mybir.dt.float32
I32 = mybir.dt.int32
U32 = mybir.dt.uint32
ALU = mybir.AluOpType
ACT = mybir.ActivationFunctionType
X = mybir.AxisListType.X

P = 128
B, T, D = 4, 512, 256
TT = T // P
NT = B * TT
NTOK = B * T
KC = D // P
H, DH = 16, 128
CAP = 50.0
E, M = 64, 176
MC = 88
MS = 352
K, NG, GS, TG = 6, 8, 8, 3
C = 96
MSC = [(0, 128), (128, 128), (256, 96)]
OFF = [0, 512, 1024, 896]
PW = 1536
RING = 4
XR = 8
AHEAD = 7
SIDE = 5
PEEL = 12
NACC = 2
SKIP = 8192.0
NOTOK = 4096.0


def build(nc, x, wqkv, wo, qkw, cossin, ct, wmod, gate, sgu, sd, wgu, wd, out):
    with ExitStack() as ctx:
        def sb(name, shape, dt=F32):
            return ctx.enter_context(nc.sbuf_tensor(name, shape, dt))

        def sem(name):
            return ctx.enter_context(nc.semaphore(name))

        ps = ctx.enter_context(nc.psum_tensor("ps", [P, 8, 512], F32))

        h2_d = nc.dram_tensor("h2_rows", (NTOK, D), F32, kind="Internal").ap()
        tab_d = nc.dram_tensor("slot_table", (E * C, 2), F32, kind="Internal").ap()
        acc_d = [nc.dram_tensor(f"acc{a}", (NTOK, D), F32, kind="Internal").ap() for a in range(NACC)]
        o95_d = nc.dram_tensor("last_rows", (E, D), F32, kind="Internal").ap()

        xs = sb("xs", [P, NT, D])
        rows = sb("rows", [P, B, 4, D])
        modt = sb("modt", [P, 4, B])
        h2t = sb("h2t", [P, KC, NTOK])
        logits = sb("logits", [P, NT, E])
        ident = sb("ident", [P, P])
        neghalf = sb("neghalf", [P, 8])
        gates = sb("gates", [P, KC, E])
        wgus = sb("wgus", [P, RING, KC, 2 * M])
        wds = sb("wds", [MC, RING, 2, D])
        warena = sb("warena", [P, KC * H * 3 * DH])
        wq = warena[:].rearrange("p (k h c) -> p k h c", k=KC, h=H)
        wos = sb("wos", [P, H, D])
        arena2 = sb("arena2", [P, 8704])
        at = [0]

        def part(n):
            v = arena2[:, at[0]:at[0] + n]
            at[0] += n
            return v

        ht = sb("ht", [P, KC, T])
        xn = sb("xn", [P, TT, D])
        qt = sb("qt", [P, T])
        kt = sb("kt", [P, T])
        prob = sb("prob", [P, PW])
        vx = sb("vx", [P, 4 * TT * (DH + 1)])
        sq = part(TT * 2 * DH).rearrange("p (i c d) -> p i c d", i=TT, c=2)
        qn = part(TT * DH).rearrange("p (i d) -> p i d", i=TT)
        kr = part(TT * DH).rearrange("p (i d) -> p i d", i=TT)
        on = part(TT * DH).rearrange("p (i d) -> p i d", i=TT)
        ot = part(T)
        yacc = part(TT * D).rearrange("p (i d) -> p i d", i=TT)
        wmods = part(KC * 6 * D).rearrange("p (k n) -> p k n", k=KC)
        scb = part(KC * B * P).rearrange("p (k b m) -> p k b m", k=KC, b=B)
        tmpg = h2t[:].rearrange("p k t -> p (k t)").rearrange("p (a c b d) -> p a c b d", a=2, b=B, c=2)
        h2s = wmods[:, :, 0:T]
        ss = sb("ss", [P, 2 * TT])
        rtmp = sb("rtmp", [P, 2 * TT])
        rn = sb("rn", [P, H, 2 * TT])
        rden = sb("rden", [P, TT])
        g = sb("g", [P, H])
        qkws = sb("qkws", [P, 2])
        css = sb("css", [P, 2, H])
        cts = sb("cts", [P, KC, B])
        sc = sb("sc", [P, KC, B])
        bst = sb("bst", [P, TT, 6])
        mv = sb("mv", [P, TT, 2])
        rstd = sb("rstd", [P, TT])
        holdp = sb("holdp", [P, 4])
        holdv = sb("holdv", [P, 2])

        apos = [0]

        def again(shape, dt=F32, parts=P):
            n = 1
            for s in shape:
                n *= s
            v = warena[0:parts, apos[0]:apos[0] + n]
            apos[0] += n
            assert apos[0] <= KC * H * 3 * DH
            if dt != F32:
                v = v.bitcast(dt)
            if len(shape) == 2:
                return v.rearrange("p (a b) -> p a b", a=shape[0])
            if len(shape) == 3:
                return v.rearrange("p (a b c) -> p a b c", a=shape[0], b=shape[1])
            return v

        oh = again([NT, K, E])
        sel = again([NT, E])
        cum = again([NT + 1, E])
        tmp = again([NT, E])
        over = again([NT, E])
        sgus = again([KC * 2, MS]).rearrange("p (k u) m -> p k u m", k=KC)
        sds = wos[:, 8:11, :]
        acts = arena2[:, 0:3 * T].rearrange("p (m t) -> p m t", m=3)
        sg = arena2[:, 3 * T:5 * T].rearrange("p (a t) -> p a t", a=2)
        shr = arena2[:, 5 * T:5 * T + NT * D].rearrange("p (i d) -> p i d", i=NT)
        w95t = arena2[0:E, 5 * T + NT * D:5 * T + NT * D + NTOK]
        assert 5 * T + NT * D + NTOK <= 8704 and at[0] <= 8704
        small = prob
        mx = small[:, 0:16]
        rs = small[:, 16:32]
        gsc = small[:, 32:160].rearrange("p (i n) -> p i n", i=NT)
        g8 = small[:, 160:288].rearrange("p (i n) -> p i n", i=NT)
        gi = small[:, 288:416].bitcast(U32).rearrange("p (i n) -> p i n", i=NT)
        gif = small[:, 416:544].rearrange("p (i n) -> p i n", i=NT)
        gm = small[:, 544:672].rearrange("p (i n) -> p i n", i=NT)
        gm2 = small[:, 672:800].rearrange("p (i n) -> p i n", i=NT)
        w8 = small[:, 800:928].rearrange("p (i n) -> p i n", i=NT)
        ei = small[:, 928:1056].bitcast(U32).rearrange("p (i n) -> p i n", i=NT)
        eif = small[:, 1056:1184].rearrange("p (i n) -> p i n", i=NT)
        slotf = small[:, 1184:1280].rearrange("p (i n) -> p i n", i=NT)
        sloti = small[:, 1280:1376].bitcast(I32)
        lastp = small[:, 1376:1440]
        pair = vx[:, 0:192].rearrange("p (i k c) -> p i k c", i=NT, k=K)
        lastr = vx[0:E, 192:194]
        tabs = vx[0:E, 200:392].rearrange("p (s c) -> p s c", c=2)
        gidx = vx[0:C, 392:456].bitcast(I32)
        sidx = vx[0:C, 456:520].bitcast(I32)
        idf = vx[0:C, 520:584]
        wcol = vx[0:C, 584:648]
        o95 = vx[0:E, 648:904]
        xg = arena2[:, 0:XR * D].rearrange("p (u d) -> p u d", u=XR)
        xgt = qt[:, 0:2 * KC * C].rearrange("p (u k c) -> p u k c", u=2, k=KC)
        gact = kt[0:C, 0:2 * M].rearrange("p (u m) -> p u m", u=2)
        act = ht[0:C, 0, 0:2 * M].rearrange("p (u m) -> p u m", u=2)
        actt = ht[0:MC, 1, 0:4 * C].rearrange("p (u m c) -> p u m c", u=2, m=2)
        orow = wos[0:C, 0:RING, :]
        accs = [warena[:, a * NT * D:(a + 1) * NT * D].rearrange("p (i d) -> p i d", i=NT) for a in range(NACC)]

        tri = sb("tri", [P, P])
        ones = sb("ones", [P, P])
        iota8 = sb("iota8", [P, NG])
        iotae = sb("iotae", [P, E])
        iota96 = sb("iota96", [P, E])
        iotat = sb("iotat", [P, NT])
        fill = sb("fill", [E, C, 2])
        zrow = sb("zrow", [P, D])

        names = """ld_x ld_c ld_wmod ld_small ld_wqkv ld_wo ld_gate ld_sh consts fills zeros tables
            silu_c scb_rdy modt_ps rows_ps modt_sb rows_sb clamp g_rdy
            stats aggr var_eps rstd_rdy xn_rdy hmod xt_ps ht_rdy h2t_rdy h2_out logit_ps logit_sb
            qkv_rdy squared k_copied v_copied ss_rdy r_tmp r_rdy q_scaled qt_ps kt_ps qt_rdy kt_rdy
            s_rdy capped expd p_rdy o_rdy den_rdy o_normed ot_ps ot_rdy y_rdy y_added h2s_rdy x2_rdy
            ones_rdy rt soft rt_exp sel_rdy pos_rdy lastp_rdy lastt_ps slot_rdy tabw tabl tabr tabt tabt_sb
            last_out w95_rdy w95_ps w95_sb idx_rdy sg_ps sg_act sa_rdy sdn_ps shr_rdy
            tr1_ps xgt_rdy gu_ps gact_rdy act_rdy tr2_ps actt_rdy dn_ps orow_rdy
            acc_ld o95_ld cmb_ps cmb cmb2 outd""".split()
        s = {n: sem(n) for n in names}
        xg_in = [sem(f"xg_in{i}") for i in range(XR)]
        w_in = [sem(f"w_in{i}") for i in range(RING)]
        ys = [sem(f"ys{a}") for a in range(NACC)]
        o95s = [sem(f"o95s{i}") for i in range(RING)]

        block = ctx.enter_context(nc.Block())

        sflat = ps[:, 4:7, :].rearrange("p a c -> p (a c)")
        yps = ps[:, 4:6, :].rearrange("p a (u d) -> p (a u) d", d=D)

        def cnt(b, n):
            return b * H + (n + 1)

        def head(n):
            return n % H if isinstance(n, int) else n

        def some(count):
            return not (isinstance(count, int) and count <= 0)

        def has_before(b):
            return not (isinstance(b, int) and b == 0)

        def is_last(b):
            return isinstance(b, int) and b == B - 1

        def ln1(b):
            return 0 if isinstance(b, int) and b == 0 else 2 * b - 1

        def ln2(b):
            return 2 * B - 1 if is_last(b) else 2 * b + 2

        def vslot(n):
            return n % 4

        @block.sync
        def _(sp):
            sp.dma_start(cts[:], ct).then_inc(s["ld_c"], 16)
            sp.dma_start(wmods, wmod).then_inc(s["ld_wmod"], 16)
            sp.dma_start(xs[:], x.rearrange("(i p) d -> p i d", p=P)).then_inc(s["ld_x"], 16)
            sp.dma_start(qkws[:], qkw).then_inc(s["ld_small"], 16)
            sp.dma_start(css[:], cossin).then_inc(s["ld_small"], 16)
            sp.dma_start(wq, wqkv).then_inc(s["ld_wqkv"], 16)
            sp.dma_start(wos[:], wo).then_inc(s["ld_wo"], 16)
            sp.dma_start(gates[:], gate).then_inc(s["ld_gate"], 16)
            for u in range(RING):
                sp.dma_start(wgus[:, u], wgu[u]).then_inc(w_in[u], 16)
                sp.dma_start(wds[:, u], wd[u]).then_inc(w_in[u], 16)
            sp.wait_ge(s["fills"], 2)
            sp.dma_start(tab_d.rearrange("(e s) c -> e (s c)", e=E), fill[:].rearrange("e s c -> e (s c)")).then_inc(s["tables"], 16)
            sp.wait_ge(s["zeros"], 1)
            for a in range(NACC):
                sp.dma_start(acc_d[a].rearrange("(i p) d -> p i d", p=P),
                             zrow[:].unsqueeze(1).to_broadcast([P, NT, D])).then_inc(s["tables"], 16)
            with sp.Fori(0, B) as b:
                sp.wait_ge(s["hmod"], 2 * b + 2)
                sp.dma_start(h2_d.rearrange("(b i p) d -> p b i d", b=B, p=P)[:, bass.ds(b, 1)].squeeze(1), xn[:]).then_inc(s["h2_out"], 16)
            sp.wait_ge(s["logit_ps"], B)
            sp.dma_start(sgus, sgu).then_inc(s["ld_sh"], 16)
            sp.dma_start(sds[:, 0:2, :], sd[0:2 * P, :].rearrange("(m p) d -> p m d", p=P)).then_inc(s["ld_sh"], 16)
            sp.dma_start(sds[0:MS - 2 * P, 2, :], sd[2 * P:MS, :]).then_inc(s["ld_sh"], 16)
            sp.wait_ge(s["lastp_rdy"], 3)
            sp.wait_ge(s["tables"], 16 * (1 + NACC))
            sp.wait_ge(s["tabw"], 16 * NT * K)
            sp.dma_start(tab_d.rearrange("(e s) c -> e s c", e=E)[:, C - 1, :], lastr).then_inc(s["last_out"], 16)
            sp.wait_ge(s["last_out"], 16)
            sp.dma_start(tabs.rearrange("e s c -> e (s c)"), tab_d.rearrange("(e s) c -> e (s c)", e=E)).then_inc(s["tabl"], 16)
            with sp.Fori(0, E // RING - 1) as r:
                for u in range(RING):
                    sp.wait_ge(s["dn_ps"], r * RING + (u + 1))
                    sp.dma_start(wgus[:, u], wgu[bass.ds((r + 1) * RING + u, 1)].squeeze(0)).then_inc(w_in[u], 16)
                    sp.dma_start(wds[:, u], wd[bass.ds((r + 1) * RING + u, 1)].squeeze(0)).then_inc(w_in[u], 16)
                    sp.wait_ge(s["orow_rdy"], r * RING + (u + 1))
                    sp.dma_start(o95_d[bass.ds(r * RING + u, 1)], orow[C - 1:C, u, :]).then_inc(o95s[u], 16)
            for u in range(RING):
                sp.wait_ge(s["orow_rdy"], E - RING + u + 1)
                sp.dma_start(o95_d[E - RING + u:E - RING + u + 1], orow[C - 1:C, u, :]).then_inc(o95s[u], 16)
            for u in range(RING):
                sp.wait_ge(o95s[u], 16 * (E // RING))
            sp.dma_start(o95, o95_d).then_inc(s["o95_ld"], 16)
            for a in range(NACC):
                sp.wait_ge(ys[a], 16 * (E // NACC))
                sp.dma_start(accs[a], acc_d[a].rearrange("(i p) d -> p i d", p=P)).then_inc(s["acc_ld"], 16)
            for b in range(B):
                sp.wait_ge(s["cmb"], 4 * (b + 1))
                sp.dma_start(out[b * T:(b + 1) * T].rearrange("(i p) d -> p i d", p=P), xs[:, b * TT:(b + 1) * TT, :]).then_inc(s["outd"], 16)
            sp.wait_ge(s["outd"], 16 * B)
            sp.wait_ge(s["h2_out"], 16 * B)

        @block.gpsimd
        def _(pool):
            def hold(c):
                pool.tensor_tensor(holdp[:, c:c + 1], neghalf[:, 0:1], neghalf[:, 0:1], ALU.mult)

            pool.memset(ident[:], 0.0).then_inc(s["consts"], 1)
            pool.memset(tri[:], 1.0).then_inc(s["consts"], 1)
            pool.memset(neghalf[:], -0.5).then_inc(s["consts"], 1)
            pool.wait_ge(s["consts"], 3)
            pool.affine_select(out=ident[:], in_=ident[:], compare_op=ALU.not_equal, fill=1.0, base=0,
                               pattern=[[-1, P]], channel_multiplier=1).then_inc(s["consts"], 1)
            pool.affine_select(out=tri[:], in_=tri[:], compare_op=ALU.is_gt, fill=0.0, base=0,
                               pattern=[[1, P]], channel_multiplier=-1).then_inc(s["consts"], 1)
            pool.memset(ones[:], 1.0).then_inc(s["consts"], 1)
            pool.memset(vx[:], 1.0).then_inc(s["ones_rdy"], 1)
            pool.memset(zrow[:], 0.0).then_inc(s["zeros"], 1)
            pool.memset(fill[:, :, 0:1], NOTOK).then_inc(s["fills"], 1)
            pool.memset(fill[:, :, 1:2], 0.0).then_inc(s["fills"], 1)
            pool.iota(iota8[:], pattern=[[1, NG]], base=0, channel_multiplier=0, allow_small_or_imprecise_dtypes=True).then_inc(s["consts"], 1)
            pool.iota(iotae[:], pattern=[[1, E]], base=0, channel_multiplier=0, allow_small_or_imprecise_dtypes=True).then_inc(s["consts"], 1)
            pool.iota(iota96[:], pattern=[[C, E]], base=0, channel_multiplier=0, allow_small_or_imprecise_dtypes=True).then_inc(s["consts"], 1)
            pool.iota(iotat[:], pattern=[[P, NT]], base=0, channel_multiplier=1, allow_small_or_imprecise_dtypes=True).then_inc(s["consts"], 1)

            def ln_rstd(l):
                pool.wait_ge(s["aggr"], TT * (l + 1))
                hold(3)
                pool.tensor_scalar(rstd[:], mv[:, :, 1], 1e-5, None, ALU.add).then_inc(s["var_eps"], 1)
                pool.wait_ge(s["var_eps"], l + 1)
                pool.tensor_tensor(rstd[:], rstd[:], neghalf[:, 0:TT], ALU.pow).then_inc(s["rstd_rdy"], 1)

            def norms(b, n):
                pool.wait_ge(s["ss_rdy"], cnt(b, n))
                hold(2)
                pool.tensor_scalar(rtmp[:], ss[:], 1.0 / DH, 1e-6, ALU.mult, ALU.add).then_inc(s["r_tmp"], 1)
                pool.wait_ge(s["r_tmp"], cnt(b, n))
                pool.tensor_tensor(rn[:, bass.ds(head(n), 1), :].squeeze(1), rtmp[:], neghalf[:], ALU.pow).then_inc(s["r_rdy"], 1)

            def mask(b, n):
                pool.wait_ge(s["expd"], cnt(b, n))
                hold(1 if isinstance(n, int) and n == H - 1 else 0)
                d = prob[:].rearrange("p (a c) -> p a c", a=3)[:, :, 0:P]
                pool.affine_select(out=d, in_=d, compare_op=ALU.is_ge, fill=0.0, base=0,
                                   pattern=[[0, 3], [1, P]], channel_multiplier=-1).then_inc(s["p_rdy"], 1)
                d = prob[:, OFF[3]:OFF[3] + P]
                pool.affine_select(out=d, in_=d, compare_op=ALU.is_ge, fill=0.0, base=0,
                                   pattern=[[1, P]], channel_multiplier=-1).then_inc(s["p_rdy"], 1)

            def period(b, p):
                mask(b, p)
                if isinstance(p, int) and p == 1 and has_before(b):
                    ln_rstd(ln2(b - 1))
                if isinstance(p, int) and p == PEEL and not is_last(b):
                    ln_rstd(ln1(b + 1))
                if not (is_last(b) and isinstance(p, int) and p >= H - 2):
                    norms(b, p + 2)

            ln_rstd(0)
            norms(0, 0)
            norms(0, 1)
            for p in range(SIDE):
                period(0, p)
            with pool.Fori(0, B - 1) as b:
                with pool.Fori(SIDE, PEEL) as p:
                    period(b, p)
                for p in range(PEEL, H):
                    period(b, p)
                for p in range(SIDE):
                    period(b + 1, p)
            with pool.Fori(SIDE, PEEL) as p:
                period(B - 1, p)
            for p in range(PEEL, H):
                period(B - 1, p)
            ln_rstd(ln2(B - 1))

            pool.wait_ge(s["slot_rdy"], 1)
            pool.wait_ge(s["tables"], 16 * (1 + NACC))
            for i in range(NT):
                for k in range(K):
                    pool.indirect_dma_start(tab_d, bass.IndirectOffsetOnAxis(ap=sloti[:, i * K + k:i * K + k + 1], axis=0),
                                            pair[:, i, k, :], None, bounds_check=E * C - 1, oob_is_err=False).then_inc(s["tabw"], 16)

            def gather(e):
                if e >= XR:
                    pool.wait_ge(s["tr1_ps"], e - XR + 1)
                pool.indirect_dma_start(xg[0:C, e % XR, :], None, h2_d, bass.IndirectOffsetOnAxis(ap=gidx[:, e:e + 1], axis=0),
                                        bounds_check=NTOK - 1, oob_is_err=False).then_inc(xg_in[e % XR], 16)

            pool.wait_ge(s["idx_rdy"], 4)
            pool.wait_ge(s["h2_out"], 16 * B)
            for e in range(AHEAD):
                gather(e)
            for e in range(E):
                if e + AHEAD < E:
                    gather(e + AHEAD)
                pool.wait_ge(s["orow_rdy"], e + 1)
                if e >= NACC:
                    pool.wait_ge(ys[e % NACC], 16 * (e // NACC))
                pool.indirect_dma_start(acc_d[e % NACC], bass.IndirectOffsetOnAxis(ap=sidx[0:C - 1, e:e + 1], axis=0),
                                        orow[0:C - 1, e % RING, :], None, bounds_check=NTOK - 1, oob_is_err=False,
                                        compute_op=ALU.add).then_inc(ys[e % NACC], 16)

        @block.scalar
        def _(a):
            act_ = nc.scalar.activation
            a.wait_ge(s["ld_c"], 16)
            act_(sc[:], cts[:], ACT.Silu).then_inc(s["silu_c"], 1)
            a.wait_ge(s["silu_c"], 1)
            a.wait_ge(s["modt_ps"], 1)
            act_(modt[:].rearrange("p j b -> p (j b)"), ps[:, 0, 0:4 * B], ACT.Tanh).then_inc(s["modt_sb"], 1)
            a.wait_ge(s["modt_sb"], 1)
            act_(modt[:].rearrange("p j b -> p (j b)"), ps[:, 0, 0:4 * B], ACT.Copy).then_inc(s["modt_sb"], 1)

            def take(b, n):
                a.wait_ge(s["qkv_rdy"], cnt(b, n))
                if some(cnt(b, n - 1)):
                    a.wait_ge(s["ss_rdy"], cnt(b, n - 1))
                act_(sq, ps[:, 0:TT, 0:2 * DH].rearrange("p i (c d) -> p i c d", c=2), ACT.Square).then_inc(s["squared"], 1)
                act_(kr, ps[:, 0:TT, DH:2 * DH], ACT.Copy).then_inc(s["k_copied"], 1)
                dst = vx[:, bass.ds(vslot(n) * TT * (DH + 1), TT * (DH + 1))].rearrange("p (i d) -> p i d", i=TT)[:, :, 0:DH]
                a.wait_ge(s["ones_rdy"], 1)
                act_(dst, ps[:, 0:TT, 2 * DH:3 * DH], ACT.Copy).then_inc(s["v_copied"], 1)

            def cap(b, n):
                for q, (j, w) in ((1, (0, 512)), (2, (1, 384)), (2, (3, 128)), (3, (2, 256))):
                    a.wait_ge(s["s_rdy"], 3 * cnt(b, n) + (q - 3))
                    act_(prob[:, OFF[j]:OFF[j] + w], sflat[:, OFF[j]:OFF[j] + w], ACT.Tanh,
                         scale=rn[:, bass.ds(head(n), 1), TT + j:TT + j + 1].squeeze(1)).then_inc(s["capped"], 1)

            def exps(b, n):
                a.wait_ge(s["capped"], 4 * cnt(b, n))
                act_(prob[:, 0:1280], prob[:, 0:1280], ACT.Exp, scale=CAP).then_inc(s["expd"], 1)

            def out_t(b, n):
                a.wait_ge(s["ot_ps"], cnt(b, n))
                act_(ot, ps[:, 7, :], ACT.Copy).then_inc(s["ot_rdy"], 1)

            def h2_static(b):
                a.wait_ge(s["xt_ps"], ln2(b) + 1)
                act_(h2s, ps[:, 0:KC, :], ACT.Copy).then_inc(s["h2s_rdy"], 1)

            def logits_out(b):
                a.wait_ge(s["logit_ps"], b + 1)
                act_(logits[:, bass.ds(b * TT, TT), :], ps[:, 0, 0:TT * E].rearrange("p (i e) -> p i e", i=TT), ACT.Copy).then_inc(s["logit_sb"], 1)

            def h2_keep(b):
                a.wait_ge(s["h2s_rdy"], b + 1)
                act_(h2t[:, :, bass.ds(b * T, T)], h2s, ACT.Copy).then_inc(s["h2t_rdy"], 1)

            def period(b, p):
                cap(b, p)
                if some(cnt(b, p - 1)):
                    out_t(b, p - 1)
                if isinstance(p, int) and p == 3 and has_before(b):
                    h2_static(b - 1)
                if isinstance(p, int) and p == 4 and has_before(b):
                    logits_out(b - 1)
                exps(b, p)
                if not (is_last(b) and isinstance(p, int) and p >= H - 2):
                    take(b, p + 2)
                if isinstance(p, int) and p == 4 and has_before(b):
                    h2_keep(b - 1)

            take(0, 0)
            take(0, 1)
            for p in range(SIDE):
                period(0, p)
            with a.Fori(0, B - 1) as b:
                with a.Fori(SIDE, PEEL) as p:
                    period(b, p)
                for p in range(PEEL, H):
                    period(b, p)
                for p in range(SIDE):
                    period(b + 1, p)
            with a.Fori(SIDE, PEEL) as p:
                period(B - 1, p)
            for p in range(PEEL, H):
                period(B - 1, p)
            out_t(B - 1, H - 1)
            h2_static(B - 1)
            logits_out(B - 1)
            h2_keep(B - 1)

            a.wait_ge(s["soft"], 2)
            act_(logits[:], logits[:], ACT.Exp).then_inc(s["rt_exp"], 1)

            with a.Fori(0, B) as b:
                for m, (m0, mw) in enumerate(MSC):
                    a.wait_ge(s["sg_ps"], b * 3 + (m + 1))
                    if m < 2:
                        a.wait_ge(s["sa_rdy"], b * 3 + max(m - 1, 0) if m else b * 3)
                    else:
                        a.wait_ge(s["sa_rdy"], b * 3 + 1)
                    act_(sg[0:mw, m % 2, :], ps[0:mw, 2 * (m % 2), :], ACT.Silu).then_inc(s["sg_act"], 1)

            def e_xgt(e, base):
                a.wait_ge(s["tr1_ps"], base + e + 1)
                act_(xgt[:, e % 2], ps[:, 0, 0:KC * C].rearrange("p (k c) -> p k c", k=KC), ACT.Copy).then_inc(s["xgt_rdy"], 1)

            def e_silu(e, base):
                a.wait_ge(s["gu_ps"], base + e + 1)
                act_(gact[:, e % 2], ps[0:C, 1 + e % 2, 0:M], ACT.Silu).then_inc(s["gact_rdy"], 1)

            def e_orow(e, base):
                a.wait_ge(s["dn_ps"], base + e + 1)
                if isinstance(base, int):
                    if e >= RING:
                        a.wait_ge(ys[e % NACC], 16 * ((e - RING) // NACC + 1))
                        a.wait_ge(o95s[e % RING], 16 * (e // RING))
                else:
                    a.wait_ge(ys[e % NACC], (base + e - RING + NACC - e % NACC) * (16 // NACC))
                    a.wait_ge(o95s[e % RING], (base + e - e % RING) * (16 // RING))
                act_(orow[:, e % RING, :], ps[0:C, 4 + e % 2, 0:D], ACT.Copy,
                     scale=wcol[:, bass.ds(base + e, 1)]).then_inc(s["orow_rdy"], 1)

            def e_period(e, base):
                if e == 0 and isinstance(base, int):
                    e_xgt(0, 0)
                if not (isinstance(base, int) and base + e + 1 >= E):
                    e_xgt(e + 1, base)
                e_silu(e, base)
                if not (isinstance(base, int) and base + e < 2):
                    e_orow(e - 2, base) if e >= 2 or isinstance(base, int) else e_orow(e - 2 + RING, base - RING)

            a.wait_ge(s["idx_rdy"], 4)
            for e in range(RING):
                e_period(e, 0)
            with a.Fori(1, E // RING - 1) as r:
                for e in range(RING):
                    e_period(e, r * RING)
            for e in range(E - RING, E):
                e_period(e, 0)
            e_orow(E - 2, 0)
            e_orow(E - 1, 0)

        @block.vector
        def _(v):
            tt, ts, cp = nc.vector.tensor_tensor, nc.vector.tensor_scalar, nc.vector.tensor_copy

            def hold(c):
                nc.vector.memset(holdv[:, c:c + 1], 0.0)

            def ln_stats(l, b):
                for i in range(TT):
                    nc.vector.bn_stats(bst[:, i, :], xs[:, bass.ds(b * TT + i, 1), :].squeeze(1)).then_inc(s["stats"], 1)
                v.wait_ge(s["stats"], TT * (l + 1))
                hold(1)
                for i in range(TT):
                    nc.vector.bn_aggr(mv[:, i, :], bst[:, i, :]).then_inc(s["aggr"], 1)

            def ln_norm(l, b):
                v.wait_ge(s["aggr"], TT * (l + 1))
                v.wait_ge(s["rstd_rdy"], l + 1)
                for i in range(TT):
                    ts(xn[:, i, :], xs[:, bass.ds(b * TT + i, 1), :].squeeze(1), mv[:, i, 0:1], rstd[:, i:i + 1],
                       ALU.subtract, ALU.mult).then_inc(s["xn_rdy"], 1)

            def ht_modulated(b):
                v.wait_ge(s["xt_ps"], ln1(b) + 1)
                for k in range(KC):
                    ts(ht[:, k, :], ps[:, k, :], modt[:, 2 + k, bass.ds(b, 1)], modt[:, k, bass.ds(b, 1)], ALU.mult, ALU.add).then_inc(s["ht_rdy"], 1)

            def x_attended(b):
                v.wait_ge(s["y_added"], cnt(b, H - 1))
                tt(yacc, yacc, rows[:, bass.ds(b, 1), 0:1, :].squeeze(1).to_broadcast([P, TT, D]), ALU.mult).then_inc(s["x2_rdy"], 1)
                v.wait_ge(s["x2_rdy"], 2 * b + 1)
                xb = xs[:, bass.ds(b * TT, TT), :]
                tt(xb, xb, yacc, ALU.add).then_inc(s["x2_rdy"], 1)
                v.wait_ge(s["x2_rdy"], 2 * b + 2)
                hold(0)

            def h2_modulated(b):
                v.wait_ge(s["xn_rdy"], TT * (ln2(b) + 1))
                tt(xn[:], xn[:], rows[:, bass.ds(b, 1), 2:3, :].squeeze(1).to_broadcast([P, TT, D]), ALU.mult).then_inc(s["hmod"], 1)
                v.wait_ge(s["hmod"], 2 * b + 1)
                tt(xn[:], xn[:], rows[:, bass.ds(b, 1), 1:2, :].squeeze(1).to_broadcast([P, TT, D]), ALU.add).then_inc(s["hmod"], 1)

            v.wait_ge(s["silu_c"], 1)
            for k in range(KC):
                cp(scb[:, k], sc[:, k].unsqueeze(2).to_broadcast([P, B, P])).then_inc(s["scb_rdy"], 1)
            v.wait_ge(s["ld_small"], 32)
            tt(css[:].rearrange("p a h -> p (a h)"), css[:].rearrange("p a h -> p (a h)"), css[:].rearrange("p a h -> p (a h)"), ALU.mult).then_inc(s["g_rdy"], 1)
            tt(qkws[:, 0:1], qkws[:, 0:1], qkws[:, 1:2], ALU.mult).then_inc(s["g_rdy"], 1)
            v.wait_ge(s["g_rdy"], 2)
            tt(g[:], css[:, 0, :], css[:, 1, :], ALU.add).then_inc(s["g_rdy"], 1)
            v.wait_ge(s["g_rdy"], 3)
            ts(g[:], g[:], qkws[:, 0:1], DH ** -0.5 / CAP, ALU.mult, ALU.mult).then_inc(s["g_rdy"], 1)
            v.wait_ge(s["modt_sb"], 2)
            ts(modt[:, 2:4, :], modt[:, 2:4, :], 1.0, None, ALU.add).then_inc(s["modt_sb"], 1)
            for b in range(B):
                v.wait_ge(s["rows_ps"], b + 1)
                bk = (2 * b + 2) % 8
                cp(rows[:, b], ps[:, bk:bk + 2, :].rearrange("p a (u d) -> p (a u) d", d=D)).then_inc(s["rows_sb"], 1)
            v.wait_ge(s["rows_sb"], B)
            for n, c in enumerate((0, 3)):
                gate_rows = rows[:, :, c, :]
                ts(tmpg[:, 0, n], gate_rows, 0.0, 2.0, ALU.is_ge, ALU.mult).then_inc(s["clamp"], 1)
                nc.vector.scalar_tensor_tensor(out=tmpg[:, 1, n], in0=gate_rows, scalar=-1.0, in1=gate_rows, op0=ALU.mult, op1=ALU.max).then_inc(s["clamp"], 1)
            v.wait_ge(s["clamp"], 4)
            ts(tmpg[:, 1], tmpg[:, 1], 0.25, None, ALU.max).then_inc(s["clamp"], 1)
            ts(rows[:, :, 2, :], rows[:, :, 2, :], 1.0, None, ALU.add).then_inc(s["clamp"], 1)
            v.wait_ge(s["clamp"], 6)
            for n, c in enumerate((0, 3)):
                nc.vector.scalar_tensor_tensor(out=rows[:, :, c, :], in0=tmpg[:, 0, n], scalar=-1.0, in1=tmpg[:, 1, n], op0=ALU.add, op1=ALU.mult).then_inc(s["clamp"], 1)
            v.wait_ge(s["clamp"], 8)
            v.wait_ge(s["g_rdy"], 4)
            v.wait_ge(s["modt_sb"], 3)
            v.wait_ge(s["ld_x"], 16)

            def squares_sum(b, n):
                v.wait_ge(s["squared"], cnt(b, n))
                if some(cnt(b, n - 1)):
                    v.wait_ge(s["r_rdy"], cnt(b, n - 1))
                nc.vector.tensor_reduce(ss[:].rearrange("p (c i) -> p i c", c=2), sq, X, ALU.add).then_inc(s["ss_rdy"], 1)

            def q_scale(b, n):
                v.wait_ge(s["r_rdy"], cnt(b, n))
                v.wait_ge(s["v_copied"], cnt(b, n))
                tt(qn, ps[:, 0:TT, 0:DH], rn[:, bass.ds(head(n), 1), 0:TT].squeeze(1).unsqueeze(2).to_broadcast([P, TT, DH]), ALU.mult).then_inc(s["q_scaled"], 1)

            def qk_t(b, n):
                v.wait_ge(s["qt_ps"], cnt(b, n))
                cp(qt[:], ps[:, 2, :]).then_inc(s["qt_rdy"], 1)
                v.wait_ge(s["kt_ps"], cnt(b, n))
                ts(kt[:], ps[:, 3, :], g[:, bass.ds(head(n), 1)], None, ALU.mult).then_inc(s["kt_rdy"], 1)

            def y_add(b, n):
                v.wait_ge(s["y_rdy"], cnt(b, n))
                if isinstance(n, int) and n == 0:
                    cp(yacc, yps).then_inc(s["y_added"], 1)
                    return
                v.wait_ge(s["y_added"], cnt(b, n - 1))
                tt(yacc, yps, yacc, ALU.add).then_inc(s["y_added"], 1)

            def o_norm(b, n):
                v.wait_ge(s["o_rdy"], cnt(b, n))
                o3 = ps[:, 7, 0:3 * (DH + 1)].rearrange("p (i d) -> p i d", i=3)
                nc.vector.reciprocal(rden[:, 0:3], o3[:, :, DH]).then_inc(s["den_rdy"], 1)
                nc.vector.reciprocal(rden[:, 3:4], ps[:, 6, 256 + DH:257 + DH]).then_inc(s["den_rdy"], 1)
                v.wait_ge(s["den_rdy"], 2 * cnt(b, n))
                tt(on[:, 0:3, :], o3[:, :, 0:DH], rden[:, 0:3].unsqueeze(2).to_broadcast([P, 3, DH]), ALU.mult).then_inc(s["o_normed"], 1)
                ts(on[:, 3, :], ps[:, 6, 256:256 + DH], rden[:, 3:4], None, ALU.mult).then_inc(s["o_normed"], 1)

            def period(b, p):
                if not (is_last(b) and isinstance(p, int) and p == H - 1):
                    qk_t(b, p + 1)
                if isinstance(p, int) and has_before(b):
                    if p == 1:
                        x_attended(b - 1)
                        ln_stats(ln2(b - 1), b - 1)
                    if p == 2:
                        ln_norm(ln2(b - 1), b - 1)
                        h2_modulated(b - 1)
                    if p == 4:
                        v.wait_ge(s["h2_out"], 16 * b)
                        v.wait_ge(s["h2s_rdy"], b)
                if isinstance(p, int) and not is_last(b):
                    if p == PEEL:
                        ln_stats(ln1(b + 1), b + 1)
                    if p == PEEL + 1:
                        ln_norm(ln1(b + 1), b + 1)
                    if p == H - 2:
                        ht_modulated(b + 1)
                if not (is_last(b) and isinstance(p, int) and p >= H - 2):
                    squares_sum(b, p + 2)
                if some(cnt(b, p - 1)):
                    y_add(b, p - 1)
                o_norm(b, p)
                if not (is_last(b) and isinstance(p, int) and p >= H - 2):
                    q_scale(b, p + 2)

            ln_stats(0, 0)
            ln_norm(0, 0)
            ht_modulated(0)
            squares_sum(0, 0)
            q_scale(0, 0)
            qk_t(0, 0)
            squares_sum(0, 1)
            q_scale(0, 1)
            for p in range(SIDE):
                period(0, p)
            with v.Fori(0, B - 1) as b:
                with v.Fori(SIDE, PEEL) as p:
                    period(b, p)
                for p in range(PEEL, H):
                    period(b, p)
                for p in range(SIDE):
                    period(b + 1, p)
            with v.Fori(SIDE, PEEL) as p:
                period(B - 1, p)
            for p in range(PEEL, H):
                period(B - 1, p)
            y_add(B - 1, H - 1)
            x_attended(B - 1)
            ln_stats(ln2(B - 1), B - 1)
            ln_norm(ln2(B - 1), B - 1)
            h2_modulated(B - 1)

            rt = [0]

            def step(ins):
                rt[0] += 1
                ins.then_inc(s["rt"], 1)
                v.wait_ge(s["rt"], rt[0])

            def e3(ap, n):
                return ap.unsqueeze(2).to_broadcast([P, NT, n])

            v.wait_ge(s["logit_sb"], B)
            v.wait_ge(s["consts"], 10)
            step(nc.vector.tensor_reduce(mx, logits[:], X, ALU.max))
            tt(logits[:], logits[:], e3(mx, E), ALU.subtract).then_inc(s["soft"], 2)
            v.wait_ge(s["rt_exp"], 1)
            step(nc.vector.tensor_reduce(rs, logits[:], X, ALU.add))
            step(nc.vector.reciprocal(rs, rs))
            step(tt(logits[:], logits[:], e3(rs, E), ALU.mult))
            step(nc.vector.tensor_reduce(gsc.rearrange("p i n -> p (i n)"), logits[:].rearrange("p i (n c) -> p (i n) c", n=NG), X, ALU.max))
            for i in range(NT):
                ins = nc.vector.max(g8[:, i, :], gsc[:, i, :])
                if i < NT - 1:
                    ins.then_inc(s["rt"], 1)
                    rt[0] += 1
            step(ins)
            for i in range(NT):
                ins = nc.vector.max_index(gi[:, i, :], g8[:, i, :], gsc[:, i, :])
                if i < NT - 1:
                    ins.then_inc(s["rt"], 1)
                    rt[0] += 1
            step(ins)
            step(cp(gif, gi))
            i8b = iota8[:].unsqueeze(1).to_broadcast([P, NT, NG])
            step(tt(gm, i8b, e3(gif[:, :, 0], NG), ALU.is_equal))
            for k in range(1, TG):
                step(tt(gm2, i8b, e3(gif[:, :, k], NG), ALU.is_equal))
                step(tt(gm, gm, gm2, ALU.add))
            step(tt(tmp.rearrange("p i (n c) -> p (i n) c", n=NG), logits[:].rearrange("p i (n c) -> p (i n) c", n=NG),
                    gm.rearrange("p i n -> p (i n)").unsqueeze(2).to_broadcast([P, NT * NG, GS]), ALU.mult))
            for i in range(NT):
                ins = nc.vector.max(w8[:, i, :], tmp[:, i, :])
                if i < NT - 1:
                    ins.then_inc(s["rt"], 1)
                    rt[0] += 1
            step(ins)
            for i in range(NT):
                ins = nc.vector.max_index(ei[:, i, :], w8[:, i, :], tmp[:, i, :])
                if i < NT - 1:
                    ins.then_inc(s["rt"], 1)
                    rt[0] += 1
            step(ins)
            step(cp(eif, ei))
            for k in range(K):
                step(tt(oh[:, :, k, :], iotae[:].unsqueeze(1).to_broadcast([P, NT, E]), e3(eif[:, :, k], E), ALU.is_equal))
            step(nc.vector.tensor_reduce(sel, oh.rearrange("p i k e -> p i e k"), X, ALU.add))
            step(nc.vector.memset(cum[:, 0, :], 0.0))
            for i in range(NT):
                step(tt(cum[:, i + 1, :], cum[:, i, :], sel[:, i, :], ALU.add))
            v.sem_inc(s["sel_rdy"], 1)
            v.wait_ge(s["pos_rdy"], 1)
            posv = ps[:, 6:8, :].rearrange("p a (i e) -> p (a i) e", e=E)
            step(ts(over, posv, float(C - 1), None, ALU.is_ge))
            step(tt(cum[:, 0:NT, :], posv, iota96[:].unsqueeze(1).to_broadcast([P, NT, E]), ALU.add))
            step(nc.vector.scalar_tensor_tensor(out=cum[:, 0:NT, :], in0=over, scalar=SKIP, in1=cum[:, 0:NT, :], op0=ALU.mult, op1=ALU.add))
            for k in range(K):
                step(tt(oh[:, :, k, :], oh[:, :, k, :], cum[:, 0:NT, :], ALU.mult))
            step(nc.vector.tensor_reduce(slotf, oh, X, ALU.add))
            step(cp(sloti, slotf.rearrange("p i k -> p (i k)")))
            step(cp(pair[:, :, :, 0], iotat[:].unsqueeze(2).to_broadcast([P, NT, K])))
            step(cp(pair[:, :, :, 1], w8[:, :, 0:K]))
            v.sem_inc(s["slot_rdy"], 1)
            step(tt(over, over, sel, ALU.mult))
            step(tt(over, over, tmp, ALU.mult))
            v.sem_inc(s["w95_rdy"], 1)
            step(ts(iotat[:], iotat[:], 1.0, None, ALU.add))
            step(tt(sel, sel, e3(iotat[:], E), ALU.mult))
            step(nc.vector.tensor_reduce(lastp, sel.rearrange("p i e -> p e i"), X, ALU.max))
            v.sem_inc(s["lastp_rdy"], 1)
            v.wait_ge(s["lastt_ps"], 1)
            step(nc.vector.tensor_reduce(lastr[:, 0:1], ps[0:E, 6, 0:P], X, ALU.max))
            step(ts(lastr[:, 0:1], lastr[:, 0:1], -1.0, 0.0, ALU.add, ALU.max))
            step(nc.vector.memset(lastr[:, 1:2], 1.0))
            v.sem_inc(s["lastp_rdy"], 2)
            for q in range(4):
                v.wait_ge(s["w95_ps"], q + 1)
                cp(w95t[:, q * T:(q + 1) * T], ps[0:E, 6 + q % 2, :]).then_inc(s["w95_sb"], 1)

            with v.Fori(0, B) as b:
                for m, (m0, mw) in enumerate(MSC):
                    v.wait_ge(s["sg_act"], b * 3 + (m + 1))
                    if m == 0:
                        v.wait_ge(s["sdn_ps"], 2 * b)
                    tt(acts[0:mw, m, :], ps[0:mw, 2 * (m % 2) + 1, :], sg[0:mw, m % 2, :], ALU.mult).then_inc(s["sa_rdy"], 1)
                for q in range(2):
                    v.wait_ge(s["sdn_ps"], 2 * b + (q + 1))
                    cp(shr[:, bass.ds(b * TT + 2 * q, 2), :], ps[:, 4 + q, :].rearrange("p (i d) -> p i d", i=2)).then_inc(s["shr_rdy"], 1)

            v.wait_ge(s["tabt"], 1)
            cp(idf, ps[0:C, 6, 0:E]).then_inc(s["tabt_sb"], 1)
            cp(wcol, ps[0:C, 6, E:2 * E]).then_inc(s["idx_rdy"], 1)
            v.wait_ge(s["tabt_sb"], 1)
            cp(sidx, idf).then_inc(s["idx_rdy"], 1)
            v.wait_ge(s["idx_rdy"], 2)
            ts(idf, idf, float(NTOK - 1), None, ALU.min).then_inc(s["idx_rdy"], 1)
            v.wait_ge(s["idx_rdy"], 3)
            cp(gidx, idf).then_inc(s["idx_rdy"], 1)

            def e_mul(e, base):
                v.wait_ge(s["gact_rdy"], base + e + 1)
                v.wait_ge(s["gu_ps"], base + e + 1)
                tt(act[:, e % 2], ps[0:C, 1 + e % 2, M:2 * M], gact[:, e % 2], ALU.mult).then_inc(s["act_rdy"], 1)

            def e_act_t(e, base):
                v.wait_ge(s["tr2_ps"], base + e + 1)
                cp(actt[:, e % 2], ps[0:MC, 3, 0:2 * C].rearrange("p (m c) -> p m c", m=2)).then_inc(s["actt_rdy"], 1)

            def e_period(e, base):
                e_mul(e, base)
                if not (isinstance(base, int) and base + e < 1):
                    e_act_t(e - 1, base)

            for e in range(2):
                e_period(e, 0)
            with v.Fori(0, (E - 2) // 2) as r:
                e_period(2, r * 2)
                e_period(3, r * 2)
            e_act_t(E - 1, 0)

            v.wait_ge(s["acc_ld"], 16 * NACC)
            v.wait_ge(s["shr_rdy"], 2 * B)
            for b in range(B):
                sl = slice(b * TT, (b + 1) * TT)
                tt(accs[0][:, sl], accs[0][:, sl], accs[1][:, sl], ALU.add).then_inc(s["cmb2"], 1)
                v.wait_ge(s["cmb2"], 5 * b + 1)
                tt(accs[0][:, sl], accs[0][:, sl], shr[:, sl], ALU.add).then_inc(s["cmb2"], 1)
                v.wait_ge(s["cmb2"], 5 * b + 2)
                v.wait_ge(s["cmb_ps"], b + 1)
                tt(accs[0][:, sl], ps[:, 2 * b:2 * b + 2, :].rearrange("p a (u d) -> p (a u) d", d=D), accs[0][:, sl], ALU.add).then_inc(s["cmb2"], 1)
                v.wait_ge(s["cmb2"], 5 * b + 3)
                tt(accs[0][:, sl], accs[0][:, sl], rows[:, b, 3:4, :].to_broadcast([P, TT, D]), ALU.mult).then_inc(s["cmb2"], 1)
                v.wait_ge(s["cmb2"], 5 * b + 4)
                tt(xs[:, sl], xs[:, sl], accs[0][:, sl], ALU.add).then_inc(s["cmb"], 4)
                v.sem_inc(s["cmb2"], 1)

        @block.tensor
        def _(pe):
            mm = pe.matmul
            pe.wait_ge(s["ld_wmod"], 16)
            pe.wait_ge(s["silu_c"], 1)
            for j in range(4):
                for k in range(KC):
                    last = mm(ps[:, 0, j * B:(j + 1) * B], wmods[:, k, j * P:(j + 1) * P], sc[:, k, :], start=(k == 0), stop=(k == KC - 1))
            last.then_inc(s["modt_ps"], 1)
            pe.wait_ge(s["scb_rdy"], KC)
            for b in range(B):
                if b == B - 1:
                    pe.wait_ge(s["modt_sb"], 2)
                for h in range(2):
                    for k in range(KC):
                        last = mm(ps[:, (2 * b + 2 + h) % 8, :], scb[:, k, b, :], wmods[:, k, 2 * D + h * T:2 * D + (h + 1) * T],
                                  start=(k == 0), stop=(k == KC - 1))
                last.then_inc(s["rows_ps"], 1)

            def xn_t():
                for k in range(KC):
                    for i in range(TT):
                        last = pe.transpose(ps[:, k, i * P:(i + 1) * P], xn[:, i, k * P:(k + 1) * P], ident[:])
                last.then_inc(s["xt_ps"], 1)

            def qkv(b, n):
                before = cnt(b, n - 1)
                if some(before):
                    pe.wait_ge(s["v_copied"], before)
                    pe.wait_ge(s["q_scaled"], before)
                if isinstance(n, int) and n % H == 0:
                    pe.wait_ge(s["ht_rdy"], KC * (b + n // H + 1))
                for i in range(TT):
                    if i == 2 and some(before):
                        pe.wait_ge(s["qt_rdy"], before)
                    if i == 3 and some(before):
                        pe.wait_ge(s["kt_rdy"], before)
                    for k in range(KC):
                        last = mm(ps[:, i, 0:3 * DH], ht[:, k, i * P:(i + 1) * P], wq[:, k, bass.ds(head(n), 1), :].squeeze(1),
                                  start=(k == 0), stop=(k == KC - 1))
                last.then_inc(s["qkv_rdy"], 1)

            def qk_t(b, n):
                pe.wait_ge(s["q_scaled"], cnt(b, n))
                pe.wait_ge(s["v_copied"], cnt(b, n))
                for i in range(TT):
                    last = pe.transpose(ps[:, 2, i * P:(i + 1) * P], qn[:, i, :], ident[:])
                last.then_inc(s["qt_ps"], 1)
                for i in range(TT):
                    last = pe.transpose(ps[:, 3, i * P:(i + 1) * P], kr[:, i, :], ident[:])
                last.then_inc(s["kt_ps"], 1)

            def scores(b, n):
                pe.wait_ge(s["qt_rdy"], cnt(b, n))
                pe.wait_ge(s["kt_rdy"], cnt(b, n))
                if some(cnt(b, n - 2)):
                    pe.wait_ge(s["y_added"], cnt(b, n - 2))
                for j, w in ((0, 512), (1, 384), (3, 128), (2, 256)):
                    if j == 2 and some(cnt(b, n - 1)):
                        pe.wait_ge(s["o_normed"], 2 * cnt(b, n - 1))
                    last = mm(sflat[:, OFF[j]:OFF[j] + w], kt[:, j * P:(j + 1) * P], qt[:, T - w:T], start=True, stop=True)
                    if j != 1:
                        last.then_inc(s["s_rdy"], 1)

            def o_t(b, n):
                pe.wait_ge(s["o_normed"], 2 * cnt(b, n))
                for i in range(TT):
                    last = pe.transpose(ps[:, 7, i * P:(i + 1) * P], on[:, i, :], ident[:])
                last.then_inc(s["ot_ps"], 1)

            def proj(b, n):
                pe.wait_ge(s["ot_rdy"], cnt(b, n))
                for i in range(TT):
                    last = mm(yps[:, i, :], ot[:, i * P:(i + 1) * P], wos[:, bass.ds(head(n), 1), :].squeeze(1), start=True, stop=True)
                last.then_inc(s["y_rdy"], 1)

            def pv(b, n):
                pe.wait_ge(s["p_rdy"], 2 * cnt(b, n))
                if some(cnt(b, n - 1)):
                    pe.wait_ge(s["ot_rdy"], cnt(b, n - 1))
                for i in range(TT):
                    o = ps[:, 7, i * (DH + 1):(i + 1) * (DH + 1)] if i < 3 else ps[:, 6, 256:257 + DH]
                    for j in range(i + 1):
                        c = OFF[j] + (i - j) * P
                        last = mm(o, prob[:, c:c + P], vx[:, bass.ds((vslot(n) * TT + j) * (DH + 1), DH + 1)],
                                  start=(j == 0), stop=(j == i))
                last.then_inc(s["o_rdy"], 1)

            pe.wait_ge(s["consts"], 4)
            pe.wait_ge(s["rows_sb"], B)
            pe.wait_ge(s["ld_wqkv"], 16)
            pe.wait_ge(s["ld_wo"], 16)
            pe.wait_ge(s["ld_gate"], 16)
            def h1_t(b):
                pe.wait_ge(s["xn_rdy"], TT * (ln1(b) + 1))
                xn_t()

            def h2_t(b):
                pe.wait_ge(s["hmod"], 2 * b + 2)
                xn_t()

            def router(b):
                pe.wait_ge(s["h2s_rdy"], b + 1)
                for i in range(TT):
                    for k in range(KC):
                        last = mm(ps[:, 0, i * E:(i + 1) * E], h2s[:, k, i * P:(i + 1) * P], gates[:, k, :], start=(k == 0), stop=(k == KC - 1))
                last.then_inc(s["logit_ps"], 1)

            def period(b, p):
                static = isinstance(p, int)
                scores(b, p)
                if some(cnt(b, p - 1)):
                    o_t(b, p - 1)
                if not (is_last(b) and static and p == H - 1):
                    qk_t(b, p + 1)
                side = True
                if static and p == 3 and has_before(b):
                    h2_t(b - 1)
                elif static and p == 4 and has_before(b):
                    router(b - 1)
                elif static and p == H - 2 and not is_last(b):
                    h1_t(b + 1)
                else:
                    side = False
                if side:
                    pe.wait_ge(s["capped"], 4 * cnt(b, p))
                    proj(b, p - 1)
                if not (is_last(b) and static and p >= H - 2):
                    if static and p == 3 and has_before(b):
                        pe.wait_ge(s["h2s_rdy"], b)
                    if static and p == 4 and has_before(b):
                        pe.wait_ge(s["logit_sb"], b)
                    qkv(b, p + 2)
                if not side and some(cnt(b, p - 1)):
                    pe.wait_ge(s["capped"], 4 * cnt(b, p))
                    proj(b, p - 1)
                pv(b, p)

            h1_t(0)
            qkv(0, 0)
            qk_t(0, 0)
            qkv(0, 1)
            for p in range(SIDE):
                period(0, p)
            with pe.Fori(0, B - 1) as b:
                with pe.Fori(SIDE, PEEL) as p:
                    period(b, p)
                for p in range(PEEL, H):
                    period(b, p)
                for p in range(SIDE):
                    period(b + 1, p)
            with pe.Fori(SIDE, PEEL) as p:
                period(B - 1, p)
            for p in range(PEEL, H):
                period(B - 1, p)
            o_t(B - 1, H - 1)
            pe.wait_ge(s["y_added"], cnt(B - 1, H - 2))
            proj(B - 1, H - 1)
            h2_t(B - 1)
            router(B - 1)

            pe.wait_ge(s["logit_sb"], B)
            pe.wait_ge(s["sel_rdy"], 1)
            for q in range(2):
                n = NT // 2
                mm(ps[:, 6 + q, :], tri[:], sel[:, q * n:(q + 1) * n, :].rearrange("p i e -> p (i e)"), start=True, stop=False)
                last = mm(ps[:, 6 + q, :], ones[:], cum[:, q * n:(q + 1) * n, :].rearrange("p i e -> p (i e)"), start=False, stop=True)
            last.then_inc(s["pos_rdy"], 1)
            pe.wait_ge(s["lastp_rdy"], 1)
            pe.transpose(ps[0:E, 6, 0:P], lastp, ident[:]).then_inc(s["lastt_ps"], 1)
            pe.wait_ge(s["lastp_rdy"], 3)
            for q in range(4):
                if q >= 2:
                    pe.wait_ge(s["w95_sb"], q - 1)
                for i in range(TT):
                    last = pe.transpose(ps[0:E, 6 + q % 2, i * P:(i + 1) * P], over[:, q * TT + i, :], ident[:])
                last.then_inc(s["w95_ps"], 1)

            pe.wait_ge(s["ld_sh"], 48)
            with pe.Fori(0, B) as b:
                for m, (m0, mw) in enumerate(MSC):
                    pe.wait_ge(s["sa_rdy"], b * 3 + (m - 1) if m else b * 3)
                    for u in range(2):
                        for k in range(KC):
                            last = mm(ps[0:mw, 2 * (m % 2) + u, :], sgus[:, k, u, m0:m0 + mw], h2t[:, k, bass.ds(b * T, T)],
                                      start=(k == 0), stop=(k == KC - 1))
                    last.then_inc(s["sg_ps"], 1)
                pe.wait_ge(s["sa_rdy"], b * 3 + 3)
                for q in range(2):
                    pe.wait_ge(s["shr_rdy"], 2 * b)
                    for i in range(2 * q, 2 * q + 2):
                        for m, (m0, mw) in enumerate(MSC):
                            last = mm(ps[:, 4 + q, (i % 2) * D:(i % 2 + 1) * D], acts[0:mw, m, i * P:(i + 1) * P], sds[0:mw, m, :],
                                      start=(m == 0), stop=(m == 2))
                    last.then_inc(s["sdn_ps"], 1)

            pe.wait_ge(s["tabl"], 16)
            pe.wait_ge(s["w95_sb"], 4)
            pe.wait_ge(s["shr_rdy"], 2 * B)
            for c in range(2):
                last = pe.transpose(ps[0:C, 6, c * E:(c + 1) * E], tabs[:, :, c], ident[0:E, 0:E])
            last.then_inc(s["tabt"], 1)

            def tr1(e, base, use):
                pe.wait_ge(xg_in[e % XR], 16 * use)
                pe.wait_ge(s["xgt_rdy"], base + e)
                for k in range(KC):
                    last = pe.transpose(ps[:, 0, k * C:(k + 1) * C], xg[0:C, e % XR, k * P:(k + 1) * P], ident[0:C, 0:C])
                last.then_inc(s["tr1_ps"], 1)

            def gu(e, base, use):
                pe.wait_ge(s["xgt_rdy"], base + e + 1)
                pe.wait_ge(w_in[e % RING], 32 * use)
                for k in range(KC):
                    last = mm(ps[0:C, 1 + e % 2, 0:2 * M], xgt[:, e % 2, k, :], wgus[:, e % RING, k, :], start=(k == 0), stop=(k == KC - 1))
                last.then_inc(s["gu_ps"], 1)

            def tr2(e, base):
                pe.wait_ge(s["act_rdy"], base + e + 1)
                pe.wait_ge(s["actt_rdy"], base + e)
                for m in range(2):
                    last = pe.transpose(ps[0:MC, 3, m * C:(m + 1) * C], act[:, e % 2, m * MC:(m + 1) * MC], ident[0:C, 0:C])
                last.then_inc(s["tr2_ps"], 1)

            def down(e, base):
                pe.wait_ge(s["actt_rdy"], base + e + 1)
                if not (isinstance(base, int) and base + e < 2):
                    pe.wait_ge(s["orow_rdy"], base + e - 1)
                for m in range(2):
                    last = mm(ps[0:C, 4 + e % 2, 0:D], actt[:, e % 2, m, :], wds[:, e % RING, m, :], start=(m == 0), stop=(m == 1))
                last.then_inc(s["dn_ps"], 1)

            def period(e, base, r):
                static = isinstance(base, int)
                if not (static and base + e + 1 >= E):
                    tr1(e + 1, base, r + 1 if e + 1 < XR else r + 2)
                gu(e, base, (XR // RING) * r + (e // RING + 1))
                if not (static and base + e < 1):
                    tr2(e + XR - 1, base - XR) if e < 1 else tr2(e - 1, base)
                if not (static and base + e < 2):
                    down(e + XR - 2, base - XR) if e < 2 else down(e - 2, base)

            pe.wait_ge(s["idx_rdy"], 4)
            tr1(0, 0, 1)
            for e in range(XR):
                period(e, 0, 0)
            with pe.Fori(1, E // XR - 1) as r:
                for e in range(XR):
                    period(e, r * XR, r)
            for e in range(XR):
                period(e, E - XR, E // XR - 1)
            down(E - 2, 0)
            tr2(E - 1, 0)
            down(E - 1, 0)

            pe.wait_ge(s["o95_ld"], 16)
            pe.wait_ge(s["orow_rdy"], E)
            for b in range(B):
                for i in range(TT):
                    t = b * TT + i
                    last = mm(ps[:, 2 * b + i // 2, (i % 2) * D:(i % 2 + 1) * D], w95t[:, t * P:(t + 1) * P], o95, start=True, stop=True)
                last.then_inc(s["cmb_ps"], 1)


def kernel(**inputs):
    import numpy as np
    import concourse.bacc as bacc
    from concourse.bass_utils import run_bass_kernel_spmd as run

    def a(name):
        return np.asarray(inputs[name])

    def headw(name):
        return a(name).reshape(H, DH, D).transpose(2, 0, 1)

    c = np.ascontiguousarray
    arrays = {
        "x": a("L0_attn_x").reshape(NTOK, D),
        "wqkv": np.concatenate([headw("L0_attn_wq"), headw("L0_attn_wk"), headw("L0_attn_wv")], axis=2)
                .reshape(KC, P, H, 3 * DH).transpose(1, 0, 2, 3),
        "wo": a("L0_attn_wo").reshape(D, H, DH).transpose(2, 1, 0),
        "qkw": np.stack([a("L0_attn_q_norm_w"), a("L0_attn_k_norm_w")], axis=1),
        "cossin": np.stack([np.repeat(a("L0_attn_rope_cos")[:H].T, 2, axis=0),
                            np.repeat(a("L0_attn_rope_sin")[:H].T, 2, axis=0)], axis=1),
        "ct": a("L0_c").T.reshape(KC, P, B).transpose(1, 0, 2),
        "wmod": a("L0_wmod").reshape(KC, P, 6 * D).transpose(1, 0, 2),
        "gate": a("L0_ffn_gate_weight").T.reshape(KC, P, E).transpose(1, 0, 2),
        "sgu": np.stack([a("L0_ffn_Sg").T, a("L0_ffn_Su").T], axis=1).reshape(KC, P, 2, MS).transpose(1, 0, 2, 3),
        "sd": a("L0_ffn_Sd").T,
        "wgu": np.concatenate([a("L0_ffn_Wg"), a("L0_ffn_Wu")], axis=1).transpose(0, 2, 1)
               .reshape(E, KC, P, 2 * M).transpose(0, 2, 1, 3),
        "wd": a("L0_ffn_Wd").transpose(0, 2, 1).reshape(E, 2, MC, D).transpose(0, 2, 1, 3),
    }
    nc = bacc.Bacc("TRN2", target_bir_lowering=False, num_devices=1)
    feed, args = {}, []
    for name, v in arrays.items():
        feed[f"in_{name}"] = c(v)
        args.append(nc.dram_tensor(f"in_{name}", v.shape, F32, kind="ExternalInput").ap())
    args.append(nc.dram_tensor("out_0", (NTOK, D), F32, kind="ExternalOutput").ap())
    build(nc, *args)
    r = run(nc, [feed], core_ids=[0])
    return r.results[0]["out_0"].reshape(B, T, D)
```

```python
from contextlib import ExitStack

import concourse.bass as bass
from concourse import mybir

F32 = mybir.dt.float32
I32 = mybir.dt.int32
U32 = mybir.dt.uint32
F32R = mybir.dt.float32r
ALU = mybir.AluOpType
ACT = mybir.ActivationFunctionType
X = mybir.AxisListType.X

P = 128
B, T, D = 4, 512, 256
TT = T // P
NT = B * TT
NTOK = B * T
KC = D // P
H, DH = 16, 128
CAP = 50.0
E, M = 64, 176
MC = 88
MS = 352
K, NG, GS, TG = 6, 8, 8, 3
C = 96
MSC = [(0, 128), (128, 128), (256, 96)]
OFF = [0, 512, 1024, 896]
PW = 1536
RING = 4
XR = 8
AHEAD = 7
SIDE = 12
STEPS = 45
NACC = 2
SKIP = 8192.0
NOTOK = 4096.0


def build(nc, x, wqkv, wo, qkw, cossin, ct, wmod, gate, sgu, sd, wgu, wd, out):
    with ExitStack() as ctx:
        def sb(name, shape, dt=F32):
            return ctx.enter_context(nc.sbuf_tensor(name, shape, dt))

        def sem(name):
            return ctx.enter_context(nc.semaphore(name))

        ps = ctx.enter_context(nc.psum_tensor("ps", [P, 8, 512], F32))

        h2_d = nc.dram_tensor("h2_rows", (NTOK, D), F32, kind="Internal").ap()
        tab_d = nc.dram_tensor("slot_table", (E * C, 2), F32, kind="Internal").ap()
        h2t_d = nc.dram_tensor("h2_transposed", (B, P, KC * T), F32, kind="Internal").ap()
        acc_d = [nc.dram_tensor(f"acc{a}", (NTOK, D), F32, kind="Internal").ap() for a in range(NACC)]
        o95_d = nc.dram_tensor("last_rows", (E, D), F32, kind="Internal").ap()

        xs = sb("xs", [P, NT, D])
        rows = sb("rows", [P, B, 4, D])
        modt = sb("modt", [P, 4, B])
        w95 = sb("w95", [P, NT, E])
        ident = sb("ident", [P, P])
        neghalf = sb("neghalf", [P, 8])
        gates = sb("gates", [P, KC, E])
        wgus = sb("wgus", [P, RING, KC, 2 * M])
        wds = sb("wds", [MC, RING, 2, D])
        warena = sb("warena", [P, KC * H * 3 * DH])
        wq = warena[:].rearrange("p (k h c) -> p k h c", k=KC, h=H)
        wos = sb("wos", [P, H, D])
        arena2 = sb("arena2", [P, 8704])
        at = [0]

        def part(n):
            v = arena2[:, at[0]:at[0] + n]
            at[0] += n
            return v

        hth = sb("hth", [P, KC, T], F32R)
        htl = sb("htl", [P, KC, T], F32R)
        wh = sb("wh", [P, KC, 3 * DH], F32R)
        wl = sb("wl", [P, KC, 3 * DH], F32R)
        xn = sb("xn", [P, TT, D])
        qt = sb("qt", [P, T])
        kt = sb("kt", [P, T])
        prob = sb("prob", [P, PW])
        vx = sb("vx", [P, 4 * TT * (DH + 1)])
        sq = part(TT * 2 * DH).rearrange("p (i c d) -> p i c d", i=TT, c=2)
        qn = part(TT * DH).rearrange("p (i d) -> p i d", i=TT)
        kr = part(TT * DH).rearrange("p (i d) -> p i d", i=TT)
        on = part(TT * DH).rearrange("p (i d) -> p i d", i=TT)
        ot = part(T)
        yacc = part(TT * D).rearrange("p (i d) -> p i d", i=TT)
        wmods = part(KC * 6 * D).rearrange("p (k n) -> p k n", k=KC)
        scb = part(KC * B * P).rearrange("p (k b m) -> p k b m", k=KC, b=B)
        rat = [at[0] - KC * 6 * D - KC * B * P]

        def again(shape, dt=F32):
            n = 1
            for m in shape:
                n *= m
            v = arena2[:, rat[0]:rat[0] + n]
            rat[0] += n
            assert rat[0] <= 8704
            if dt != F32:
                v = v.bitcast(dt)
            if len(shape) == 2:
                return v.rearrange("p (a b) -> p a b", a=shape[0])
            if len(shape) == 3:
                return v.rearrange("p (a b c) -> p a b c", a=shape[0], b=shape[1])
            return v

        h2s = again([KC, T])
        oh = again([TT, K, E])
        sel = again([TT, E])
        cum = again([TT + 1, E])
        tmp = again([TT, E])
        over = again([TT, E])
        gsc = again([TT, NG])
        g8 = again([TT, 8])
        gi = again([TT, 8], U32)
        gif = again([TT, 8])
        gm = again([TT, NG])
        gm2 = again([TT, NG])
        w8 = again([TT, 8])
        ei = again([TT, 8], U32)
        eif = again([TT * K])
        slotf = again([TT * K])
        sloti = again([TT * K], I32)
        lastp = again([E])
        rmax = again([E])
        lg = again([TT, E])
        mx = again([TT])
        rs = again([TT])
        pair = again([TT, K, 2])
        ss = sb("ss", [P, 2 * TT])
        rtmp = sb("rtmp", [P, 2 * TT])
        rn = sb("rn", [P, H, 2 * TT])
        rden = sb("rden", [P, TT])
        g = sb("g", [P, H])
        qkws = sb("qkws", [P, 2])
        css = sb("css", [P, 2, H])
        cts = sb("cts", [P, KC, B])
        sc = sb("sc", [P, KC, B])
        bst = sb("bst", [P, TT, 6])
        mv = sb("mv", [P, TT, 2])
        rstd = sb("rstd", [P, TT])
        holdp = sb("holdp", [P, 5])
        holdv = sb("holdv", [P, 4])

        shr = warena[:, 0:TT * D].rearrange("p (i d) -> p i d", i=TT)
        acts = warena[:, 4096:4096 + 3 * T].rearrange("p (m t) -> p m t", m=3)
        sg = warena[:, 5632:5632 + 2 * T].rearrange("p (a t) -> p a t", a=2)
        sgus = warena[:, 6656:6656 + KC * 2 * MS].rearrange("p (k u m) -> p k u m", k=KC, u=2)
        h2t = warena[:, 8064:8064 + B * KC * T].rearrange("p (b k t) -> p b k t", b=B, k=KC)
        sds = wos[:, 8:11, :]
        w95t = arena2[0:E, XR * D:XR * D + NTOK]
        lastr = vx[0:E, 192:194]
        tabs = vx[0:E, 200:392].rearrange("p (s c) -> p s c", c=2)
        gidx = vx[0:C, 392:456].bitcast(I32)
        sidx = vx[0:C, 456:520].bitcast(I32)
        idf = vx[0:C, 520:584]
        wcol = vx[0:C, 584:648]
        o95 = vx[0:E, 648:904]
        xg = arena2[:, 0:XR * D].rearrange("p (u d) -> p u d", u=XR)
        xgt = qt[:, 0:2 * KC * C].rearrange("p (u k c) -> p u k c", u=2, k=KC)
        gact = kt[0:C, 0:2 * M].rearrange("p (u m) -> p u m", u=2)
        xnf = xn[:].rearrange("p i d -> p (i d)")
        act = xnf[0:C, 0:2 * M].rearrange("p (u m) -> p u m", u=2)
        actt = xnf[0:MC, 512:512 + 4 * C].rearrange("p (u m c) -> p u m c", u=2, m=2)
        orow = wos[0:C, 0:RING, :]
        accs = [warena[:, (a + 1) * NT * D:(a + 2) * NT * D].rearrange("p (i d) -> p i d", i=NT) for a in range(NACC)]

        tri = sb("tri", [P, P])
        ones = sb("ones", [P, P])
        iota8 = sb("iota8", [P, NG])
        iotae = sb("iotae", [P, E])
        iota96 = sb("iota96", [P, E])
        iotat = sb("iotat", [P, NT])
        iotat1 = sb("iotat1", [P, NT])
        fill = sb("fill", [E, C, 2])
        zrow = sb("zrow", [P, D])

        names = """ld_x0 ld_wq0 ld_x ld_c ld_wmod ld_small ld_wqkv ld_wo ld_gate ld_sh consts fills zeros tables
            silu_c scb_rdy modt_ps rows_ps modt_sb rows_sb clamp cb_rdy g_rdy
            wh_rdy wl_rdy h_full h_high stats aggr var_eps rstd_rdy xn_rdy hmod xt_ps ht_rdy h2t_out h2_out logit_ps logit_sb
            qkv_rdy squared k_copied v_copied ss_rdy r_tmp r_rdy q_scaled qt_ps kt_ps qt_rdy kt_rdy
            s_rdy capped expd p_rdy o_rdy den_rdy o_normed ot_ps ot_rdy y_rdy y_added h2s_rdy x2_rdy
            ones_rdy rt soft rt_exp sel_rdy pos_rdy lastp_rdy lastt_ps slot_rdy tabw tab_free last_in lastp_upd carry pos_used tabl tabr tabt tabt_sb
            last_out w95_ps w95_sb idx_rdy sg_ps sg_act sa_rdy sdn_ps shr_rdy
            tr1_ps xgt_rdy gu_ps gact_rdy act_rdy tr2_ps actt_rdy dn_ps orow_rdy
            x_shared o95_ld cmb_ps cmb cmb2 outd""".split()
        s = {n: sem(n) for n in names}
        xg_in = [sem(f"xg_in{i}") for i in range(XR)]
        w_in = [sem(f"w_in{i}") for i in range(RING)]
        ys = [sem(f"ys{a}") for a in range(NACC)]
        o95s = [sem(f"o95s{i}") for i in range(RING)]
        acc_in = [sem(f"acc_in{b}") for b in range(B)]

        block = ctx.enter_context(nc.Block())

        sflat = ps[:, 4:7, :].rearrange("p a c -> p (a c)")
        yps = ps[:, 4:6, :].rearrange("p a (u d) -> p (a u) d", d=D)

        def cnt(b, n):
            return b * H + (n + 1)

        def head(n):
            return n % H if isinstance(n, int) else n

        def some(count):
            return not (isinstance(count, int) and count <= 0)

        def has_before(b):
            return not (isinstance(b, int) and b == 0)

        def is_last(b):
            return isinstance(b, int) and b == B - 1

        def ln1(b):
            return 0 if isinstance(b, int) and b == 0 else 2 * b - 1

        def ln2(b):
            return 2 * B - 1 if is_last(b) else 2 * b + 2

        def vslot(n):
            return n % 4

        @block.sync
        def _(sp):
            sp.dma_start(cts[:], ct).then_inc(s["ld_c"], 16)
            xr, nf = x.rearrange("(i p) d -> p i d", p=P), 3
            sp.dma_start(xs[:, 0:TT, :], xr[:, 0:TT, :]).then_inc(s["ld_x0"], 16)
            sp.dma_start(wmods, wmod).then_inc(s["ld_wmod"], 16)
            sp.dma_start(wq[:, :, 0:nf, :], wqkv[:, :, 0:nf, :]).then_inc(s["ld_wq0"], 16)
            sp.dma_start(qkws[:], qkw).then_inc(s["ld_small"], 16)
            sp.dma_start(css[:], cossin).then_inc(s["ld_small"], 16)
            sp.dma_start(wq[:, :, nf:H, :], wqkv[:, :, nf:H, :]).then_inc(s["ld_wqkv"], 16)
            sp.dma_start(xs[:, TT:NT, :], xr[:, TT:NT, :]).then_inc(s["ld_x"], 16)
            sp.dma_start(wos[:], wo).then_inc(s["ld_wo"], 16)
            sp.dma_start(gates[:], gate).then_inc(s["ld_gate"], 16)
            for u in range(RING):
                sp.dma_start(wgus[:, u], wgu[u]).then_inc(w_in[u], 16)
                sp.dma_start(wds[:, u], wd[u]).then_inc(w_in[u], 16)
            sp.wait_ge(s["fills"], 2)
            sp.dma_start(tab_d.rearrange("(e s) c -> e (s c)", e=E), fill[:].rearrange("e s c -> e (s c)")).then_inc(s["tables"], 16)
            sp.wait_ge(s["zeros"], 1)
            for a in range(NACC):
                sp.dma_start(acc_d[a].rearrange("(i p) d -> p i d", p=P),
                             zrow[:].unsqueeze(1).to_broadcast([P, NT, D])).then_inc(s["tables"], 16)
            h2_rows = h2_d.rearrange("(b i p) d -> p b i d", b=B, p=P)
            sp.sem_inc(s["tab_free"], 1)
            with sp.Fori(0, B - 1) as b:
                sp.wait_ge(s["hmod"], 2 * b + 2)
                sp.dma_start(h2_rows[:, bass.ds(b, 1)].squeeze(1), xn[:]).then_inc(s["h2_out"], 16)
                sp.wait_ge(s["h2s_rdy"], b + 1)
                sp.dma_start(h2t_d[bass.ds(b, 1)].squeeze(0), h2s.rearrange("p k t -> p (k t)")).then_inc(s["h2t_out"], 16)
                sp.wait_ge(s["tabw"], 16 * TT * K * (b + 1))
                sp.sem_inc(s["tab_free"], 1)
            sp.wait_ge(s["hmod"], 2 * B)
            sp.dma_start(h2_rows[:, B - 1], xn[:]).then_inc(s["h2_out"], 16)
            sp.wait_ge(s["h2s_rdy"], B)
            sp.dma_start(h2t_d[B - 1], h2s.rearrange("p k t -> p (k t)")).then_inc(s["h2t_out"], 16)
            sp.wait_ge(s["logit_ps"], B)
            sp.wait_ge(s["h2t_out"], 16 * B)
            sp.dma_start(h2t.rearrange("p b k t -> p b (k t)"), h2t_d.rearrange("b p n -> p b n")).then_inc(s["ld_sh"], 16)
            sp.dma_start(sgus, sgu).then_inc(s["ld_sh"], 16)
            sp.dma_start(sds[:, 0:2, :], sd[0:2 * P, :].rearrange("(m p) d -> p m d", p=P)).then_inc(s["ld_sh"], 16)
            sp.dma_start(sds[0:MS - 2 * P, 2, :], sd[2 * P:MS, :]).then_inc(s["ld_sh"], 16)
            sp.wait_ge(s["lastp_rdy"], 2)
            sp.wait_ge(s["tables"], 16 * (1 + NACC))
            sp.wait_ge(s["tabw"], 16 * NT * K)
            sp.dma_start(tab_d.rearrange("(e s) c -> e s c", e=E)[:, C - 1, :], lastr).then_inc(s["last_out"], 16)
            sp.wait_ge(s["last_out"], 16)
            sp.dma_start(tabs.rearrange("e s c -> e (s c)"), tab_d.rearrange("(e s) c -> e (s c)", e=E)).then_inc(s["tabl"], 16)
            def gate_up(base, u):
                sp.wait_ge(s["gu_ps"], base + (u + 1))
                sp.dma_start(wgus[:, u], wgu[bass.ds(base + (RING + u), 1)].squeeze(0)).then_inc(w_in[u], 16)

            def last_row(base, u):
                sp.wait_ge(s["orow_rdy"], base + (u + 1))
                sp.dma_start(o95_d[bass.ds(base + u, 1)], orow[C - 1:C, u % RING, :]).then_inc(o95s[u % RING], 16)

            def down_and_row(base, u):
                sp.wait_ge(s["dn_ps"], base + (u + 1))
                sp.dma_start(wds[:, u % RING], wd[bass.ds(base + (RING + u), 1)].squeeze(0)).then_inc(w_in[u % RING], 16)
                last_row(base, u)

            for u in range(RING):
                gate_up(0, u)
                if u >= 2:
                    down_and_row(0, u - 2)
            with sp.Fori(1, E // RING - 1) as r:
                for u in range(RING):
                    gate_up(r * RING, u)
                    down_and_row(r * RING, u - 2)
            for u in (-2, -1):
                down_and_row(E - RING, u)
            for u in range(RING):
                last_row(E - RING, u)
            for u in range(RING):
                sp.wait_ge(o95s[u], 16 * (E // RING))
            sp.dma_start(o95, o95_d).then_inc(s["o95_ld"], 16)
            for a in range(NACC):
                sp.wait_ge(ys[a], 16 * (E // NACC))
            for b in range(B):
                for a in range(NACC):
                    sp.dma_start(accs[a][:, b * TT:(b + 1) * TT], acc_d[a][b * T:(b + 1) * T].rearrange("(i p) d -> p i d", p=P)).then_inc(acc_in[b], 16)
            for b in range(B):
                sp.wait_ge(s["cmb"], b + 1)
                sp.dma_start(out[b * T:(b + 1) * T].rearrange("(i p) d -> p i d", p=P), xs[:, b * TT:(b + 1) * TT, :]).then_inc(s["outd"], 16)
            sp.wait_ge(s["outd"], 16 * B)
            sp.wait_ge(s["h2_out"], 16 * B)

        @block.gpsimd
        def _(pool):
            def hold(c):
                pool.tensor_tensor(holdp[:, c:c + 1], neghalf[:, 0:1], neghalf[:, 0:1], ALU.mult)

            pool.memset(ident[:], 0.0).then_inc(s["consts"], 1)
            pool.memset(tri[:], 1.0).then_inc(s["consts"], 1)
            pool.memset(neghalf[:], -0.5).then_inc(s["consts"], 1)
            pool.wait_ge(s["consts"], 3)
            pool.affine_select(out=ident[:], in_=ident[:], compare_op=ALU.not_equal, fill=1.0, base=0,
                               pattern=[[-1, P]], channel_multiplier=1).then_inc(s["consts"], 1)
            pool.affine_select(out=tri[:], in_=tri[:], compare_op=ALU.is_gt, fill=0.0, base=0,
                               pattern=[[1, P]], channel_multiplier=-1).then_inc(s["consts"], 1)
            pool.memset(ones[:], 1.0).then_inc(s["consts"], 1)
            pool.memset(vx[:], 1.0).then_inc(s["ones_rdy"], 1)
            pool.memset(zrow[:], 0.0).then_inc(s["zeros"], 1)
            pool.memset(fill[:, :, 0:1], NOTOK).then_inc(s["fills"], 1)
            pool.memset(fill[:, :, 1:2], 0.0).then_inc(s["fills"], 1)
            pool.iota(iota8[:], pattern=[[1, NG]], base=0, channel_multiplier=0, allow_small_or_imprecise_dtypes=True).then_inc(s["consts"], 1)
            pool.iota(iotae[:], pattern=[[1, E]], base=0, channel_multiplier=0, allow_small_or_imprecise_dtypes=True).then_inc(s["consts"], 1)
            pool.iota(iota96[:], pattern=[[C, E]], base=0, channel_multiplier=0, allow_small_or_imprecise_dtypes=True).then_inc(s["consts"], 1)
            pool.iota(iotat[:], pattern=[[P, NT]], base=0, channel_multiplier=1, allow_small_or_imprecise_dtypes=True).then_inc(s["consts"], 1)
            pool.iota(iotat1[:], pattern=[[P, NT]], base=1, channel_multiplier=1, allow_small_or_imprecise_dtypes=True).then_inc(s["consts"], 1)

            def ln_rstd(l):
                pool.wait_ge(s["aggr"], TT * (l + 1))
                hold(3)
                pool.tensor_scalar(rstd[:], mv[:, :, 1], 1e-5, None, ALU.add).then_inc(s["var_eps"], 1)
                pool.wait_ge(s["var_eps"], l + 1)
                pool.tensor_tensor(rstd[:], rstd[:], neghalf[:, 0:TT], ALU.pow).then_inc(s["rstd_rdy"], 1)

            def norms(b, n):
                pool.wait_ge(s["ss_rdy"], cnt(b, n))
                hold(2)
                pool.tensor_scalar(rtmp[:], ss[:], 1.0 / DH, 1e-6, ALU.mult, ALU.add).then_inc(s["r_tmp"], 1)
                pool.wait_ge(s["r_tmp"], cnt(b, n))
                pool.tensor_tensor(rn[:, bass.ds(head(n), 1), :].squeeze(1), rtmp[:], neghalf[:], ALU.pow).then_inc(s["r_rdy"], 1)

            def mask(b, n):
                pool.wait_ge(s["expd"], cnt(b, n))
                hold(0 if not isinstance(n, int) or n % 2 else 4)
                d = prob[:].rearrange("p (a c) -> p a c", a=3)[:, :, 0:P]
                pool.affine_select(out=d, in_=d, compare_op=ALU.is_ge, fill=0.0, base=0,
                                   pattern=[[0, 3], [1, P]], channel_multiplier=-1).then_inc(s["p_rdy"], 1)
                d = prob[:, OFF[3]:OFF[3] + P]
                pool.affine_select(out=d, in_=d, compare_op=ALU.is_ge, fill=0.0, base=0,
                                   pattern=[[1, P]], channel_multiplier=-1).then_inc(s["p_rdy"], 1)

            def table(ks):
                for i, k in ks:
                    pool.indirect_dma_start(tab_d, bass.IndirectOffsetOnAxis(ap=sloti[:, i * K + k:i * K + k + 1], axis=0),
                                            pair[:, i, k, :], None, bounds_check=E * C - 1, oob_is_err=False).then_inc(s["tabw"], 16)

            ik = [(i, k) for i in range(TT) for k in range(K)]

            def period(b, p):
                static = isinstance(p, int)
                mask(b, p)
                if static and p == 1 and has_before(b):
                    ln_rstd(ln2(b - 1))
                if static and p == H - 4 and not is_last(b):
                    ln_rstd(ln1(b + 1))
                if static and 9 <= p < 12 and has_before(b):
                    if p == 9:
                        pool.wait_ge(s["slot_rdy"], b)
                        hold(1)
                    table(ik[8 * (p - 9):8 * (p - 9) + 4])
                if not (is_last(b) and static and p >= H - 2):
                    norms(b, p + 2)
                if static and 9 <= p < 12 and has_before(b):
                    table(ik[8 * (p - 9) + 4:8 * (p - 9) + 8])

            ln_rstd(0)
            norms(0, 0)
            norms(0, 1)
            pool.wait_ge(s["tables"], 16 * (1 + NACC))
            for p in range(2):
                period(0, p)
            with pool.Fori(2, SIDE) as p:
                period(0, p)
            with pool.Fori(0, B - 1) as b:
                for p in range(SIDE, H):
                    period(b, p)
                for p in range(SIDE):
                    period(b + 1, p)
            for p in range(SIDE, H):
                period(B - 1, p)
            ln_rstd(ln2(B - 1))
            pool.wait_ge(s["slot_rdy"], B)
            table(ik)

            def gather(e):
                if e >= XR:
                    pool.wait_ge(s["tr1_ps"], e - XR + 1)
                pool.indirect_dma_start(xg[0:C, e % XR, :], None, h2_d, bass.IndirectOffsetOnAxis(ap=gidx[:, e:e + 1], axis=0),
                                        bounds_check=NTOK - 1, oob_is_err=False).then_inc(xg_in[e % XR], 16)

            pool.wait_ge(s["idx_rdy"], 4)
            pool.wait_ge(s["h2_out"], 16 * B)
            for e in range(AHEAD):
                gather(e)
            for e in range(E):
                if e + AHEAD < E:
                    gather(e + AHEAD)
                pool.wait_ge(s["orow_rdy"], e + 1)
                if e >= NACC:
                    pool.wait_ge(ys[e % NACC], 16 * (e // NACC))
                pool.indirect_dma_start(acc_d[e % NACC], bass.IndirectOffsetOnAxis(ap=sidx[0:C - 1, e:e + 1], axis=0),
                                        orow[0:C - 1, e % RING, :], None, bounds_check=NTOK - 1, oob_is_err=False,
                                        compute_op=ALU.add).then_inc(ys[e % NACC], 16)

        @block.scalar
        def _(a):
            act_ = nc.scalar.activation
            a.wait_ge(s["ld_c"], 16)
            act_(sc[:], cts[:], ACT.Silu).then_inc(s["silu_c"], 1)
            a.wait_ge(s["silu_c"], 1)
            a.wait_ge(s["modt_ps"], 1)
            act_(modt[:].rearrange("p j b -> p (j b)"), ps[:, 0, 0:4 * B], ACT.Tanh).then_inc(s["modt_sb"], 1)
            a.wait_ge(s["modt_sb"], 1)
            act_(modt[:].rearrange("p j b -> p (j b)"), ps[:, 0, 0:4 * B], ACT.Copy).then_inc(s["modt_sb"], 1)

            def take(b, n):
                a.wait_ge(s["qkv_rdy"], cnt(b, n))
                if some(cnt(b, n - 1)):
                    a.wait_ge(s["ss_rdy"], cnt(b, n - 1))
                act_(sq, ps[:, 0:TT, 0:2 * DH].rearrange("p i (c d) -> p i c d", c=2), ACT.Square).then_inc(s["squared"], 1)
                act_(kr, ps[:, 0:TT, DH:2 * DH], ACT.Copy).then_inc(s["k_copied"], 1)
                dst = vx[:, bass.ds(vslot(n) * TT * (DH + 1), TT * (DH + 1))].rearrange("p (i d) -> p i d", i=TT)[:, :, 0:DH]
                a.wait_ge(s["ones_rdy"], 1)
                act_(dst, ps[:, 0:TT, 2 * DH:3 * DH], ACT.Copy).then_inc(s["v_copied"], 1)

            def weights_high(b, n):
                if some(cnt(b, n - 1)):
                    a.wait_ge(s["qkv_rdy"], cnt(b, n - 1))
                act_(wh[:], wq[:, :, bass.ds(head(n), 1), :].squeeze(2), ACT.Copy).then_inc(s["wh_rdy"], 1)

            def cap(b, n):
                for q, (j, w) in ((1, (0, 512)), (2, (1, 384)), (2, (3, 128)), (3, (2, 256))):
                    a.wait_ge(s["s_rdy"], 3 * cnt(b, n) + (q - 3))
                    act_(prob[:, OFF[j]:OFF[j] + w], sflat[:, OFF[j]:OFF[j] + w], ACT.Tanh,
                         scale=rn[:, bass.ds(head(n), 1), TT + j:TT + j + 1].squeeze(1)).then_inc(s["capped"], 1)

            def exps(b, n):
                a.wait_ge(s["capped"], 4 * cnt(b, n))
                act_(prob[:, 0:1280], prob[:, 0:1280], ACT.Exp, scale=CAP).then_inc(s["expd"], 1)

            def out_t(b, n):
                a.wait_ge(s["ot_ps"], cnt(b, n))
                act_(ot, ps[:, 7, :], ACT.Copy).then_inc(s["ot_rdy"], 1)

            def h2_static(b):
                a.wait_ge(s["xt_ps"], ln2(b) + 1)
                act_(h2s, ps[:, 0:KC, :], ACT.Copy).then_inc(s["h2s_rdy"], 1)

            def logits_out(b):
                a.wait_ge(s["logit_ps"], b + 1)
                act_(lg, ps[:, 0, 0:TT * E].rearrange("p (i e) -> p i e", i=TT), ACT.Copy).then_inc(s["logit_sb"], 1)

            def route_exp(b):
                a.wait_ge(s["soft"], b + 1)
                act_(lg, lg, ACT.Exp).then_inc(s["rt_exp"], 1)

            def period(b, p):
                static = isinstance(p, int)
                cap(b, p)
                if some(cnt(b, p - 1)):
                    out_t(b, p - 1)
                if isinstance(p, int) and p == 3 and has_before(b):
                    h2_static(b - 1)
                exps(b, p)
                if isinstance(p, int) and p == 3 and has_before(b):
                    logits_out(b - 1)
                if not (is_last(b) and isinstance(p, int) and p >= H - 2):
                    take(b, p + 2)
                    if not (is_last(b) and static and p == H - 3):
                        weights_high(b, p + 3)
                if static and p == 8 and has_before(b):
                    a.wait_ge(s["h2t_out"], 16 * b)
                if static and p == 4 and has_before(b):
                    route_exp(b - 1)

            a.wait_ge(s["ld_wq0"], 16)
            weights_high(0, 0)
            take(0, 0)
            weights_high(0, 1)
            take(0, 1)
            weights_high(0, 2)
            a.wait_ge(s["ld_wqkv"], 16)
            for p in range(2):
                period(0, p)
            with a.Fori(2, SIDE) as p:
                period(0, p)
            with a.Fori(0, B - 1) as b:
                for p in range(SIDE, H):
                    period(b, p)
                for p in range(SIDE):
                    period(b + 1, p)
            for p in range(SIDE, H):
                period(B - 1, p)
            out_t(B - 1, H - 1)
            h2_static(B - 1)
            logits_out(B - 1)
            route_exp(B - 1)

            with a.Fori(0, B) as b:
                for m, (m0, mw) in enumerate(MSC):
                    a.wait_ge(s["sg_ps"], b * 3 + (m + 1))
                    if m < 2:
                        a.wait_ge(s["sa_rdy"], b * 3 + max(m - 1, 0) if m else b * 3)
                    else:
                        a.wait_ge(s["sa_rdy"], b * 3 + 1)
                    act_(sg[0:mw, m % 2, :], ps[0:mw, 2 * (m % 2), :], ACT.Silu).then_inc(s["sg_act"], 1)

            def e_xgt(e, base):
                a.wait_ge(s["tr1_ps"], base + e + 1)
                act_(xgt[:, e % 2], ps[:, 0, 0:KC * C].rearrange("p (k c) -> p k c", k=KC), ACT.Copy).then_inc(s["xgt_rdy"], 1)

            def e_silu(e, base):
                a.wait_ge(s["gu_ps"], base + e + 1)
                act_(gact[:, e % 2], ps[0:C, 1 + e % 2, 0:M], ACT.Silu).then_inc(s["gact_rdy"], 1)

            def e_orow(e, base):
                a.wait_ge(s["dn_ps"], base + e + 1)
                if isinstance(base, int):
                    if e >= RING:
                        a.wait_ge(ys[e % NACC], 16 * ((e - RING) // NACC + 1))
                        a.wait_ge(o95s[e % RING], 16 * (e // RING))
                else:
                    a.wait_ge(ys[e % NACC], (base + e - RING + NACC - e % NACC) * (16 // NACC))
                    a.wait_ge(o95s[e % RING], (base + e - e % RING) * (16 // RING))
                act_(orow[:, e % RING, :], ps[0:C, 4 + e % 2, 0:D], ACT.Copy,
                     scale=wcol[:, bass.ds(base + e, 1)]).then_inc(s["orow_rdy"], 1)

            def e_period(e, base):
                if e == 0 and isinstance(base, int):
                    e_xgt(0, 0)
                if not (isinstance(base, int) and base + e + 1 >= E):
                    e_xgt(e + 1, base)
                e_silu(e, base)
                if not (isinstance(base, int) and base + e < 2):
                    e_orow(e - 2, base) if e >= 2 or isinstance(base, int) else e_orow(e - 2 + RING, base - RING)

            a.wait_ge(s["idx_rdy"], 4)
            for e in range(RING):
                e_period(e, 0)
            with a.Fori(1, E // RING - 1) as r:
                for e in range(RING):
                    e_period(e, r * RING)
            for e in range(E - RING, E):
                e_period(e, 0)
            e_orow(E - 2, 0)
            e_orow(E - 1, 0)

        @block.vector
        def _(v):
            tt, ts, cp = nc.vector.tensor_tensor, nc.vector.tensor_scalar, nc.vector.tensor_copy

            def hold(c):
                nc.vector.memset(holdv[:, c:c + 1], 0.0)

            def ln_stats(l, b):
                for i in range(TT):
                    nc.vector.bn_stats(bst[:, i, :], xs[:, bass.ds(b * TT + i, 1), :].squeeze(1)).then_inc(s["stats"], 1)
                v.wait_ge(s["stats"], TT * (l + 1))
                hold(1)
                for i in range(TT):
                    nc.vector.bn_aggr(mv[:, i, :], bst[:, i, :]).then_inc(s["aggr"], 1)

            def ln_norm(l, b):
                v.wait_ge(s["aggr"], TT * (l + 1))
                v.wait_ge(s["rstd_rdy"], l + 1)
                for i in range(TT):
                    ts(xn[:, i, :], xs[:, bass.ds(b * TT + i, 1), :].squeeze(1), mv[:, i, 0:1], rstd[:, i:i + 1],
                       ALU.subtract, ALU.mult).then_inc(s["xn_rdy"], 1)

            def h_modulated(b):
                v.wait_ge(s["xt_ps"], ln1(b) + 1)
                for k in range(KC):
                    ts(full[:, k, :], ps[:, k, :], modt[:, 2 + k, bass.ds(b, 1)], modt[:, k, bass.ds(b, 1)], ALU.mult, ALU.add).then_inc(s["h_full"], 1)

            full = xn[:].rearrange("p i d -> p (i d)").rearrange("p (k t) -> p k t", k=KC)

            def h_split(b):
                v.wait_ge(s["h_full"], KC * (b + 1))
                cp(hth[:], full).then_inc(s["h_high"], 1)
                v.wait_ge(s["h_high"], b + 1)
                tt(htl[:], full, hth[:].bitcast(F32), ALU.subtract).then_inc(s["ht_rdy"], KC)

            def weights_low(b, n):
                v.wait_ge(s["wh_rdy"], cnt(b, n))
                tt(wl[:], wq[:, :, bass.ds(head(n), 1), :].squeeze(2), wh[:].bitcast(F32), ALU.subtract).then_inc(s["wl_rdy"], 1)

            def x_attended(b):
                v.wait_ge(s["y_added"], cnt(b, H - 1))
                tt(yacc, yacc, rows[:, bass.ds(b, 1), 0:1, :].squeeze(1).to_broadcast([P, TT, D]), ALU.mult).then_inc(s["x2_rdy"], 1)
                v.wait_ge(s["x2_rdy"], 2 * b + 1)
                xb = xs[:, bass.ds(b * TT, TT), :]
                tt(xb, xb, yacc, ALU.add).then_inc(s["x2_rdy"], 1)
                v.wait_ge(s["x2_rdy"], 2 * b + 2)
                hold(0)

            def h2_modulated(b):
                v.wait_ge(s["xn_rdy"], TT * (ln2(b) + 1))
                tt(xn[:], xn[:], rows[:, bass.ds(b, 1), 2:3, :].squeeze(1).to_broadcast([P, TT, D]), ALU.mult).then_inc(s["hmod"], 1)
                v.wait_ge(s["hmod"], 2 * b + 1)
                tt(xn[:], xn[:], rows[:, bass.ds(b, 1), 1:2, :].squeeze(1).to_broadcast([P, TT, D]), ALU.add).then_inc(s["hmod"], 1)

            v.wait_ge(s["silu_c"], 1)
            for k in range(KC):
                cp(scb[:, k], sc[:, k].unsqueeze(2).to_broadcast([P, B, P])).then_inc(s["scb_rdy"], 1)
            def rows_out(b):
                v.wait_ge(s["rows_ps"], b + 1)
                bk = 4 + 2 * (b % 2)
                cp(rows[:, b], ps[:, bk:bk + 2, :].rearrange("p a (u d) -> p (a u) d", d=D)).then_inc(s["rows_sb"], 1)

            def squares_sum(b, n):
                v.wait_ge(s["squared"], cnt(b, n))
                if some(cnt(b, n - 1)):
                    v.wait_ge(s["r_rdy"], cnt(b, n - 1))
                nc.vector.tensor_reduce(ss[:].rearrange("p (c i) -> p i c", c=2), sq, X, ALU.add).then_inc(s["ss_rdy"], 1)

            def q_scale(b, n):
                v.wait_ge(s["r_rdy"], cnt(b, n))
                v.wait_ge(s["v_copied"], cnt(b, n))
                tt(qn, ps[:, 0:TT, 0:DH], rn[:, bass.ds(head(n), 1), 0:TT].squeeze(1).unsqueeze(2).to_broadcast([P, TT, DH]), ALU.mult).then_inc(s["q_scaled"], 1)

            def qk_t(b, n):
                v.wait_ge(s["qt_ps"], cnt(b, n))
                cp(qt[:], ps[:, 2, :]).then_inc(s["qt_rdy"], 1)
                v.wait_ge(s["kt_ps"], cnt(b, n))
                ts(kt[:], ps[:, 3, :], g[:, bass.ds(head(n), 1)], None, ALU.mult).then_inc(s["kt_rdy"], 1)

            def y_add(b, n):
                v.wait_ge(s["y_rdy"], cnt(b, n))
                if isinstance(n, int) and n == 0:
                    cp(yacc, yps).then_inc(s["y_added"], 1)
                    return
                v.wait_ge(s["y_added"], cnt(b, n - 1))
                tt(yacc, yps, yacc, ALU.add).then_inc(s["y_added"], 1)

            def o_norm(b, n):
                v.wait_ge(s["o_rdy"], cnt(b, n))
                o3 = ps[:, 7, 0:3 * (DH + 1)].rearrange("p (i d) -> p i d", i=3)
                nc.vector.reciprocal(rden[:, 0:3], o3[:, :, DH]).then_inc(s["den_rdy"], 1)
                nc.vector.reciprocal(rden[:, 3:4], ps[:, 6, 256 + DH:257 + DH]).then_inc(s["den_rdy"], 1)
                v.wait_ge(s["den_rdy"], 2 * cnt(b, n))
                tt(on[:, 0:3, :], o3[:, :, 0:DH], rden[:, 0:3].unsqueeze(2).to_broadcast([P, 3, DH]), ALU.mult).then_inc(s["o_normed"], 1)
                ts(on[:, 3, :], ps[:, 6, 256:256 + DH], rden[:, 3:4], None, ALU.mult).then_inc(s["o_normed"], 1)

            rt = [0]

            def step(b, ins, wait=True):
                rt[0] += 1
                ins.then_inc(s["rt"], 1)
                if wait:
                    v.wait_ge(s["rt"], STEPS * b + rt[0])

            def e3(ap, n):
                return ap.unsqueeze(2).to_broadcast([P, TT, n])

            def max8(b, v8, i8, src):
                hold(2)
                for i in range(TT):
                    step(b, nc.vector.max(v8[:, i, :], src[:, i, :]), i == TT - 1)
                hold(3)
                for i in range(TT):
                    step(b, nc.vector.max_index(i8[:, i, :], v8[:, i, :], src[:, i, :]), i == TT - 1)

            def route_soft(b):
                rt[0] = 0
                v.wait_ge(s["logit_sb"], b + 1)
                step(b, nc.vector.tensor_reduce(mx, lg, X, ALU.max))
                tt(lg, lg, e3(mx, E), ALU.subtract).then_inc(s["soft"], 1)

            def route_groups(b):
                v.wait_ge(s["rt_exp"], b + 1)
                step(b, nc.vector.tensor_reduce(rs, lg, X, ALU.add))
                step(b, nc.vector.reciprocal(rs, rs))
                step(b, tt(lg, lg, e3(rs, E), ALU.mult))
                step(b, nc.vector.tensor_reduce(gsc.rearrange("p i n -> p (i n)"), lg.rearrange("p i (n c) -> p (i n) c", n=NG), X, ALU.max))
                max8(b, g8, gi, gsc)
                step(b, cp(gif, gi))
                i8b = iota8[:].unsqueeze(1).to_broadcast([P, TT, NG])
                step(b, tt(gm, i8b, e3(gif[:, :, 0], NG), ALU.is_equal))
                for k in range(1, TG):
                    step(b, tt(gm2, i8b, e3(gif[:, :, k], NG), ALU.is_equal))
                    step(b, tt(gm, gm, gm2, ALU.add))
                step(b, tt(tmp.rearrange("p i (n c) -> p (i n) c", n=NG), lg.rearrange("p i (n c) -> p (i n) c", n=NG),
                           gm.rearrange("p i n -> p (i n)").unsqueeze(2).to_broadcast([P, TT * NG, GS]), ALU.mult))

            def route_experts(b):
                max8(b, w8, ei, tmp)
                step(b, cp(eif.rearrange("p (i k) -> p i k", i=TT), ei[:, :, 0:K]))
                step(b, tt(oh.rearrange("p i k e -> p (i k) e"), iotae[:].unsqueeze(1).to_broadcast([P, TT * K, E]),
                           eif.unsqueeze(2).to_broadcast([P, TT * K, E]), ALU.is_equal))

            def route_counts(b):
                step(b, nc.vector.tensor_reduce(sel, oh.rearrange("p i k e -> p i e k"), X, ALU.add))
                step(b, cp(cum[:, 0, :], cum[:, TT, :]))
                for i in range(TT):
                    ins = tt(cum[:, i + 1, :], cum[:, i, :], sel[:, i, :], ALU.add)
                    if i < TT - 1:
                        step(b, ins)
                ins.then_inc(s["sel_rdy"], 1)

            def route_slots(b):
                v.wait_ge(s["sel_rdy"], b + 1)
                v.wait_ge(s["pos_rdy"], b + 1)
                posv = ps[:, 0, 0:TT * E].rearrange("p (i e) -> p i e", e=E)
                step(b, ts(over, posv, float(C - 1), None, ALU.is_ge))
                tt(cum[:, 0:TT, :], posv, iota96[:].unsqueeze(1).to_broadcast([P, TT, E]), ALU.add).then_inc(s["pos_used"], 1)
                v.wait_ge(s["pos_used"], b + 1)
                step(b, nc.vector.scalar_tensor_tensor(out=cum[:, 0:TT, :], in0=over, scalar=SKIP, in1=cum[:, 0:TT, :], op0=ALU.mult, op1=ALU.add))
                step(b, tt(oh, oh, cum[:, 0:TT, :].unsqueeze(2).to_broadcast([P, TT, K, E]), ALU.mult))
                v.wait_ge(s["tab_free"], b + 1)
                step(b, nc.vector.tensor_reduce(slotf, oh.rearrange("p i k e -> p (i k) e"), X, ALU.add))

            def route_pairs(b):
                step(b, cp(sloti, slotf))
                step(b, cp(pair[:, :, :, 0], iotat[:, bass.ds(b * TT, TT)].unsqueeze(2).to_broadcast([P, TT, K])))
                cp(pair[:, :, :, 1], w8[:, :, 0:K]).then_inc(s["slot_rdy"], 1)
                step(b, tt(over, over, sel, ALU.mult))
                step(b, tt(w95[:, bass.ds(b * TT, TT), :], over, tmp, ALU.mult))
                step(b, tt(sel, sel, e3(iotat1[:, bass.ds(b * TT, TT)], E), ALU.mult))
                step(b, nc.vector.tensor_reduce(rmax, sel.rearrange("p i e -> p e i"), X, ALU.max))
                tt(lastp, lastp, rmax, ALU.max).then_inc(s["lastp_upd"], 1)
                v.wait_ge(s["lastp_upd"], b + 1)
                assert rt[0] == STEPS, rt[0]

            route = [route_soft, route_groups, route_experts, route_counts, route_slots, route_pairs]

            def clamp_gate(n, c):
                gate_rows = rows[:, :, c, :]
                ts(sign, gate_rows, 0.0, 2.0, ALU.is_ge, ALU.mult).then_inc(s["clamp"], 1)
                nc.vector.scalar_tensor_tensor(out=gate_rows, in0=gate_rows, scalar=-1.0, in1=gate_rows, op0=ALU.mult, op1=ALU.max).then_inc(s["clamp"], 1)
                v.wait_ge(s["clamp"], 4 * n + 2)
                ts(gate_rows, gate_rows, 0.25, None, ALU.max).then_inc(s["clamp"], 1)
                v.wait_ge(s["clamp"], 4 * n + 3)
                nc.vector.scalar_tensor_tensor(out=gate_rows, in0=sign, scalar=-1.0, in1=gate_rows, op0=ALU.add, op1=ALU.mult).then_inc(s["clamp"], 1)
                v.wait_ge(s["clamp"], 4 * n + 4)

            sign = w95[:].rearrange("p i e -> p (i e)").rearrange("p (b d) -> p b d", b=B)

            def period(b, p):
                if not (is_last(b) and isinstance(p, int) and p == H - 1):
                    qk_t(b, p + 1)
                if not has_before(b) and isinstance(p, int) and p < 2:
                    if p == 0:
                        v.wait_ge(s["rows_sb"], B)
                        ts(rows[:, :, 2, :], rows[:, :, 2, :], 1.0, None, ALU.add).then_inc(s["cb_rdy"], 1)
                    clamp_gate(p, (0, 3)[p])
                if isinstance(p, int) and has_before(b):
                    if p == 1:
                        x_attended(b - 1)
                        ln_stats(ln2(b - 1), b - 1)
                    if p == 2:
                        ln_norm(ln2(b - 1), b - 1)
                        h2_modulated(b - 1)
                    if 4 <= p < 4 + len(route):
                        if p == 4:
                            v.wait_ge(s["h2_out"], 16 * b)
                            v.wait_ge(s["h2s_rdy"], b)
                        route[p - 4](b - 1)
                if isinstance(p, int) and not is_last(b):
                    if p == H - 4:
                        ln_stats(ln1(b + 1), b + 1)
                        ln_norm(ln1(b + 1), b + 1)
                    if p == H - 3:
                        h_modulated(b + 1)
                if not (is_last(b) and isinstance(p, int) and p >= H - 2):
                    squares_sum(b, p + 2)
                if some(cnt(b, p - 1)):
                    y_add(b, p - 1)
                o_norm(b, p)
                if not (is_last(b) and isinstance(p, int) and p >= H - 2):
                    q_scale(b, p + 2)
                    if not (is_last(b) and isinstance(p, int) and p == H - 3):
                        weights_low(b, p + 3)
                if isinstance(p, int) and p == H - 3 and not is_last(b):
                    v.wait_ge(s["qkv_rdy"], cnt(b, H - 1))
                    h_split(b + 1)

            v.wait_ge(s["ld_x0"], 16)
            ln_stats(0, 0)
            v.wait_ge(s["ld_small"], 32)
            tt(css[:].rearrange("p a h -> p (a h)"), css[:].rearrange("p a h -> p (a h)"), css[:].rearrange("p a h -> p (a h)"), ALU.mult).then_inc(s["g_rdy"], 1)
            tt(qkws[:, 0:1], qkws[:, 0:1], qkws[:, 1:2], ALU.mult).then_inc(s["g_rdy"], 1)
            v.wait_ge(s["g_rdy"], 2)
            tt(g[:], css[:, 0, :], css[:, 1, :], ALU.add).then_inc(s["g_rdy"], 1)
            v.wait_ge(s["g_rdy"], 3)
            ts(g[:], g[:], qkws[:, 0:1], DH ** -0.5 / CAP, ALU.mult, ALU.mult).then_inc(s["g_rdy"], 1)
            v.wait_ge(s["modt_sb"], 2)
            ts(modt[:, 2:4, :], modt[:, 2:4, :], 1.0, None, ALU.add).then_inc(s["modt_sb"], 1)
            v.wait_ge(s["g_rdy"], 4)
            v.wait_ge(s["modt_sb"], 3)
            ln_norm(0, 0)
            h_modulated(0)
            h_split(0)
            weights_low(0, 0)
            squares_sum(0, 0)
            q_scale(0, 0)
            weights_low(0, 1)
            rows_out(0)
            rows_out(1)
            qk_t(0, 0)
            squares_sum(0, 1)
            q_scale(0, 1)
            weights_low(0, 2)
            rows_out(2)
            rows_out(3)
            v.wait_ge(s["consts"], 11)
            v.wait_ge(s["ld_x"], 16)
            for p in range(2):
                period(0, p)
            with v.Fori(2, SIDE) as p:
                period(0, p)
            nc.vector.memset(cum[:, TT, :], 0.0).then_inc(s["carry"], 1)
            nc.vector.memset(lastp, 0.0).then_inc(s["carry"], 1)
            v.wait_ge(s["carry"], 2)
            v.wait_ge(s["cb_rdy"], 1)
            with v.Fori(0, B - 1) as b:
                for p in range(SIDE, H):
                    period(b, p)
                for p in range(SIDE):
                    period(b + 1, p)
            for p in range(SIDE, H):
                period(B - 1, p)
            y_add(B - 1, H - 1)
            x_attended(B - 1)
            ln_stats(ln2(B - 1), B - 1)
            ln_norm(ln2(B - 1), B - 1)
            h2_modulated(B - 1)

            for part_ in route:
                part_(B - 1)
            v.wait_ge(s["lastt_ps"], 1)
            nc.vector.tensor_reduce(lastr[:, 0:1], ps[0:E, 6, 0:P], X, ALU.max).then_inc(s["last_in"], 1)
            v.wait_ge(s["last_in"], 1)
            ts(lastr[:, 0:1], lastr[:, 0:1], -1.0, 0.0, ALU.add, ALU.max).then_inc(s["lastp_rdy"], 1)
            nc.vector.memset(lastr[:, 1:2], 1.0).then_inc(s["lastp_rdy"], 1)
            for q in range(4):
                v.wait_ge(s["w95_ps"], q + 1)
                cp(w95t[:, q * T:(q + 1) * T], ps[0:E, 6 + q % 2, :]).then_inc(s["w95_sb"], 1)

            with v.Fori(0, B) as b:
                for m, (m0, mw) in enumerate(MSC):
                    v.wait_ge(s["sg_act"], b * 3 + (m + 1))
                    if m == 0:
                        v.wait_ge(s["sdn_ps"], 2 * b)
                    tt(acts[0:mw, m, :], ps[0:mw, 2 * (m % 2) + 1, :], sg[0:mw, m % 2, :], ALU.mult).then_inc(s["sa_rdy"], 1)
                for q in range(2):
                    v.wait_ge(s["sdn_ps"], 2 * b + (q + 1))
                    cp(shr[:, 2 * q:2 * q + 2, :], ps[:, 4 + q, :].rearrange("p (i d) -> p i d", i=2)).then_inc(s["shr_rdy"], 1)
                v.wait_ge(s["shr_rdy"], 2 * b + 2)
                tt(shr, shr, rows[:, bass.ds(b, 1), 3:4, :].squeeze(1).to_broadcast([P, TT, D]), ALU.mult).then_inc(s["x_shared"], 1)
                v.wait_ge(s["x_shared"], 2 * b + 1)
                xb = xs[:, bass.ds(b * TT, TT), :]
                tt(xb, xb, shr, ALU.add).then_inc(s["x_shared"], 1)

            v.wait_ge(s["tabt"], 1)
            cp(idf, ps[0:C, 6, 0:E]).then_inc(s["tabt_sb"], 1)
            cp(wcol, ps[0:C, 6, E:2 * E]).then_inc(s["idx_rdy"], 1)
            v.wait_ge(s["tabt_sb"], 1)
            cp(sidx, idf).then_inc(s["idx_rdy"], 1)
            v.wait_ge(s["idx_rdy"], 2)
            ts(idf, idf, float(NTOK - 1), None, ALU.min).then_inc(s["idx_rdy"], 1)
            v.wait_ge(s["idx_rdy"], 3)
            cp(gidx, idf).then_inc(s["idx_rdy"], 1)

            def e_mul(e, base):
                v.wait_ge(s["gact_rdy"], base + e + 1)
                v.wait_ge(s["gu_ps"], base + e + 1)
                tt(act[:, e % 2], ps[0:C, 1 + e % 2, M:2 * M], gact[:, e % 2], ALU.mult).then_inc(s["act_rdy"], 1)

            def e_act_t(e, base):
                v.wait_ge(s["tr2_ps"], base + e + 1)
                cp(actt[:, e % 2], ps[0:MC, 3, 0:2 * C].rearrange("p (m c) -> p m c", m=2)).then_inc(s["actt_rdy"], 1)

            def e_period(e, base):
                e_mul(e, base)
                if not (isinstance(base, int) and base + e < 1):
                    e_act_t(e - 1, base)

            for e in range(2):
                e_period(e, 0)
            with v.Fori(0, (E - 2) // 2) as r:
                e_period(2, r * 2)
                e_period(3, r * 2)
            e_act_t(E - 1, 0)

            v.wait_ge(s["x_shared"], 2 * B)
            for b in range(B):
                sl = slice(b * TT, (b + 1) * TT)
                v.wait_ge(acc_in[b], 16 * NACC)
                tt(accs[0][:, sl], accs[0][:, sl], accs[1][:, sl], ALU.add).then_inc(s["cmb2"], 1)
                v.wait_ge(s["cmb2"], 3 * b + 1)
                v.wait_ge(s["cmb_ps"], b + 1)
                tt(accs[0][:, sl], ps[:, 2 * b:2 * b + 2, :].rearrange("p a (u d) -> p (a u) d", d=D), accs[0][:, sl], ALU.add).then_inc(s["cmb2"], 1)
                v.wait_ge(s["cmb2"], 3 * b + 2)
                tt(accs[0][:, sl], accs[0][:, sl], rows[:, b, 3:4, :].to_broadcast([P, TT, D]), ALU.mult).then_inc(s["cmb2"], 1)
                v.wait_ge(s["cmb2"], 3 * b + 3)
                tt(xs[:, sl], xs[:, sl], accs[0][:, sl], ALU.add).then_inc(s["cmb"], 1)

        @block.tensor
        def _(pe):
            mm = pe.matmul
            pe.wait_ge(s["ld_wmod"], 16)
            pe.wait_ge(s["silu_c"], 1)
            for j in range(4):
                for k in range(KC):
                    last = mm(ps[:, 0, j * B:(j + 1) * B], wmods[:, k, j * P:(j + 1) * P], sc[:, k, :], start=(k == 0), stop=(k == KC - 1))
            last.then_inc(s["modt_ps"], 1)
            def mod_rows(b):
                for h in range(2):
                    for k in range(KC):
                        last = mm(ps[:, 4 + 2 * (b % 2) + h, :], scb[:, k, b, :], wmods[:, k, 2 * D + h * T:2 * D + (h + 1) * T],
                                  start=(k == 0), stop=(k == KC - 1))
                last.then_inc(s["rows_ps"], 1)

            def xn_t():
                for k in range(KC):
                    for i in range(TT):
                        last = pe.transpose(ps[:, k, i * P:(i + 1) * P], xn[:, i, k * P:(k + 1) * P], ident[:])
                last.then_inc(s["xt_ps"], 1)

            def qkv(b, n):
                before = cnt(b, n - 1)
                if some(before):
                    pe.wait_ge(s["v_copied"], before)
                    pe.wait_ge(s["q_scaled"], before)
                if isinstance(n, int) and n % H == 0:
                    pe.wait_ge(s["ht_rdy"], KC * (b + n // H + 1))
                pe.wait_ge(s["wl_rdy"], cnt(b, n))
                for i in range(TT):
                    if i == 2 and some(before):
                        pe.wait_ge(s["qt_rdy"], before)
                    if i == 3 and some(before):
                        pe.wait_ge(s["kt_rdy"], before)
                    for k in range(KC):
                        for m, (hp, wp) in enumerate(((hth, wh), (hth, wl), (htl, wh))):
                            last = mm(ps[:, i, 0:3 * DH], hp[:, k, i * P:(i + 1) * P], wp[:, k, :],
                                      start=(k == 0 and m == 0), stop=(k == KC - 1 and m == 2))
                last.then_inc(s["qkv_rdy"], 1)

            def qk_t(b, n):
                pe.wait_ge(s["q_scaled"], cnt(b, n))
                pe.wait_ge(s["v_copied"], cnt(b, n))
                for i in range(TT):
                    last = pe.transpose(ps[:, 2, i * P:(i + 1) * P], qn[:, i, :], ident[:])
                last.then_inc(s["qt_ps"], 1)
                for i in range(TT):
                    last = pe.transpose(ps[:, 3, i * P:(i + 1) * P], kr[:, i, :], ident[:])
                last.then_inc(s["kt_ps"], 1)

            def scores(b, n):
                pe.wait_ge(s["qt_rdy"], cnt(b, n))
                pe.wait_ge(s["kt_rdy"], cnt(b, n))
                if some(cnt(b, n - 2)):
                    pe.wait_ge(s["y_added"], cnt(b, n - 2))
                for j, w in ((0, 512), (1, 384), (3, 128), (2, 256)):
                    if j == 2 and some(cnt(b, n - 1)):
                        pe.wait_ge(s["o_normed"], 2 * cnt(b, n - 1))
                    last = mm(sflat[:, OFF[j]:OFF[j] + w], kt[:, j * P:(j + 1) * P], qt[:, T - w:T], start=True, stop=True)
                    if j != 1:
                        last.then_inc(s["s_rdy"], 1)

            def o_t(b, n):
                pe.wait_ge(s["o_normed"], 2 * cnt(b, n))
                for i in range(TT):
                    last = pe.transpose(ps[:, 7, i * P:(i + 1) * P], on[:, i, :], ident[:])
                last.then_inc(s["ot_ps"], 1)

            def proj(b, n):
                pe.wait_ge(s["ot_rdy"], cnt(b, n))
                for i in range(TT):
                    last = mm(yps[:, i, :], ot[:, i * P:(i + 1) * P], wos[:, bass.ds(head(n), 1), :].squeeze(1), start=True, stop=True)
                last.then_inc(s["y_rdy"], 1)

            def pv(b, n):
                pe.wait_ge(s["p_rdy"], 2 * cnt(b, n))
                if some(cnt(b, n - 1)):
                    pe.wait_ge(s["ot_rdy"], cnt(b, n - 1))
                for i in range(TT):
                    o = ps[:, 7, i * (DH + 1):(i + 1) * (DH + 1)] if i < 3 else ps[:, 6, 256:257 + DH]
                    for j in range(i + 1):
                        c = OFF[j] + (i - j) * P
                        last = mm(o, prob[:, c:c + P], vx[:, bass.ds((vslot(n) * TT + j) * (DH + 1), DH + 1)],
                                  start=(j == 0), stop=(j == i))
                last.then_inc(s["o_rdy"], 1)

            pe.wait_ge(s["consts"], 4)
            def h1_t(b):
                pe.wait_ge(s["xn_rdy"], TT * (ln1(b) + 1))
                xn_t()

            def h2_t(b):
                pe.wait_ge(s["hmod"], 2 * b + 2)
                xn_t()

            def router(b):
                pe.wait_ge(s["h2s_rdy"], b + 1)
                for i in range(TT):
                    for k in range(KC):
                        last = mm(ps[:, 0, i * E:(i + 1) * E], h2s[:, k, i * P:(i + 1) * P], gates[:, k, :], start=(k == 0), stop=(k == KC - 1))
                last.then_inc(s["logit_ps"], 1)

            def positions(b):
                pe.wait_ge(s["sel_rdy"], b + 1)
                mm(ps[:, 0, 0:TT * E], tri[:], sel.rearrange("p i e -> p (i e)"), start=True, stop=False)
                mm(ps[:, 0, 0:TT * E], ones[:], cum[:, 0:TT, :].rearrange("p i e -> p (i e)"), start=False, stop=True).then_inc(s["pos_rdy"], 1)

            def period(b, p):
                static = isinstance(p, int)
                scores(b, p)
                if some(cnt(b, p - 1)):
                    o_t(b, p - 1)
                if not (is_last(b) and static and p == H - 1):
                    qk_t(b, p + 1)
                side = True
                if static and p == 3 and has_before(b):
                    h2_t(b - 1)
                elif static and p == 8 and has_before(b):
                    positions(b - 1)
                elif static and p == H - 3 and not is_last(b):
                    h1_t(b + 1)
                else:
                    side = False
                if side:
                    pe.wait_ge(s["capped"], 4 * cnt(b, p))
                    proj(b, p - 1)
                    if p == 3:
                        router(b - 1)
                if not (is_last(b) and static and p >= H - 2):
                    if static and p == 3 and has_before(b):
                        pe.wait_ge(s["logit_sb"], b)
                    if static and p == 8 and has_before(b):
                        pe.wait_ge(s["pos_used"], b)
                    if static and p == H - 3 and not is_last(b):
                        pe.wait_ge(s["h_full"], KC * (b + 2))
                    qkv(b, p + 2)
                if not side and some(cnt(b, p - 1)):
                    pe.wait_ge(s["capped"], 4 * cnt(b, p))
                    proj(b, p - 1)
                pv(b, p)

            h1_t(0)
            qkv(0, 0)
            pe.wait_ge(s["scb_rdy"], KC)
            mod_rows(0)
            mod_rows(1)
            qk_t(0, 0)
            qkv(0, 1)
            pe.wait_ge(s["rows_sb"], 2)
            mod_rows(2)
            mod_rows(3)
            pe.wait_ge(s["rows_sb"], B)
            pe.wait_ge(s["ld_wo"], 16)
            pe.wait_ge(s["ld_gate"], 16)
            for p in range(2):
                period(0, p)
            with pe.Fori(2, SIDE) as p:
                period(0, p)
            with pe.Fori(0, B - 1) as b:
                for p in range(SIDE, H):
                    period(b, p)
                for p in range(SIDE):
                    period(b + 1, p)
            for p in range(SIDE, H):
                period(B - 1, p)
            o_t(B - 1, H - 1)
            pe.wait_ge(s["y_added"], cnt(B - 1, H - 2))
            proj(B - 1, H - 1)
            h2_t(B - 1)
            router(B - 1)

            pe.wait_ge(s["logit_sb"], B)
            positions(B - 1)
            pe.wait_ge(s["lastp_upd"], B)
            pe.transpose(ps[0:E, 6, 0:P], lastp, ident[:]).then_inc(s["lastt_ps"], 1)
            pe.wait_ge(s["lastp_rdy"], 2)
            for q in range(4):
                if q >= 2:
                    pe.wait_ge(s["w95_sb"], q - 1)
                for i in range(TT):
                    last = pe.transpose(ps[0:E, 6 + q % 2, i * P:(i + 1) * P], w95[:, q * TT + i, :], ident[:])
                last.then_inc(s["w95_ps"], 1)

            pe.wait_ge(s["ld_sh"], 64)
            with pe.Fori(0, B) as b:
                for m, (m0, mw) in enumerate(MSC):
                    pe.wait_ge(s["sa_rdy"], b * 3 + (m - 1) if m else b * 3)
                    for u in range(2):
                        for k in range(KC):
                            last = mm(ps[0:mw, 2 * (m % 2) + u, :], sgus[:, k, u, m0:m0 + mw], h2t[:, bass.ds(b, 1), k, :].squeeze(1),
                                      start=(k == 0), stop=(k == KC - 1))
                    last.then_inc(s["sg_ps"], 1)
                pe.wait_ge(s["sa_rdy"], b * 3 + 3)
                for q in range(2):
                    pe.wait_ge(s["shr_rdy"], 2 * b)
                    for i in range(2 * q, 2 * q + 2):
                        for m, (m0, mw) in enumerate(MSC):
                            last = mm(ps[:, 4 + q, (i % 2) * D:(i % 2 + 1) * D], acts[0:mw, m, i * P:(i + 1) * P], sds[0:mw, m, :],
                                      start=(m == 0), stop=(m == 2))
                    last.then_inc(s["sdn_ps"], 1)

            pe.wait_ge(s["tabl"], 16)
            pe.wait_ge(s["w95_sb"], 4)
            pe.wait_ge(s["shr_rdy"], 2 * B)
            for c in range(2):
                last = pe.transpose(ps[0:C, 6, c * E:(c + 1) * E], tabs[:, :, c], ident[0:E, 0:E])
            last.then_inc(s["tabt"], 1)

            def tr1(e, base, use):
                pe.wait_ge(xg_in[e % XR], 16 * use)
                pe.wait_ge(s["xgt_rdy"], base + e)
                for k in range(KC):
                    last = pe.transpose(ps[:, 0, k * C:(k + 1) * C], xg[0:C, e % XR, k * P:(k + 1) * P], ident[0:C, 0:C])
                last.then_inc(s["tr1_ps"], 1)

            def gu(e, base, use):
                pe.wait_ge(s["xgt_rdy"], base + e + 1)
                pe.wait_ge(w_in[e % RING], 32 * use)
                for k in range(KC):
                    last = mm(ps[0:C, 1 + e % 2, 0:2 * M], xgt[:, e % 2, k, :], wgus[:, e % RING, k, :], start=(k == 0), stop=(k == KC - 1))
                last.then_inc(s["gu_ps"], 1)

            def tr2(e, base):
                pe.wait_ge(s["act_rdy"], base + e + 1)
                pe.wait_ge(s["actt_rdy"], base + e)
                for m in range(2):
                    last = pe.transpose(ps[0:MC, 3, m * C:(m + 1) * C], act[:, e % 2, m * MC:(m + 1) * MC], ident[0:C, 0:C])
                last.then_inc(s["tr2_ps"], 1)

            def down(e, base):
                pe.wait_ge(s["actt_rdy"], base + e + 1)
                if not (isinstance(base, int) and base + e < 2):
                    pe.wait_ge(s["orow_rdy"], base + e - 1)
                for m in range(2):
                    last = mm(ps[0:C, 4 + e % 2, 0:D], actt[:, e % 2, m, :], wds[:, e % RING, m, :], start=(m == 0), stop=(m == 1))
                last.then_inc(s["dn_ps"], 1)

            def period(e, base, r):
                static = isinstance(base, int)
                if not (static and base + e + 1 >= E):
                    tr1(e + 1, base, r + 1 if e + 1 < XR else r + 2)
                gu(e, base, (XR // RING) * r + (e // RING + 1))
                if not (static and base + e < 1):
                    tr2(e + XR - 1, base - XR) if e < 1 else tr2(e - 1, base)
                if not (static and base + e < 2):
                    down(e + XR - 2, base - XR) if e < 2 else down(e - 2, base)

            pe.wait_ge(s["idx_rdy"], 4)
            tr1(0, 0, 1)
            for e in range(XR):
                period(e, 0, 0)
            with pe.Fori(1, E // XR - 1) as r:
                for e in range(XR):
                    period(e, r * XR, r)
            for e in range(XR):
                period(e, E - XR, E // XR - 1)
            down(E - 2, 0)
            tr2(E - 1, 0)
            down(E - 1, 0)

            pe.wait_ge(s["o95_ld"], 16)
            pe.wait_ge(s["orow_rdy"], E)
            for b in range(B):
                for i in range(TT):
                    t = b * TT + i
                    last = mm(ps[:, 2 * b + i // 2, (i % 2) * D:(i % 2 + 1) * D], w95t[:, t * P:(t + 1) * P], o95, start=True, stop=True)
                last.then_inc(s["cmb_ps"], 1)


def kernel(**inputs):
    import numpy as np
    import concourse.bacc as bacc
    from concourse.bass_utils import run_bass_kernel_spmd as run

    def a(name):
        return np.asarray(inputs[name])

    def headw(name):
        return a(name).reshape(H, DH, D).transpose(2, 0, 1)

    c = np.ascontiguousarray
    arrays = {
        "x": a("L0_attn_x").reshape(NTOK, D),
        "wqkv": np.concatenate([headw("L0_attn_wq"), headw("L0_attn_wk"), headw("L0_attn_wv")], axis=2)
                .reshape(KC, P, H, 3 * DH).transpose(1, 0, 2, 3),
        "wo": a("L0_attn_wo").reshape(D, H, DH).transpose(2, 1, 0),
        "qkw": np.stack([a("L0_attn_q_norm_w"), a("L0_attn_k_norm_w")], axis=1),
        "cossin": np.stack([np.repeat(a("L0_attn_rope_cos")[:H].T, 2, axis=0),
                            np.repeat(a("L0_attn_rope_sin")[:H].T, 2, axis=0)], axis=1),
        "ct": a("L0_c").T.reshape(KC, P, B).transpose(1, 0, 2),
        "wmod": a("L0_wmod").reshape(KC, P, 6 * D).transpose(1, 0, 2),
        "gate": a("L0_ffn_gate_weight").T.reshape(KC, P, E).transpose(1, 0, 2),
        "sgu": np.stack([a("L0_ffn_Sg").T, a("L0_ffn_Su").T], axis=1).reshape(KC, P, 2, MS).transpose(1, 0, 2, 3),
        "sd": a("L0_ffn_Sd").T,
        "wgu": np.concatenate([a("L0_ffn_Wg"), a("L0_ffn_Wu")], axis=1).transpose(0, 2, 1)
               .reshape(E, KC, P, 2 * M).transpose(0, 2, 1, 3),
        "wd": a("L0_ffn_Wd").transpose(0, 2, 1).reshape(E, 2, MC, D).transpose(0, 2, 1, 3),
    }
    nc = bacc.Bacc("TRN2", target_bir_lowering=False, num_devices=1)
    feed, args = {}, []
    for name, v in arrays.items():
        feed[f"in_{name}"] = c(v)
        args.append(nc.dram_tensor(f"in_{name}", v.shape, F32, kind="ExternalInput").ap())
    args.append(nc.dram_tensor("out_0", (NTOK, D), F32, kind="ExternalOutput").ap())
    build(nc, *args)
    r = run(nc, [feed], core_ids=[0])
    return r.results[0]["out_0"].reshape(B, T, D)
```
